# Optimizing a Trainium2 kernel written in Bass

```python
import numpy as np
import jax
import jax.numpy as jnp

def _softmax(x, axis=-1):
    return jax.nn.softmax(x, axis=axis)

def _gelu(x):
    return jax.nn.gelu(x, approximate=True)

def _silu(x):
    return jax.nn.silu(x)

def _sigmoid(x):
    return jax.nn.sigmoid(x)

def _layernorm(x, axis=-1, eps=1e-05):
    m = jnp.mean(x, axis=axis, keepdims=True)
    v = jnp.var(x, axis=axis, keepdims=True)
    return (x - m) / jnp.sqrt(v + eps)

def _scatter_add(tgt, idx, src, axis=0):
    return tgt.at[idx].add(src)

def _segment_sum(src, seg, n):
    return jax.ops.segment_sum(src, seg, n)
kernel_name = 'mk_prb_d1_jaxref_r8_b5f641'

def setup_inputs(seed: int=0):
    np.random.seed(seed)
    _w = jnp.asarray

    def _L0_attn_setup():
        import jax, jax.numpy as jnp
        import numpy as np
        H, HD, D = (16, 64, 128)
        SCALE = HD ** (-0.5)
        TEMP = 1.0
        EPS = 1e-05
        key = jax.random.key(seed)
        ks = jax.random.split(key, 10)
        B, N = (2, 256)
        lim = 1.0 / np.sqrt(D)

        def lin(k, out_d, in_d):
            k1, k2 = jax.random.split(k)
            W = jax.random.uniform(k1, (out_d, in_d), jnp.float32, -lim, lim)
            b = jax.random.uniform(k2, (out_d,), jnp.float32, -lim, lim)
            return (W, b)
        Wq, bq = lin(ks[0], H * HD, D)
        Wk, bk = lin(ks[1], H * HD, D)
        Wv, bv = lin(ks[2], H * HD, D)
        Wo, bo = lin(ks[3], D, H * HD)
        return {'x': jax.random.normal(ks[4], (B, N, D), jnp.float32), 'adaptive_scale': jnp.ones((H,), jnp.float32), 'Wq': Wq, 'bq': bq, 'Wk': Wk, 'bk': bk, 'Wv': Wv, 'bv': bv, 'Wo': Wo, 'bo': bo, 'gamma': jnp.ones((D,), jnp.float32), 'beta': jnp.zeros((D,), jnp.float32)}
    _L0_attn_in = _L0_attn_setup()

    def _L0_ffn_setup():
        import jax, jax.numpy as jnp
        import numpy as np
        B, S, D, H, E = (4, 256, 128, 512, 8)
        EPS = 1e-12

        def _wn(v, g):
            n = jnp.sqrt(jnp.sum(v * v, axis=-1, keepdims=True))
            return v / jnp.maximum(n, EPS) * g[:, None]
        key = jax.random.key(seed)
        ks = jax.random.split(key, 8)
        return {'x': jax.random.normal(ks[0], (B, S, D), dtype=jnp.float32), 'gate_v': jax.random.normal(ks[1], (E, D), dtype=jnp.float32), 'gate_g': jnp.ones((E,), dtype=jnp.float32), 'gate_b': jnp.zeros((E,), dtype=jnp.float32), 'w1_v': jax.random.normal(ks[2], (E, H, D), dtype=jnp.float32), 'w1_g': jnp.ones((E, H), dtype=jnp.float32), 'b1': jnp.zeros((E, H), dtype=jnp.float32), 'w2_v': jax.random.normal(ks[3], (E, D, H), dtype=jnp.float32), 'w2_g': jnp.ones((E, D), dtype=jnp.float32), 'b2': jnp.zeros((E, D), dtype=jnp.float32)}
    _L0_ffn_in = _L0_ffn_setup()
    _d = {'L0_attn_x': _L0_attn_in['x'], 'L0_attn_adaptive_scale': _L0_attn_in['adaptive_scale'], 'L0_attn_Wq': _L0_attn_in['Wq'], 'L0_attn_bq': _L0_attn_in['bq'], 'L0_attn_Wk': _L0_attn_in['Wk'], 'L0_attn_bk': _L0_attn_in['bk'], 'L0_attn_Wv': _L0_attn_in['Wv'], 'L0_attn_bv': _L0_attn_in['bv'], 'L0_attn_Wo': _L0_attn_in['Wo'], 'L0_attn_bo': _L0_attn_in['bo'], 'L0_attn_gamma': _L0_attn_in['gamma'], 'L0_attn_beta': _L0_attn_in['beta'], 'L0_ffn_gate_v': _L0_ffn_in['gate_v'], 'L0_ffn_gate_g': _L0_ffn_in['gate_g'], 'L0_ffn_gate_b': _L0_ffn_in['gate_b'], 'L0_ffn_w1_v': _L0_ffn_in['w1_v'], 'L0_ffn_w1_g': _L0_ffn_in['w1_g'], 'L0_ffn_b1': _L0_ffn_in['b1'], 'L0_ffn_w2_v': _L0_ffn_in['w2_v'], 'L0_ffn_w2_g': _L0_ffn_in['w2_g'], 'L0_ffn_b2': _L0_ffn_in['b2']}
    _x0 = _d['L0_attn_x']
    _d['L0_attn_x'] = jax.random.normal(jax.random.fold_in(jax.random.key(seed), 1), (8, 512, 128), dtype=_x0.dtype)
    del _x0
    return _d

def reference(L0_attn_x, L0_attn_adaptive_scale, L0_attn_Wq, L0_attn_bq, L0_attn_Wk, L0_attn_bk, L0_attn_Wv, L0_attn_bv, L0_attn_Wo, L0_attn_bo, L0_attn_gamma, L0_attn_beta, L0_ffn_gate_v, L0_ffn_gate_g, L0_ffn_gate_b, L0_ffn_w1_v, L0_ffn_w1_g, L0_ffn_b1, L0_ffn_w2_v, L0_ffn_w2_g, L0_ffn_b2):

    def _L0_attn_ref(x, adaptive_scale, Wq, bq, Wk, bk, Wv, bv, Wo, bo, gamma, beta):
        import jax, jax.numpy as jnp
        import numpy as np
        H, HD, D = (16, 64, 128)
        SCALE = HD ** (-0.5)
        TEMP = 1.0
        EPS = 1e-05
        B, N, _ = x.shape
        Q = (x @ Wq.T + bq).reshape(B, N, H, HD)
        K = (x @ Wk.T + bk).reshape(B, N, H, HD)
        V = (x @ Wv.T + bv).reshape(B, N, H, HD)
        scores = jnp.einsum('bnhd,bmhd->bhnm', Q, K)
        scores = scores * (SCALE * adaptive_scale)[None, :, None, None] / TEMP
        w = jax.nn.softmax(scores, axis=-1)
        attn = jnp.einsum('bhnm,bmhd->bnhd', w, V).reshape(B, N, H * HD)
        y = x + (attn @ Wo.T + bo)
        mu = jnp.mean(y, axis=-1, keepdims=True)
        var = jnp.var(y, axis=-1, keepdims=True)
        return (y - mu) / jnp.sqrt(var + EPS) * gamma + beta

    def _L0_ffn_ref(x, gate_v, gate_g, gate_b, w1_v, w1_g, b1, w2_v, w2_g, b2):
        import jax, jax.numpy as jnp
        import numpy as np
        B, S, D, H, E = (4, 256, 128, 512, 8)
        EPS = 1e-12

        def _wn(v, g):
            n = jnp.sqrt(jnp.sum(v * v, axis=-1, keepdims=True))
            return v / jnp.maximum(n, EPS) * g[:, None]
        b, s, d = x.shape
        xf = x.reshape(-1, d)
        gw = _wn(gate_v, gate_g)
        gates = jax.nn.softmax(xf @ gw.T + gate_b, axis=-1)
        top_k = min(2, E)
        _, top_idx = jax.lax.top_k(gates, top_k)
        out = jnp.zeros_like(xf)
        for i in range(E):
            mask = jnp.any(top_idx == i, axis=1).astype(xf.dtype)[:, None]
            xm = xf * mask
            W1 = _wn(w1_v[i], w1_g[i])
            h = xm @ W1.T + b1[i]
            h = h * jax.nn.sigmoid(h)
            W2 = _wn(w2_v[i], w2_g[i])
            out = out + mask * (h @ W2.T + b2[i])
        return out.reshape(b, s, d)
    x = L0_attn_x
    xn = _layernorm(x, axis=-1)
    x = x + _L0_attn_ref(xn, L0_attn_adaptive_scale, L0_attn_Wq, L0_attn_bq, L0_attn_Wk, L0_attn_bk, L0_attn_Wv, L0_attn_bv, L0_attn_Wo, L0_attn_bo, L0_attn_gamma, L0_attn_beta) + _L0_ffn_ref(xn, L0_ffn_gate_v, L0_ffn_gate_g, L0_ffn_gate_b, L0_ffn_w1_v, L0_ffn_w1_g, L0_ffn_b1, L0_ffn_w2_v, L0_ffn_w2_g, L0_ffn_b2)
    return x

_drawn_inputs = setup_inputs


def setup_inputs(seed=0):
    import zlib

    import numpy as np

    out = dict(_drawn_inputs(seed))
    spreads = {'L0_attn_adaptive_scale': (1.0, 0.6),
     'L0_attn_gamma': (1.0, 0.2),
     'L0_attn_beta': (0.0, 0.1),
     'L0_ffn_gate_g': (1.0, 0.2),
     'L0_ffn_gate_b': (0.0, 0.1),
     'L0_ffn_w1_g': (1.0, 0.2),
     'L0_ffn_b1': (0.0, 0.1),
     'L0_ffn_w2_g': (1.0, 0.2),
     'L0_ffn_b2': (0.0, 0.1)}
    factors = {'L0_attn_Wq': 3.48, 'L0_attn_bq': 8.0, 'L0_attn_Wk': 3.457, 'L0_attn_bk': 8.0}
    for name, (base, spread) in spreads.items():
        noise = np.random.default_rng([zlib.crc32(name.encode()), seed]).standard_normal(out[name].shape)
        drawn = base * np.exp(spread * noise) if base else spread * noise
        out[name] = jnp.asarray(drawn.astype(out[name].dtype))
    for name, factor in factors.items():
        out[name] = (out[name] * factor).astype(out[name].dtype)
    return out
```

```python
from contextlib import ExitStack

import concourse.bass as bass
from concourse import mybir

F32 = mybir.dt.float32
F32R = mybir.dt.float32r
BF16 = mybir.dt.bfloat16
ALU = mybir.AluOpType
ACT = mybir.ActivationFunctionType
AX = mybir.AxisListType

P = 128
B, N, D = 8, 512, 128
H, HD = 16, 64
E, FH = 8, 512
QT = N // P
NPAIR = H // 2
PAIRS = B * NPAIR
UNITS = PAIRS * 2 * QT
HC = FH // P
SCALE = float(HD) ** -0.5
LN_EPS = 1e-5
WN_EPS = 1e-12
QH, QL, KH, KL, VH, VL, WCOLS = 0, 128, 256, 512, 768, 896, 1024


def below(eng, sem, value):
    if not isinstance(value, int) or value > 0:
        eng.wait_ge(sem, value)


def make_identity(nc, ctx, name):
    ident = ctx.enter_context(nc.sbuf_tensor(name, [P, P], F32))
    cleared = ctx.enter_context(nc.semaphore(name + "_cleared"))
    with nc.Block() as block:
        @block.gpsimd
        def _(pool):
            pool.memset(ident[:], 0.0).then_inc(cleared, 1)
            pool.wait_ge(cleared, 1)
            pool.affine_select(out=ident[:], in_=ident[:], compare_op=ALU.not_equal, fill=1.0,
                               base=0, pattern=[[-1, P]], channel_multiplier=1)
    return ident


def prepare_attention(nc, a, t):
    with ExitStack() as ctx:
        def sb(name, shape, dt=F32):
            return ctx.enter_context(nc.sbuf_tensor(name, shape, dt))

        def sem(name):
            return ctx.enter_context(nc.semaphore(name))

        x_in = sb("x_in", [P, 2, QT, P])
        xn = sb("xn", [P, 2, QT, P])
        w_in = sb("w_in", [P, 2, 4, P])
        stats = sb("stats", [P, 2, QT, 6])
        mv = sb("mv", [P, 2, QT, 2])
        rstd = sb("rstd", [P, 2, QT])
        wo_nat = sb("wo_nat", [P, H * HD])
        bv_row = sb("bv_row", [P, H * HD])
        wo_bv = sb("wo_bv", [P, H * HD])
        out_bias = sb("out_bias", [P, 4])
        q_scale = sb("q_scale", [P, NPAIR])
        b_in = sb("b_in", [P, 3, NPAIR])
        xT_ps = ctx.enter_context(nc.psum_tensor("xT_ps", [P, 2, N], F32))
        wT_ps = ctx.enter_context(nc.psum_tensor("wT_ps", [P, 2, 4, P], F32))
        once = sem("once")
        x_loaded = [sem("x_loaded0"), sem("x_loaded1")]
        w_loaded = [sem("w_loaded0"), sem("w_loaded1")]
        x_free, w_free = sem("x_free"), sem("w_free")
        xn_free, xT_free, wT_free = sem("xn_free"), sem("xT_free"), sem("wT_free")
        chain = sem("chain")
        var_ready, std_ready = sem("var_ready"), sem("std_ready")
        xn_ready, wq_scaled = sem("xn_ready"), sem("wq_scaled")
        xT_done, wT_done = sem("xT_done"), sem("wT_done")
        x_high, w_high = sem("x_high"), sem("w_high")

        x_v = a["x"].rearrange("b (t p) d -> b p t d", p=P)
        steps = B
        assert steps == NPAIR

        with nc.Block() as block:
            @block.sync
            def _(sp):
                sp.dma_start(wo_nat[:], a["Wo"]).then_inc(once, 16)
                sp.dma_start(bv_row[:], a["bv"].rearrange("(o n) -> o n", o=1).broadcast_to([P, H * HD])).then_inc(once, 16)
                sp.dma_start(out_bias[:, 0:1], a["bo"].rearrange("(p o) -> p o", o=1)).then_inc(once, 16)
                for half in range(2):
                    rows = slice(half * HD, half * HD + HD)
                    sp.dma_start(q_scale[rows, :], a["adaptive_scale"].rearrange("(o r h) -> h o r", h=2, o=1)[half]
                                 .broadcast_to([HD, NPAIR]), allow_slow_non_contiguous=True).then_inc(once, 16)
                    for head in range(2):
                        sp.dma_start(b_in[rows, 1 + head, :], a["bk"].rearrange("(r h p) -> h p r", h=2, p=HD)[head],
                                     allow_slow_non_contiguous=True)\
                            .then_inc(once, 16)
                sp.dma_start(b_in[:, 0, :], a["bq"].rearrange("(r p) -> p r", p=P), allow_slow_non_contiguous=True).then_inc(once, 16)
                with sp.Fori(0, steps // 2) as it:
                    for k in range(2):
                        j = it * 2 + k
                        sp.wait_ge(x_free, j + 1)
                        sp.dma_start(x_in[:, k], x_v[bass.ds(j, 1)].rearrange("o p t d -> p (o t) d")).then_inc(x_loaded[k], 16)
                        sp.wait_ge(w_free, j + 1)
                        for i, w in enumerate(("Wq", "Wk", "Wv")):
                            sp.dma_start(w_in[:, k, i], a[w][bass.ds(j * P, P), :]).then_inc(w_loaded[k], 16)
                        sp.dma_start(w_in[:, k, 3], a["Wo"][:, bass.ds(j * P, P)]).then_inc(w_loaded[k], 16)

            @block.vector
            def _(dve):
                dve.sem_inc(x_free, 2)
                dve.wait_ge(once, 16 * 10)
                nc.vector.tensor_tensor(wo_bv[:], wo_nat[:], bv_row[:], ALU.mult).then_inc(chain, 1)
                dve.wait_ge(chain, 1)
                nc.vector.reduce_sum(out_bias[:, 1:2], wo_bv[:], axis=AX.X).then_inc(chain, 1)
                dve.wait_ge(chain, 2)
                nc.vector.tensor_tensor(out_bias[:, 2:3], out_bias[:, 0:1], out_bias[:, 1:2], ALU.add).then_inc(chain, 1)
                nc.vector.tensor_scalar(q_scale[:], q_scale[:], SCALE, None, ALU.mult).then_inc(chain, 1)
                dve.wait_ge(chain, 4)
                nc.vector.tensor_tensor(t.bias_all[:, :, 0], b_in[:, 0, :], q_scale[:], ALU.mult).then_inc(chain, 1)
                nc.vector.tensor_copy(t.bias_all[:, :, 1:3], b_in[:, 1:3, :].rearrange("p h r -> p r h")).then_inc(chain, 1)
                nc.vector.memset(out_bias[:, 3:4], LN_EPS).then_inc(chain, 1)
                dve.wait_ge(chain, 7)
                with dve.Fori(0, steps // 2) as it:
                    for k in range(2):
                        j = it * 2 + k
                        dve.wait_ge(x_loaded[k], it * 16 + 16)
                        c0 = j * (2 * QT + 1) + 7
                        for q in range(QT):
                            nc.vector.bn_stats(stats[:, k, q], x_in[:, k, q]).then_inc(chain, 1)
                        dve.wait_ge(chain, c0 + QT)
                        dve.wait_ge(w_loaded[k], it * 64 + 64)
                        nc.vector.tensor_scalar(w_in[:, k, 0], w_in[:, k, 0], q_scale[:, bass.ds(j, 1)], None, ALU.mult)\
                            .then_inc(wq_scaled, 1)
                        for q in range(QT):
                            nc.vector.bn_aggr(mv[:, k, q], stats[:, k, q]).then_inc(chain, 1)
                        dve.wait_ge(chain, c0 + 2 * QT)
                        dve.sem_inc(var_ready, 1)
                        dve.wait_ge(std_ready, j + 1)
                        nc.vector.reciprocal(rstd[:, k], rstd[:, k]).then_inc(chain, 1)
                        dve.wait_ge(chain, c0 + 2 * QT + 1)
                        dve.wait_ge(xn_free, j + 1)
                        for q in range(QT):
                            last = nc.vector.tensor_scalar(xn[:, k, q], x_in[:, k, q], mv[:, k, q, 0:1], rstd[:, k, q:q + 1],
                                                           ALU.subtract, ALU.mult)
                        last.then_inc(xn_ready, 1)
                        dve.wait_ge(xn_ready, j + 1)
                        dve.sem_inc(x_free, 1)
                        dve.wait_ge(x_high, j + 1)
                        nc.vector.tensor_scalar(t.yacc[:, bass.ds(j * N, N)], xT_ps[:, k], out_bias[:, 2:3], None, ALU.add)
                        nc.vector.tensor_tensor(t.xs[:, bass.ds(j * 2 * N + N, N)], xT_ps[:, k],
                                                t.xs[:, bass.ds(j * 2 * N, N)], ALU.subtract).then_inc(xT_free, 1)
                        dve.wait_ge(w_high, j + 1)
                        w0 = j * WCOLS
                        nc.vector.tensor_tensor(t.wall[:, bass.ds(w0 + QL, P)], wT_ps[:, k, 0],
                                                t.wall[:, bass.ds(w0 + QH, P)], ALU.subtract)
                        for head in range(2):
                            src = wT_ps[:, k, 1, head * HD:head * HD + HD].unsqueeze(1).broadcast_to([P, 2, HD])
                            nc.vector.tensor_tensor(
                                t.wall[:, bass.ds(w0 + KL + head * P, P)].rearrange("p (c n) -> p c n", c=2), src,
                                t.wall[:, bass.ds(w0 + KH + head * P, P)].rearrange("p (c n) -> p c n", c=2), ALU.subtract)
                        nc.vector.tensor_tensor(t.wall[:, bass.ds(w0 + VL, P)], wT_ps[:, k, 2],
                                                t.wall[:, bass.ds(w0 + VH, P)], ALU.subtract).then_inc(wT_free, 1)

            @block.tensor
            def _(pe):
                pe.sem_inc(w_free, 2)
                pe.sem_inc(xn_free, 2)
                with pe.Fori(0, steps // 2) as it:
                    for k in range(2):
                        j = it * 2 + k
                        pe.wait_ge(xn_ready, j + 1)
                        pe.wait_ge(xT_free, j + 1)
                        for q in range(QT):
                            nc.tensor.transpose(xT_ps[:, k, q * P:q * P + P], xn[:, k, q], t.ident[:])\
                                .then_inc(xT_done, 1)
                        pe.wait_ge(xT_done, j * QT + QT)
                        pe.sem_inc(xn_free, 1)
                        pe.wait_ge(wq_scaled, j + 1)
                        pe.wait_ge(wT_free, j + 1)
                        for i in range(4):
                            nc.tensor.transpose(wT_ps[:, k, i], w_in[:, k, i], t.ident[:]).then_inc(wT_done, 1)
                        pe.wait_ge(wT_done, j * 4 + 4)
                        pe.sem_inc(w_free, 1)

            @block.scalar
            def _(act):
                act.sem_inc(xT_free, 2)
                act.sem_inc(wT_free, 2)
                with act.Fori(0, steps // 2) as it:
                    for k in range(2):
                        j = it * 2 + k
                        act.wait_ge(var_ready, j + 1)
                        nc.scalar.activation(rstd[:, k], mv[:, k, :, 1], ACT.Sqrt, bias=out_bias[:, 3:4]).then_inc(std_ready, 1)
                        act.wait_ge(xT_done, j * QT + QT)
                        nc.scalar.activation(t.xs[:, bass.ds(j * 2 * N, N)], xT_ps[:, k], ACT.Copy).then_inc(x_high, 1)
                        act.wait_ge(wT_done, j * 4 + 4)
                        w0 = j * WCOLS
                        nc.scalar.activation(t.wall[:, bass.ds(w0 + QH, P)], wT_ps[:, k, 0], ACT.Copy)
                        for head in range(2):
                            src = wT_ps[:, k, 1, head * HD:head * HD + HD].unsqueeze(1).broadcast_to([P, 2, HD])
                            nc.scalar.activation(t.wall[:, bass.ds(w0 + KH + head * P, P)].rearrange("p (c n) -> p c n", c=2),
                                                 src, ACT.Copy)
                        nc.scalar.activation(t.wall[:, bass.ds(w0 + VH, P)], wT_ps[:, k, 2], ACT.Copy)
                        for head in range(2):
                            for half in range(2):
                                last = nc.scalar.activation(
                                    t.wo_all[half * HD:half * HD + HD, bass.ds(j * 2 * P + head * P, P)],
                                    wT_ps[head * HD:head * HD + HD, k, 3], ACT.Copy)
                        last.then_inc(w_high, 1)


def attention(nc, t):
    with ExitStack() as ctx:
        def sb(name, shape, dt=F32):
            return ctx.enter_context(nc.sbuf_tensor(name, shape, dt))

        def psum(name, shape):
            return ctx.enter_context(nc.psum_tensor(name, shape, F32))

        def sem(name):
            return ctx.enter_context(nc.semaphore(name))

        x_st = sb("x_st", [P, 2, 2 * N], F32R)
        w_st = sb("w_st", [P, 2, WCOLS], F32R)
        b_st = sb("b_st", [P, 2, 3])
        wo_st = sb("wo_st", [P, 2, 2 * P])
        q_sb = sb("q_sb", [P, 4, N], F32R)
        kh_sb = sb("kh_sb", [P, 4, N], F32R)
        kl_sb = sb("kl_sb", [P, 4, N], F32R)
        v_sb = sb("v_sb", [P, 2, 2, QT, P], F32R)
        probs = sb("probs", [P, 4, N])
        pth = sb("pth", [P, 2, QT, N], F32R)
        ptl = sb("ptl", [P, 2, QT, N], F32R)
        o_sb = sb("o_sb", [P, 2, N])
        nmax = sb("nmax", [P, 8])
        rsum = sb("rsum", [P, 8])
        rinv = sb("rinv", [P, 8])
        s_ps = psum("s_ps", [P, 2, N])
        t_ps = psum("t_ps", [P, 2, N])
        o_ps = psum("o_ps", [P, 2, N])
        m_ps = psum("m_ps", [P, 2, N])

        st_loaded = [sem("st_loaded0"), sem("st_loaded1")]
        wo_loaded = [sem("wo_loaded0"), sem("wo_loaded1")]
        s_done, t_done, pv_done = sem("s_done"), sem("t_done"), sem("pv_done")
        q_mm, k_mm, v_mm, wo_mm = sem("q_mm"), sem("k_mm"), sem("v_mm"), sem("wo_mm")
        q_high, k_high, v_high = sem("q_high"), sem("k_high"), sem("v_high")
        q_low, k_low, v_low, y_added = sem("q_low"), sem("k_low"), sem("v_low"), sem("y_added")
        max_done, exp_done, inv_done, norm_done = sem("max_done"), sem("exp_done"), sem("inv_done"), sem("norm_done")
        ph_done, pl_done, o_done = sem("ph_done"), sem("pl_done"), sem("o_done")

        def valid(it, unit, low=0, high=UNITS):
            return not isinstance(it, int) or low <= 16 * it + unit < high

        def pair_ok(it, pair):
            return not isinstance(it, int) or 0 <= 2 * it + pair < PAIRS

        def chunks(it, l):
            w, p = l % 8, l // 8
            found = {0: ("q", 0, p + 1, 0), 1: ("wo", 1, p - 1, 0), 2: ("k", 0, p + 1, 0), 3: ("k", 1, p + 1, 1),
                     5: ("wo", 0, p - 1, 1), 6: ("v", 1, p + 1, 0)}.get(w)
            return found if found and pair_ok(it, found[2]) else None

        def pe_slot(pe, it, l):
            u = it * 16 + l
            if valid(it, l + 3):
                g, qt, bank = (l + 3) // 4, (l + 3) % 4, (l + 3) % 2
                if qt == 0:
                    pe.wait_ge(q_low, it * 2 + g // 2 + 1)
                    pe.wait_ge(k_low, it * 4 + g + 1)
                below(pe, exp_done, u + 2)
                lhs = q_sb[:, g % 4, qt * P:qt * P + P]
                nc.tensor.matmul(s_ps[:, bank], lhs, kh_sb[:, g % 4], start=True, stop=False)
                nc.tensor.matmul(s_ps[:, bank], lhs, kl_sb[:, g % 4], start=False, stop=True).then_inc(s_done, 1)
            if valid(it, l):
                below(pe, norm_done, u + 1)
                below(pe, pl_done, u - 1)
                for kc in range(QT):
                    last = nc.tensor.transpose(t_ps[:, l % 2, kc * P:kc * P + P], probs[:, l % 4, kc * P:kc * P + P],
                                               t.ident[:])
                last.then_inc(t_done, 1)
            if valid(it, l - 4):
                g, kc = l // 4 - 1, l % 4
                if kc == 0:
                    pe.wait_ge(pl_done, it * 16 + 4 * g + 4)
                    below(pe, o_done, it * 4 + g - 1)
                    if g % 2 == 0:
                        pe.wait_ge(v_low, it * 2 + g // 2 + 1)
                for part, pt in enumerate((pth, ptl)):
                    last = nc.tensor.matmul(o_ps[:, g % 2], v_sb[:, (g // 2) % 2, g % 2, kc], pt[:, g % 2, kc],
                                            start=kc + part == 0, stop=kc + part == QT)
                if kc == 3:
                    last.then_inc(pv_done, 1)
            c = chunks(it, l)
            if c:
                kind, bank, pr, head = c
                st, pi = pr % 2, it * 2 + pr
                xh, xl = x_st[:, st, 0:N], x_st[:, st, N:2 * N]
                w = w_st[:, st]
                if kind == "q":
                    pe.wait_ge(st_loaded[st], (it + pr // 2 + 1) * 48)
                    below(pe, y_added, pi * 2 - 4)
                    nc.tensor.matmul(m_ps[:, bank], w[:, QH:QH + P], xh, start=True, stop=False)
                    nc.tensor.matmul(m_ps[:, bank], w[:, QH:QH + P], xl, start=False, stop=False)
                    nc.tensor.matmul(m_ps[:, bank], w[:, QL:QL + P], xh, start=False, stop=True).then_inc(q_mm, 1)
                elif kind == "k":
                    if head == 0:
                        pe.wait_ge(q_low, pi + 1)
                    else:
                        below(pe, y_added, pi * 2 - 3)
                    hi = w[:, KH + head * P:KH + head * P + P]
                    nc.tensor.matmul(m_ps[:, bank], hi, xh, start=True, stop=False)
                    nc.tensor.matmul(m_ps[:, bank], hi, xl, start=False, stop=False)
                    nc.tensor.matmul(m_ps[:, bank], w[:, KL + head * P:KL + head * P + P], xh, start=False, stop=True)\
                        .then_inc(k_mm, 1)
                elif kind == "v":
                    pe.wait_ge(k_low, pi * 2 + 2)
                    for kc in range(QT):
                        out = m_ps[:, bank, kc * P:kc * P + P]
                        xhk, xlk = xh[:, kc * P:kc * P + P], xl[:, kc * P:kc * P + P]
                        nc.tensor.matmul(out, xhk, w[:, VH:VH + P], start=True, stop=False)
                        nc.tensor.matmul(out, xhk, w[:, VL:VL + P], start=False, stop=False)
                        last = nc.tensor.matmul(out, xlk, w[:, VH:VH + P], start=False, stop=True)
                    last.then_inc(v_mm, 1)
                else:
                    gi = pi * 2 + head
                    pe.wait_ge(o_done, gi + 1)
                    if head == 0:
                        pe.wait_ge(wo_loaded[st], (it + pr // 2 + 1) * 16)
                        if pair_ok(it, pr + 1):
                            pe.wait_ge(v_low, pi + 2)
                        else:
                            pe.wait_ge(y_added, gi - 1)
                    elif pair_ok(it, pr + 2):
                        pe.wait_ge(k_low, (pi + 2) * 2 + 1)
                    else:
                        below(pe, y_added, gi)
                    nc.tensor.matmul(m_ps[:, bank], wo_st[:, st, head * P:head * P + P], o_sb[:, head], start=True, stop=True)\
                        .then_inc(wo_mm, 1)

        def act_slot(act, it, l):
            u = it * 16 + l
            if l % 4 == 0 and valid(it, l - 8):
                g = l // 4 - 2
                gi = it * 4 + g
                act.wait_ge(pv_done, gi + 1)
                below(act, wo_mm, gi - 1)
                nc.scalar.activation(o_sb[:, g % 2], o_ps[:, g % 2], ACT.Copy).then_inc(o_done, 1)
            if valid(it, l + 2):
                act.wait_ge(max_done, u + 3)
                below(act, t_done, u - 1)
                m = (l + 2) % 8
                nc.scalar.activation(probs[:, (l + 2) % 4], s_ps[:, l % 2], ACT.Exp, bias=nmax[:, m:m + 1],
                                     accum_out=rsum[:, m:m + 1]).then_inc(exp_done, 1)
            if valid(it, l):
                g, qt = l // 4, l % 4
                act.wait_ge(t_done, u + 1)
                if qt == 0:
                    below(act, pv_done, it * 4 + g - 1)
                nc.scalar.activation(pth[:, g % 2, :, qt * P:qt * P + P],
                                     t_ps[:, l % 2].rearrange("p (c q) -> p c q", c=QT), ACT.Copy).then_inc(ph_done, 1)
            c = chunks(it, l)
            if c and c[0] != "wo":
                kind, bank, pr, head = c
                st, pi = pr % 2, it * 2 + pr
                if kind == "q":
                    act.wait_ge(q_mm, pi + 1)
                    below(act, s_done, pi * 8 - 8)
                    for hd in range(2):
                        rows = slice(hd * HD, hd * HD + HD)
                        last = nc.scalar.activation(q_sb[rows, st * 2 + hd], m_ps[rows, bank], ACT.Identity,
                                                    bias=b_st[rows, st, 0:1])
                    last.then_inc(q_high, 1)
                elif kind == "k":
                    act.wait_ge(k_mm, pi * 2 + head + 1)
                    nc.scalar.activation(kh_sb[:, st * 2 + head], m_ps[:, bank], ACT.Identity,
                                         bias=b_st[:, st, 1 + head:2 + head]).then_inc(k_high, 1)
                else:
                    act.wait_ge(v_mm, pi + 1)
                    below(act, pv_done, pi * 2 - 2)
                    nc.scalar.activation(v_sb[:, st, :, :, 0:HD].rearrange("p h c n -> p c h n"),
                                         m_ps[:, bank].rearrange("p (c h n) -> p c h n", c=QT, h=2), ACT.Copy)\
                        .then_inc(v_high, 1)

        def dve_slot(dve, it, l):
            u = it * 16 + l
            if valid(it, l + 1):
                dve.wait_ge(exp_done, u + 2)
                m = (l + 1) % 8
                nc.vector.reciprocal(rinv[:, m:m + 1], rsum[:, m:m + 1]).then_inc(inv_done, 1)
            c = chunks(it, l - 1)
            if c:
                kind, bank, pr, head = c
                st, pi = pr % 2, it * 2 + pr
                if kind == "q":
                    dve.wait_ge(q_high, pi + 1)
                    for hd in range(2):
                        rows, other = slice(hd * HD, hd * HD + HD), slice(HD - hd * HD, P - hd * HD)
                        last = nc.vector.scalar_tensor_tensor(q_sb[other, st * 2 + hd], m_ps[rows, bank], b_st[rows, st, 0:1],
                                                              q_sb[rows, st * 2 + hd], ALU.add, ALU.subtract)
                    last.then_inc(q_low, 1)
                elif kind == "k":
                    dve.wait_ge(k_high, pi * 2 + head + 1)
                    nc.vector.scalar_tensor_tensor(kl_sb[:, st * 2 + head], m_ps[:, bank], b_st[:, st, 1 + head:2 + head],
                                                   kh_sb[:, st * 2 + head], ALU.add, ALU.subtract).then_inc(k_low, 1)
                elif kind == "v":
                    dve.wait_ge(v_high, pi + 1)
                    nc.vector.tensor_tensor(v_sb[:, st, :, :, HD:P].rearrange("p h c n -> p c h n"),
                                            m_ps[:, bank].rearrange("p (c h n) -> p c h n", c=QT, h=2),
                                            v_sb[:, st, :, :, 0:HD].rearrange("p h c n -> p c h n"), ALU.subtract)\
                        .then_inc(v_low, 1)
                else:
                    dve.wait_ge(wo_mm, pi * 2 + head + 1)
                    below(dve, y_added, pi * 2 + head)
                    acc = t.yacc[:, bass.ds(pi // NPAIR * N, N)]
                    nc.vector.tensor_tensor(acc, m_ps[:, bank], acc, ALU.add).then_inc(y_added, 1)
            if valid(it, l + 3):
                dve.wait_ge(s_done, u + 4)
                m = (l + 3) % 8
                nc.vector.tensor_reduce(nmax[:, m:m + 1], s_ps[:, (l + 3) % 2], axis=AX.X, op=ALU.max, negate=True)\
                    .then_inc(max_done, 1)
            if valid(it, l):
                g, qt = l // 4, l % 4
                dve.wait_ge(ph_done, u + 1)
                sl = slice(qt * P, qt * P + P)
                nc.vector.tensor_tensor(ptl[:, g % 2, :, sl], t_ps[:, l % 2].rearrange("p (c q) -> p c q", c=QT),
                                        pth[:, g % 2, :, sl], ALU.subtract).then_inc(pl_done, 1)

        def pool_slot(pool, it, l):
            u = it * 16 + l
            if valid(it, l + 1):
                pool.wait_ge(inv_done, u + 2)
                m, pb = (l + 1) % 8, probs[:, (l + 1) % 4]
                nc.gpsimd.tensor_tensor(pb, pb, rinv[:, m:m + 1].broadcast_to([P, N]), ALU.mult).then_inc(norm_done, 1)

        def engine_program(eng, slot):
            for l in range(-8, 16):
                slot(eng, 0, l)
            with eng.Fori(1, PAIRS // 2 - 1) as it:
                for l in range(16):
                    slot(eng, it, l)
            for l in range(16, 16 + 16 + 12):
                slot(eng, PAIRS // 2 - 2, l)

        with nc.Block() as block:
            @block.sync
            def _(sp):
                def stage(it, pr):
                    st, pi = pr % 2, it * 2 + pr
                    below(sp, v_mm, pi - 1)
                    below(sp, k_low, pi * 2 - 2)
                    sp.dma_start(x_st[:, st].bitcast(F32), t.xs[:, bass.ds(pi // NPAIR * (2 * N), 2 * N)].bitcast(F32)).then_inc(st_loaded[st], 16)
                    sp.dma_start(w_st[:, st].bitcast(F32), t.wall[:, bass.ds(pi % NPAIR * WCOLS, WCOLS)].bitcast(F32)).then_inc(st_loaded[st], 16)
                    sp.dma_start(b_st[:, st], t.bias_all[:, bass.ds(pi % NPAIR, 1), :].rearrange("p o c -> p (o c)"))\
                        .then_inc(st_loaded[st], 16)

                def stage_wo(it, pr):
                    st, pi = pr % 2, it * 2 + pr
                    below(sp, wo_mm, pi * 2 - 2)
                    sp.dma_start(wo_st[:, st], t.wo_all[:, bass.ds(pi % NPAIR * (2 * P), 2 * P)]).then_inc(wo_loaded[st], 16)

                stage(0, 0)
                stage(0, 1)
                for pr in range(2):
                    stage_wo(0, pr)
                    stage(0, pr + 2)
                with sp.Fori(1, PAIRS // 2 - 1) as it:
                    for pr in range(2):
                        stage_wo(it, pr)
                        stage(it, pr + 2)
                for pr in range(2):
                    stage_wo(PAIRS // 2 - 1, pr)

            @block.tensor
            def _(pe):
                engine_program(pe, pe_slot)

            @block.scalar
            def _(act):
                engine_program(act, act_slot)

            @block.vector
            def _(dve):
                engine_program(dve, dve_slot)

            @block.gpsimd
            def _(pool):
                engine_program(pool, pool_slot)


def finish_attention(nc, a, t):
    with ExitStack() as ctx:
        def sb(name, shape, dt=F32):
            return ctx.enter_context(nc.sbuf_tensor("fin_" + name, shape, dt))

        def sem(name):
            return ctx.enter_context(nc.semaphore("fin_" + name))

        x_in = sb("x_in", [P, 2, QT, P])
        yb = sb("yb", [P, 2, N])
        stats = sb("stats", [P, 2, QT, 6])
        mv = sb("mv", [P, 2, QT, 2])
        rstd = sb("rstd", [P, 2, QT])
        yn = sb("yn", [P, 2, QT, P])
        gamma, beta, eps = sb("gamma", [P, P]), sb("beta", [P, P]), sb("eps", [P, 1])
        yT_ps = ctx.enter_context(nc.psum_tensor("fin_yT_ps", [P, 2, QT, P], F32))
        once, eps_set = sem("once"), sem("eps_set")
        x_loaded = [sem("x_loaded0"), sem("x_loaded1")]
        y_copied, yT_done = sem("y_copied"), sem("yT_done")
        chain, var_ready, std_ready, block_done = sem("chain"), sem("var_ready"), sem("std_ready"), sem("block_done")
        x_v = a["x"].rearrange("b (t p) d -> b p t d", p=P)

        with nc.Block() as block:
            @block.sync
            def _(sp):
                for dst, src in ((gamma, "gamma"), (beta, "beta")):
                    sp.dma_start(dst[:], a[src].rearrange("(o n) -> o n", o=1).broadcast_to([P, P])).then_inc(once, 16)
                with sp.Fori(0, B // 2) as it:
                    for k in range(2):
                        sp.wait_ge(block_done, it * 2 + k + 1)
                        sp.dma_start(x_in[:, k], x_v[bass.ds(it * 2 + k, 1)].rearrange("o p t d -> p (o t) d"))\
                            .then_inc(x_loaded[k], 16)

            @block.scalar
            def _(act):
                act.wait_ge(eps_set, 1)
                with act.Fori(0, B // 2) as it:
                    for k in range(2):
                        j = it * 2 + k
                        act.wait_ge(block_done, j + 1)
                        nc.scalar.activation(yb[:, k], t.yacc[:, bass.ds(j * N, N)], ACT.Copy).then_inc(y_copied, 1)
                        act.wait_ge(var_ready, j + 1)
                        nc.scalar.activation(rstd[:, k], mv[:, k, :, 1], ACT.Sqrt, bias=eps[:]).then_inc(std_ready, 1)

            @block.tensor
            def _(pe):
                with pe.Fori(0, B // 2) as it:
                    for k in range(2):
                        pe.wait_ge(y_copied, it * 2 + k + 1)
                        for q in range(QT):
                            last = nc.tensor.transpose(yT_ps[:, k, q], yb[:, k, q * P:q * P + P], t.ident[:])
                        last.then_inc(yT_done, 1)

            @block.vector
            def _(dve):
                dve.sem_inc(block_done, 2)
                nc.vector.memset(eps[:], LN_EPS).then_inc(eps_set, 1)
                dve.wait_ge(once, 32)
                with dve.Fori(0, B // 2) as it:
                    for k in range(2):
                        j = it * 2 + k
                        c0 = j * (2 * QT + 4)
                        dve.wait_ge(yT_done, j + 1)
                        for q in range(QT):
                            nc.vector.bn_stats(stats[:, k, q], yT_ps[:, k, q]).then_inc(chain, 1)
                        dve.wait_ge(chain, c0 + QT)
                        dve.wait_ge(x_loaded[k], it * 16 + 16)
                        nc.vector.tensor_tensor(x_in[:, k], x_in[:, k], beta[:].unsqueeze(1).broadcast_to([P, QT, P]), ALU.add)\
                            .then_inc(chain, 1)
                        for q in range(QT):
                            last = nc.vector.bn_aggr(mv[:, k, q], stats[:, k, q]).then_inc(chain, 1)
                        dve.wait_ge(chain, c0 + 2 * QT + 1)
                        dve.sem_inc(var_ready, 1)
                        dve.wait_ge(std_ready, j + 1)
                        nc.vector.reciprocal(rstd[:, k], rstd[:, k]).then_inc(chain, 1)
                        dve.wait_ge(chain, c0 + 2 * QT + 2)
                        for q in range(QT):
                            last = nc.vector.tensor_scalar(yn[:, k, q], yT_ps[:, k, q], mv[:, k, q, 0:1], rstd[:, k, q:q + 1],
                                                           ALU.subtract, ALU.mult)
                        last.then_inc(chain, 1)
                        dve.wait_ge(chain, c0 + 2 * QT + 3)
                        nc.vector.tensor_tensor(yn[:, k], yn[:, k], gamma[:].unsqueeze(1).broadcast_to([P, QT, P]), ALU.mult)\
                            .then_inc(chain, 1)
                        dve.wait_ge(chain, c0 + 2 * QT + 4)
                        nc.vector.tensor_tensor(t.res[:, bass.ds(j * N, N)].rearrange("p (t d) -> p t d", d=P),
                                                yn[:, k], x_in[:, k], ALU.add).then_inc(block_done, 1)


def prepare_experts(nc, a, t):
    R_G1, R_B1, R_G2, ROWS = 0, E * HC, 2 * E * HC, 2 * E * HC + E
    with ExitStack() as ctx:
        def sb(name, shape, dt=F32):
            return ctx.enter_context(nc.sbuf_tensor("wex_" + name, shape, dt))

        def sem(name):
            return ctx.enter_context(nc.semaphore("wex_" + name))

        rows = sb("rows", [P, P])
        w_in = sb("w_in", [P, 2, 2 * HC, P])
        w_sq = sb("w_sq", [P, 2 * HC, P])
        wn = sb("wn", [P, 2, 2 * HC, P])
        ss = sb("ss", [P, 2 * HC])
        nrm = sb("nrm", [P, HC + 1])
        wscale = sb("wscale", [P, HC + 1])
        gate_in, gate_sq = sb("gate_in", [P, P]), sb("gate_sq", [E, P])
        gate_s = sb("gate_s", [E, 4])
        gateT_h, gateT_l = sb("gateT_h", [P, P], F32R), sb("gateT_l", [P, P], F32R)
        lgT = sb("lgT", [E, B, N])
        lg = sb("lg", [P, B * QT, E])
        lmax = sb("lmax", [P, B * QT])
        cmp_a, cmp_b = sb("cmp_a", [P, B * QT, E, E]), sb("cmp_b", [P, B * QT, E, E])
        before = sb("before", [P, E, E])
        rank = sb("rank", [P, B * QT, E])
        wT_ps = ctx.enter_context(nc.psum_tensor("wex_wT_ps", [P, 2, 2, FH], F32))
        g_ps = ctx.enter_context(nc.psum_tensor("wex_g_ps", [P, 2, 512], F32))
        r_ps = ctx.enter_context(nc.psum_tensor("wex_r_ps", [P, 512], F32))

        rows_zero, once = sem("rows_zero"), sem("once")
        w_loaded = [sem("w_loaded0"), sem("w_loaded1")]
        chain, sq_ready, std_ready, wn_ready = sem("chain"), sem("sq_ready"), sem("std_ready"), sem("wn_ready")
        wT_done, w1_high, w1_free, w2_free = (sem(n) for n in ("wT_done", "w1_high", "w1_free", "w2_free"))
        rowsT, cols_ready, gateT_done, gate_ready = sem("rowsT"), sem("cols_ready"), sem("gateT_done"), sem("gate_ready")
        lgT_done, lgT_ready, lg_done, mask_ready, maskT_done, maskT_ready = (
            sem(n) for n in ("lgT_done", "lgT_ready", "lg_done", "mask_ready", "maskT_done", "maskT_ready"))
        order_ready = sem("order_ready")

        with nc.Block() as block:
            @block.sync
            def _(sp):
                sp.wait_ge(rows_zero, 2)
                sp.dma_start(gate_in[0:E, :], a["gate_v"]).then_inc(once, 16)
                sp.dma_start(gate_s[:, 1:2], a["gate_g"].rearrange("(p o) -> p o", o=1)).then_inc(once, 16)
                sp.dma_start(gate_s[:, 2:3], a["gate_b"].rearrange("(p o) -> p o", o=1)).then_inc(once, 16)
                for r0, name in ((R_G1, "w1_g"), (R_B1, "b1")):
                    sp.dma_start(rows[r0:r0 + E * HC, :], a[name].rearrange("e (c p) -> (e c) p", p=P)).then_inc(once, 16)
                sp.dma_start(rows[R_G2:ROWS, :], a["w2_g"]).then_inc(once, 16)
                sp.dma_start(t.b2[:], a["b2"]).then_inc(once, 16)
                with sp.Fori(0, E // 2) as it:
                    for k in range(2):
                        e = it * 2 + k
                        sp.wait_ge(wn_ready, e + 1)
                        sp.dma_start(w_in[:, k, 0:HC], a["w1_v"].rearrange("e (c p) d -> e p c d", p=P)[bass.ds(e, 1)]
                                     .rearrange("o p c d -> p (o c) d")).then_inc(w_loaded[k], 16)
                        sp.dma_start(w_in[:, k, HC:2 * HC], a["w2_v"].rearrange("e p (c n) -> e p c n", n=P)[bass.ds(e, 1)]
                                     .rearrange("o p c n -> p (o c) n")).then_inc(w_loaded[k], 16)

            @block.gpsimd
            def _(pool):
                pool.memset(rows[:], 0.0).then_inc(rows_zero, 1)
                pool.memset(gate_in[:], 0.0).then_inc(rows_zero, 1)
                pool.memset(t.select[:], 1.0).then_inc(order_ready, 1)
                pool.memset(before[:], 1.0).then_inc(order_ready, 1)
                pool.wait_ge(order_ready, 2)
                pool.affine_select(out=before[:], in_=before[:], compare_op=ALU.is_gt, fill=0.0, base=0,
                                   pattern=[[1, E], [-1, E]], channel_multiplier=0).then_inc(order_ready, 1)
                pool.affine_select(out=t.select[:], in_=t.select[:], compare_op=ALU.is_equal, fill=0.0, base=0,
                                   pattern=[[-1, E], [0, P]], channel_multiplier=1).then_inc(order_ready, 1)

            @block.vector
            def _(dve):
                n = [0]

                def link(ins):
                    n[0] += 1
                    ins.then_inc(chain, 1)
                    dve.wait_ge(chain, n[0])

                dve.sem_inc(wn_ready, 2)
                dve.wait_ge(once, 16 * 7)
                link(nc.vector.tensor_tensor(gate_sq[:], gate_in[0:E, :], gate_in[0:E, :], ALU.mult))
                link(nc.vector.reduce_sum(gate_s[:, 0:1], gate_sq[:], axis=AX.X))
                dve.sem_inc(sq_ready, 1)
                dve.wait_ge(std_ready, 1)
                link(nc.vector.tensor_scalar(gate_s[:, 0:1], gate_s[:, 3:4], WN_EPS, None, ALU.max))
                link(nc.vector.reciprocal(gate_s[:, 0:1], gate_s[:, 0:1]))
                link(nc.vector.tensor_scalar(gate_in[0:E, :], gate_in[0:E, :], gate_s[:, 0:1], gate_s[:, 1:2], ALU.mult, ALU.mult))
                dve.sem_inc(gate_ready, 1)
                dve.wait_ge(gateT_done, 1)
                nc.vector.tensor_copy(gateT_h[:], r_ps[:, P:2 * P]).then_inc(chain, 1)
                n[0] += 1
                dve.wait_ge(chain, n[0])
                link(nc.vector.tensor_tensor(gateT_l[:], r_ps[:, P:2 * P], gateT_h[:], ALU.subtract))
                link(nc.vector.tensor_copy(t.cols[:, 0:ROWS], r_ps[:, 0:ROWS]))
                dve.sem_inc(gate_ready, 1)
                c1 = n[0]
                steps = 5
                with dve.Fori(0, E // 2) as it:
                    for k in range(2):
                        e = it * 2 + k
                        c0 = e * steps + c1
                        dve.wait_ge(w_loaded[k], it * 32 + 32)
                        nc.vector.tensor_tensor(w_sq[:], w_in[:, k], w_in[:, k], ALU.mult).then_inc(chain, 1)
                        dve.wait_ge(chain, c0 + 1)
                        nc.vector.reduce_sum(ss[:, 0:HC], w_sq[:, 0:HC], axis=AX.X)
                        nc.vector.reduce_sum(ss[:, HC:HC + 1], w_sq[:, HC:2 * HC], axis=AX.XY).then_inc(sq_ready, 1)
                        dve.wait_ge(std_ready, e + 2)
                        nc.vector.tensor_scalar(nrm[:], nrm[:], WN_EPS, None, ALU.max).then_inc(chain, 1)
                        dve.wait_ge(chain, c0 + 2)
                        nc.vector.reciprocal(nrm[:], nrm[:]).then_inc(chain, 1)
                        dve.wait_ge(chain, c0 + 3)
                        nc.vector.tensor_tensor(wscale[:, 0:HC], t.cols[:, bass.ds(e * HC + R_G1, HC)], nrm[:, 0:HC], ALU.mult)\
                            .then_inc(chain, 1)
                        nc.vector.tensor_tensor(wscale[:, HC:HC + 1], t.cols[:, bass.ds(e + R_G2, 1)], nrm[:, HC:HC + 1],
                                                ALU.mult).then_inc(chain, 1)
                        dve.wait_ge(chain, c0 + 5)
                        dve.wait_ge(wT_done, e * 2 + 2)
                        nc.vector.tensor_tensor(wn[:, k, 0:HC], w_in[:, k, 0:HC],
                                                wscale[:, 0:HC].unsqueeze(2).broadcast_to([P, HC, P]), ALU.mult)
                        nc.vector.tensor_scalar(wn[:, k, HC:2 * HC], w_in[:, k, HC:2 * HC], wscale[:, HC:HC + 1], None, ALU.mult)\
                            .then_inc(wn_ready, 1)
                        dve.wait_ge(w1_high, e + 1)
                        nc.vector.tensor_tensor(t.w1[:, bass.ds(e * 2 * FH + FH, FH)], wT_ps[:, k, 0],
                                                t.w1[:, bass.ds(e * 2 * FH, FH)], ALU.subtract).then_inc(w1_free, 1)
                n[0] += E * steps
                dve.wait_ge(order_ready, 4)
                dve.wait_ge(lg_done, 1)
                nc.vector.tensor_copy(lg[:], g_ps[:, 0, 0:B * QT * E].rearrange("p (t e) -> p t e", e=E)).then_inc(chain, 1)
                n[0] += 1
                dve.wait_ge(chain, n[0])
                link(nc.vector.reduce_max(lmax[:], lg[:], axis=AX.X))
                link(nc.vector.tensor_tensor(lg[:], lg[:], lmax[:].unsqueeze(2).broadcast_to([P, B * QT, E]), ALU.subtract))
                link(nc.vector.tensor_scalar(lg[:], lg[:], -104.0, None, ALU.max))
                shape = [P, B * QT, E, E]
                li, lj = lg[:].unsqueeze(3).broadcast_to(shape), lg[:].unsqueeze(2).broadcast_to(shape)
                link(nc.vector.tensor_tensor(cmp_a[:], lj, li, ALU.is_equal))
                link(nc.vector.tensor_tensor(cmp_a[:], cmp_a[:], before[:].unsqueeze(1).broadcast_to(shape), ALU.mult))
                link(nc.vector.tensor_tensor(cmp_b[:], lj, li, ALU.is_gt))
                link(nc.vector.tensor_tensor(cmp_a[:], cmp_a[:], cmp_b[:], ALU.add))
                link(nc.vector.reduce_sum(rank[:], cmp_a[:], axis=AX.X))
                nc.vector.tensor_scalar(rank[:], rank[:], 2.0, None, ALU.is_lt).then_inc(mask_ready, 1)
                for j in range(B):
                    dve.wait_ge(maskT_done, j + 1)
                    dst = slice(j * N, j * N + N)
                    nc.vector.tensor_copy(t.maskT[:, dst], g_ps[0:E, j % 2, :]).then_inc(maskT_ready, 1)
                    nc.vector.tensor_copy(t.maskT_b[:, dst], g_ps[0:E, j % 2, :]).then_inc(maskT_ready, 1)

            @block.tensor
            def _(pe):
                pe.wait_ge(once, 16 * 7)
                nc.tensor.transpose(r_ps[:, 0:P], rows[:], t.ident[:])
                pe.wait_ge(gate_ready, 1)
                nc.tensor.transpose(r_ps[:, P:2 * P], gate_in[:], t.ident[:]).then_inc(gateT_done, 1)
                pe.wait_ge(gate_ready, 2)
                for j in range(B):
                    xh, xl = (t.xs[:, (2 * j + i) * N:(2 * j + i + 1) * N] for i in range(2))
                    below(pe, lgT_ready, j - 1)
                    nc.tensor.matmul(g_ps[:, j % 2], gateT_h[:], xh, start=True, stop=False)
                    nc.tensor.matmul(g_ps[:, j % 2], gateT_h[:], xl, start=False, stop=False)
                    nc.tensor.matmul(g_ps[:, j % 2], gateT_l[:], xh, start=False, stop=True).then_inc(lgT_done, 1)
                pe.wait_ge(lgT_ready, B)
                for j in range(B * QT):
                    last = nc.tensor.transpose(g_ps[:, 0, j * E:j * E + E], lgT[:, j // QT, j % QT * P:j % QT * P + P],
                                               t.ident[0:E, 0:E])
                last.then_inc(lg_done, 1)
                pe.sem_inc(wT_done, 2 * 2)
                with pe.Fori(0, E // 2) as it:
                    for k in range(2):
                        e = it * 2 + k
                        pe.wait_ge(wn_ready, e + 3)
                        pe.wait_ge(w1_free, e + 1)
                        pe.wait_ge(w2_free, e + 1)
                        for half in range(2):
                            for c in range(HC):
                                last = nc.tensor.transpose(wT_ps[:, k, half, c * P:c * P + P], wn[:, k, half * HC + c], t.ident[:])
                            last.then_inc(wT_done, 1)
                pe.wait_ge(mask_ready, 1)
                for j in range(B):
                    below(pe, maskT_ready, 2 * j - 2)
                    for q in range(QT):
                        last = nc.tensor.transpose(g_ps[0:E, j % 2, q * P:q * P + P], rank[:, j * QT + q, :], t.ident[:])
                    last.then_inc(maskT_done, 1)

            @block.scalar
            def _(act):
                act.wait_ge(sq_ready, 1)
                nc.scalar.activation(gate_s[:, 3:4], gate_s[:, 0:1], ACT.Sqrt).then_inc(std_ready, 1)
                for j in range(B):
                    act.wait_ge(lgT_done, j + 1)
                    nc.scalar.activation(lgT[:, j], g_ps[0:E, j % 2], ACT.Identity, bias=gate_s[:, 2:3]).then_inc(lgT_ready, 1)
                act.sem_inc(w1_free, 2)
                act.sem_inc(w2_free, 2)
                with act.Fori(0, E // 2) as it:
                    for k in range(2):
                        e = it * 2 + k
                        act.wait_ge(sq_ready, e + 2)
                        nc.scalar.activation(nrm[:], ss[:, 0:HC + 1], ACT.Sqrt).then_inc(std_ready, 1)
                        act.wait_ge(wT_done, e * 2 + 6)
                        nc.scalar.activation(t.w1[:, bass.ds(e * 2 * FH, FH)], wT_ps[:, k, 0], ACT.Copy).then_inc(w1_high, 1)
                        nc.scalar.activation(t.w2[:, bass.ds(e * FH, FH)], wT_ps[:, k, 1], ACT.Copy).then_inc(w2_free, 1)


def experts(nc, t, out):
    with ExitStack() as ctx:
        def sb(name, shape, dt=F32):
            return ctx.enter_context(nc.sbuf_tensor("exp_" + name, shape, dt))

        def psum(name, shape):
            return ctx.enter_context(nc.psum_tensor("exp_" + name, shape, F32))

        def sem(name):
            return ctx.enter_context(nc.semaphore("exp_" + name))

        hid = sb("hid", [P, 4, N])
        hidm = sb("hidm", [P, 4, N])
        f_sb = sb("f_sb", [P, N])
        o_sb = sb("o_sb", [P, 2, N])
        h_ps, k_ps = psum("h_ps", [P, 2, N]), psum("k_ps", [P, 2, N])
        f_ps, ft_ps = psum("f_ps", [P, 2, N]), psum("ft_ps", [P, N])
        h_done, k_done, f_done, ft_done = sem("h_done"), sem("k_done"), sem("f_done"), sem("ft_done")
        silu_done, masked, w2_done, f_out, ready = (
            sem(n) for n in ("silu_done", "masked", "w2_done", "f_out", "ready"))
        stored = [sem("stored0"), sem("stored1")]
        UB = E * HC
        out_v = out.rearrange("b (t p) d -> b p t d", p=P)

        with nc.Block() as block:
            @block.tensor
            def _(pe):
                pe.sem_inc(w2_done, 4)
                with pe.Fori(0, B) as j:
                    xh, xl = (t.xs[:, bass.ds(j * 2 * N + i * N, N)] for i in range(2))

                    def first(i):
                        e, c = i // HC, i % HC
                        pe.wait_ge(silu_done, j * UB + i + 1)
                        wh = t.w1[:, e * 2 * FH + c * P:e * 2 * FH + c * P + P]
                        wl = t.w1[:, e * 2 * FH + FH + c * P:e * 2 * FH + FH + c * P + P]
                        nc.tensor.matmul(h_ps[:, i % 2], wh, xh, start=True, stop=False)
                        nc.tensor.matmul(h_ps[:, i % 2], wh, xl, start=False, stop=False)
                        nc.tensor.matmul(h_ps[:, i % 2], wl, xh, start=False, stop=True).then_inc(h_done, 1)
                        if c == 0:
                            nc.tensor.matmul(k_ps[:, e % 2], t.select[:, e, :], t.maskT_b[:, bass.ds(j * N, N)],
                                             start=True, stop=True).then_inc(k_done, 1)

                    first(0)
                    first(1)
                    for i in range(UB):
                        if i + 2 < UB:
                            first(i + 2)
                        pe.wait_ge(masked, j * UB + i + 6)
                        nc.tensor.matmul(f_ps[:, 0], t.w2[:, i * P:i * P + P], hidm[:, i % 4], start=i == 0, stop=False)\
                            .then_inc(w2_done, 1)
                    nc.tensor.matmul(f_ps[:, 0], t.b2[:], t.maskT[:, bass.ds(j * N, N)], start=False, stop=True).then_inc(f_done, 1)
                    pe.wait_ge(f_out, j + 1)
                    pe.wait_ge(ready, j + 1)
                    for q in range(QT):
                        last = nc.tensor.transpose(ft_ps[:, q * P:q * P + P], f_sb[:, q * P:q * P + P], t.ident[:])
                    last.then_inc(ft_done, 1)

            @block.scalar
            def _(act):
                act.sem_inc(silu_done, 2)
                with act.Fori(0, B) as j:
                    for i in range(UB):
                        act.wait_ge(h_done, j * UB + i + 1)
                        act.wait_ge(masked, j * UB + i + 2)
                        nc.scalar.activation(hid[:, i % 4], h_ps[:, i % 2], ACT.Silu, bias=t.cols[:, UB + i:UB + i + 1])\
                            .then_inc(silu_done, 1)
                    act.wait_ge(f_done, j + 1)
                    nc.scalar.activation(f_sb[:], f_ps[:, 0], ACT.Copy).then_inc(f_out, 1)

            @block.vector
            def _(dve):
                dve.sem_inc(masked, HC + 1)
                dve.sem_inc(ready, 1)
                for s in stored:
                    dve.sem_inc(s, 16)
                with dve.Fori(0, B // 2) as it:
                    for k in range(2):
                        j = it * 2 + k
                        for i in range(UB):
                            dve.wait_ge(silu_done, j * UB + i + 3)
                            if i % HC == 0:
                                dve.wait_ge(k_done, j * E + i // HC + 1)
                            dve.wait_ge(w2_done, j * UB + i + 1)
                            nc.vector.tensor_tensor(hidm[:, i % 4], k_ps[:, (i // HC) % 2], hid[:, i % 4], ALU.mult)\
                                .then_inc(masked, 1)
                        dve.wait_ge(ft_done, j + 1)
                        dve.wait_ge(stored[k], it * 16 + 16)
                        nc.vector.tensor_tensor(o_sb[:, k], ft_ps[:], t.res[:, bass.ds(j * N, N)], ALU.add).then_inc(ready, 1)

            @block.sync
            def _(sp):
                with sp.Fori(0, B // 2) as it:
                    for k in range(2):
                        j = it * 2 + k
                        sp.wait_ge(ready, j + 2)
                        sp.dma_start(out_v[bass.ds(j, 1)].rearrange("o p t d -> p (o t) d"),
                                     o_sb[:, k].rearrange("p (t d) -> p t d", d=P)).then_inc(stored[k], 16)
                for s in stored:
                    sp.wait_ge(s, 16 + B // 2 * 16)


def build(nc, a, out):
    class Shared:
        pass

    t = Shared()
    with ExitStack() as ctx:
        def sb(name, shape, dt=F32):
            return ctx.enter_context(nc.sbuf_tensor(name, shape, dt))

        t.xs = sb("xs", [P, B * 2 * N], F32R)
        t.ident = make_identity(nc, ctx, "ident")
        t.res = sb("res", [P, B * N])
        with ExitStack() as inner:
            t.yacc = inner.enter_context(nc.sbuf_tensor("yacc", [P, B * N], F32))
            with ExitStack() as deeper:
                def sbd(name, shape, dt=F32):
                    return deeper.enter_context(nc.sbuf_tensor(name, shape, dt))

                t.wall = sbd("wall", [P, NPAIR * WCOLS], F32R)
                t.wo_all = sbd("wo_all", [P, NPAIR * 2 * P])
                t.bias_all = sbd("bias_all", [P, NPAIR, 3])
                prepare_attention(nc, a, t)
                attention(nc, t)
            finish_attention(nc, a, t)
        t.w1 = sb("w1", [P, E * 2 * FH], F32R)
        t.w2 = sb("w2", [P, E * FH])
        t.cols = sb("cols", [P, 2 * E * HC + E])
        t.b2 = sb("b2_rows", [E, P])
        t.select = sb("select", [E, E, P], BF16)
        t.maskT = sb("maskT", [E, B * N])
        t.maskT_b = sb("maskT_b", [E, B * N], BF16)
        prepare_experts(nc, a, t)
        experts(nc, t, out)


_ATTN = ["x", "adaptive_scale", "Wq", "bq", "Wk", "bk", "Wv", "bv", "Wo", "bo", "gamma", "beta"]
_FFN = ["gate_v", "gate_g", "gate_b", "w1_v", "w1_g", "b1", "w2_v", "w2_g", "b2"]


def kernel(**inputs):
    import numpy as _np
    import concourse.bacc as _bacc
    from concourse import mybir as _mybir
    from concourse.bass_utils import run_bass_kernel_spmd as _run

    nc = _bacc.Bacc("TRN2", target_bir_lowering=False, num_devices=1)
    arrays, args = {}, {}
    for prefix, names in (("L0_attn_", _ATTN), ("L0_ffn_", _FFN)):
        for name in names:
            v = _np.ascontiguousarray(inputs[prefix + name])
            arrays[f"in_{name}"] = v
            args[name] = nc.dram_tensor(f"in_{name}", v.shape, _mybir.dt.from_np(v.dtype), kind="ExternalInput").ap()
    out = nc.dram_tensor("out_0", (B, N, D), F32, kind="ExternalOutput").ap()
    build(nc, args, out)
    r = _run(nc, [arrays], core_ids=[0])
    return r.results[0]["out_0"]
```

```python
from contextlib import ExitStack

import concourse.bass as bass
from concourse import mybir

F32 = mybir.dt.float32
F32R = mybir.dt.float32r
BF16 = mybir.dt.bfloat16
I32 = mybir.dt.int32
ALU = mybir.AluOpType
ACT = mybir.ActivationFunctionType
AX = mybir.AxisListType

P = 128
B, N, D = 8, 512, 128
H, HD = 16, 64
E, FH = 8, 512
QT = N // P
NPAIR = H // 2
PAIRS = B * NPAIR
UNITS = PAIRS * 2 * QT
HC = FH // P
SCALE = float(HD) ** -0.5
TILES = B * QT
BLOCKS = (2 * B * N + E * (P - 1)) // P
BLOCKS += -BLOCKS % 4
LN_EPS = 1e-5
WN_EPS = 1e-12
QH, QL, KH, KL, VH, VL, WCOLS = 0, 128, 256, 512, 768, 896, 1024


def below(eng, sem, value):
    if not isinstance(value, int) or value > 0:
        eng.wait_ge(sem, value)


def make_identity(nc, ctx, name):
    ident = ctx.enter_context(nc.sbuf_tensor(name, [P, P], F32))
    cleared = ctx.enter_context(nc.semaphore(name + "_cleared"))
    with nc.Block() as block:
        @block.gpsimd
        def _(pool):
            pool.memset(ident[:], 0.0).then_inc(cleared, 1)
            pool.wait_ge(cleared, 1)
            pool.affine_select(out=ident[:], in_=ident[:], compare_op=ALU.not_equal, fill=1.0,
                               base=0, pattern=[[-1, P]], channel_multiplier=1)
    return ident


def prepare_attention(nc, a, t):
    with ExitStack() as ctx:
        def sb(name, shape, dt=F32):
            return ctx.enter_context(nc.sbuf_tensor(name, shape, dt))

        def sem(name):
            return ctx.enter_context(nc.semaphore(name))

        x_in = sb("x_in", [P, 2, QT, P])
        xn = sb("xn", [P, 2, QT, P])
        w_in = sb("w_in", [P, 2, 4, P])
        stats = sb("stats", [P, 2, QT, 6])
        mv = sb("mv", [P, 2, QT, 2])
        rstd = sb("rstd", [P, 2, QT])
        wo_nat = sb("wo_nat", [P, H * HD])
        bv_row = sb("bv_row", [P, H * HD])
        wo_bv = sb("wo_bv", [P, H * HD])
        out_bias = sb("out_bias", [P, 4])
        q_scale = sb("q_scale", [P, NPAIR])
        b_in = sb("b_in", [P, 3, NPAIR])
        xT_ps = ctx.enter_context(nc.psum_tensor("xT_ps", [P, 2, N], F32))
        wT_ps = ctx.enter_context(nc.psum_tensor("wT_ps", [P, 2, 4, P], F32))
        once = sem("once")
        x_loaded = [sem("x_loaded0"), sem("x_loaded1")]
        w_loaded = [sem("w_loaded0"), sem("w_loaded1")]
        x_free, w_free = sem("x_free"), sem("w_free")
        xn_free, xT_free, wT_free = sem("xn_free"), sem("xT_free"), sem("wT_free")
        chain = sem("chain")
        var_ready, std_ready = sem("var_ready"), sem("std_ready")
        xn_ready, wq_scaled = sem("xn_ready"), sem("wq_scaled")
        xn_kept, zeroed, zero_ready = [sem("xn_kept0"), sem("xn_kept1")], sem("zeroed"), sem("zero_ready")
        zeros = sb("zeros", [P, BLOCKS // 8 * P])
        xT_done, wT_done = sem("xT_done"), sem("wT_done")
        x_high, w_high = sem("x_high"), sem("w_high")

        x_v = a["x"].rearrange("b (t p) d -> b p t d", p=P)
        steps = B
        assert steps == NPAIR

        with nc.Block() as block:
            @block.sync
            def _(sp):
                sp.dma_start(wo_nat[:], a["Wo"]).then_inc(once, 16)
                sp.dma_start(bv_row[:], a["bv"].rearrange("(o n) -> o n", o=1).broadcast_to([P, H * HD])).then_inc(once, 16)
                sp.dma_start(out_bias[:, 0:1], a["bo"].rearrange("(p o) -> p o", o=1)).then_inc(once, 16)
                for half in range(2):
                    rows = slice(half * HD, half * HD + HD)
                    sp.dma_start(q_scale[rows, :], a["adaptive_scale"].rearrange("(o r h) -> h o r", h=2, o=1)[half]
                                 .broadcast_to([HD, NPAIR]), allow_slow_non_contiguous=True).then_inc(once, 16)
                    for head in range(2):
                        sp.dma_start(b_in[rows, 1 + head, :], a["bk"].rearrange("(r h p) -> h p r", h=2, p=HD)[head],
                                     allow_slow_non_contiguous=True)\
                            .then_inc(once, 16)
                sp.dma_start(b_in[:, 0, :], a["bq"].rearrange("(r p) -> p r", p=P), allow_slow_non_contiguous=True).then_inc(once, 16)
                sp.wait_ge(zero_ready, 1)
                for part in range(8):
                    sp.dma_start(t.x_rows.rearrange("(g p r) d -> g p (r d)", g=8, p=P)[part], zeros[:]).then_inc(zeroed, 16)
                with sp.Fori(0, steps // 2) as it:
                    for k in range(2):
                        j = it * 2 + k
                        sp.wait_ge(x_free, j + 1)
                        sp.dma_start(x_in[:, k], x_v[bass.ds(j, 1)].rearrange("o p t d -> p (o t) d")).then_inc(x_loaded[k], 16)
                        sp.wait_ge(w_free, j + 1)
                        for i, w in enumerate(("Wq", "Wk", "Wv")):
                            sp.dma_start(w_in[:, k, i], a[w][bass.ds(j * P, P), :]).then_inc(w_loaded[k], 16)
                        sp.dma_start(w_in[:, k, 3], a["Wo"][:, bass.ds(j * P, P)]).then_inc(w_loaded[k], 16)

            @block.vector
            def _(dve):
                dve.sem_inc(x_free, 2)
                for s in xn_kept:
                    dve.sem_inc(s, 1)
                dve.wait_ge(once, 16 * 10)
                nc.vector.tensor_tensor(wo_bv[:], wo_nat[:], bv_row[:], ALU.mult).then_inc(chain, 1)
                dve.wait_ge(chain, 1)
                nc.vector.reduce_sum(out_bias[:, 1:2], wo_bv[:], axis=AX.X).then_inc(chain, 1)
                dve.wait_ge(chain, 2)
                nc.vector.tensor_tensor(out_bias[:, 2:3], out_bias[:, 0:1], out_bias[:, 1:2], ALU.add).then_inc(chain, 1)
                nc.vector.tensor_scalar(q_scale[:], q_scale[:], SCALE, None, ALU.mult).then_inc(chain, 1)
                dve.wait_ge(chain, 4)
                nc.vector.tensor_tensor(t.bias_all[:, :, 0], b_in[:, 0, :], q_scale[:], ALU.mult).then_inc(chain, 1)
                nc.vector.tensor_copy(t.bias_all[:, :, 1:3], b_in[:, 1:3, :].rearrange("p h r -> p r h")).then_inc(chain, 1)
                nc.vector.memset(out_bias[:, 3:4], LN_EPS).then_inc(chain, 1)
                dve.wait_ge(chain, 7)
                with dve.Fori(0, steps // 2) as it:
                    for k in range(2):
                        j = it * 2 + k
                        dve.wait_ge(x_loaded[k], it * 16 + 16)
                        c0 = j * (2 * QT + 1) + 7
                        for q in range(QT):
                            nc.vector.bn_stats(stats[:, k, q], x_in[:, k, q]).then_inc(chain, 1)
                        dve.wait_ge(chain, c0 + QT)
                        dve.wait_ge(w_loaded[k], it * 64 + 64)
                        nc.vector.tensor_scalar(w_in[:, k, 0], w_in[:, k, 0], q_scale[:, bass.ds(j, 1)], None, ALU.mult)\
                            .then_inc(wq_scaled, 1)
                        for q in range(QT):
                            nc.vector.bn_aggr(mv[:, k, q], stats[:, k, q]).then_inc(chain, 1)
                        dve.wait_ge(chain, c0 + 2 * QT)
                        dve.sem_inc(var_ready, 1)
                        dve.wait_ge(std_ready, j + 1)
                        nc.vector.reciprocal(rstd[:, k], rstd[:, k]).then_inc(chain, 1)
                        dve.wait_ge(chain, c0 + 2 * QT + 1)
                        dve.wait_ge(xn_free, j + 1)
                        dve.wait_ge(xn_kept[k], it + 1)
                        for q in range(QT):
                            last = nc.vector.tensor_scalar(xn[:, k, q], x_in[:, k, q], mv[:, k, q, 0:1], rstd[:, k, q:q + 1],
                                                           ALU.subtract, ALU.mult)
                        last.then_inc(xn_ready, 1)
                        dve.wait_ge(xn_ready, j + 1)
                        dve.sem_inc(x_free, 1)
                        dve.wait_ge(x_high, j + 1)
                        nc.vector.tensor_scalar(t.yacc[:, bass.ds(j * N, N)], xT_ps[:, k], out_bias[:, 2:3], None, ALU.add)
                        nc.vector.tensor_tensor(t.xs[:, bass.ds(j * 2 * N + N, N)], xT_ps[:, k],
                                                t.xs[:, bass.ds(j * 2 * N, N)], ALU.subtract).then_inc(xT_free, 1)
                        dve.wait_ge(w_high, j + 1)
                        w0 = j * WCOLS
                        nc.vector.tensor_tensor(t.wall[:, bass.ds(w0 + QL, P)], wT_ps[:, k, 0],
                                                t.wall[:, bass.ds(w0 + QH, P)], ALU.subtract)
                        for head in range(2):
                            src = wT_ps[:, k, 1, head * HD:head * HD + HD].unsqueeze(1).broadcast_to([P, 2, HD])
                            nc.vector.tensor_tensor(
                                t.wall[:, bass.ds(w0 + KL + head * P, P)].rearrange("p (c n) -> p c n", c=2), src,
                                t.wall[:, bass.ds(w0 + KH + head * P, P)].rearrange("p (c n) -> p c n", c=2), ALU.subtract)
                        nc.vector.tensor_tensor(t.wall[:, bass.ds(w0 + VL, P)], wT_ps[:, k, 2],
                                                t.wall[:, bass.ds(w0 + VH, P)], ALU.subtract).then_inc(wT_free, 1)

            @block.gpsimd
            def _(pool):
                pool.memset(zeros[:], 0.0).then_inc(zero_ready, 1)
                with pool.Fori(0, steps // 2) as it:
                    for k in range(2):
                        j = it * 2 + k
                        pool.wait_ge(xn_ready, j + 1)
                        pool.tensor_copy(t.xn_rows[:, bass.ds(j * N, N)].rearrange("p (t d) -> p t d", d=P), xn[:, k])\
                            .then_inc(xn_kept[k], 1)
                pool.wait_ge(zeroed, 8 * 16)

            @block.tensor
            def _(pe):
                pe.sem_inc(w_free, 2)
                pe.sem_inc(xn_free, 2)
                with pe.Fori(0, steps // 2) as it:
                    for k in range(2):
                        j = it * 2 + k
                        pe.wait_ge(xn_ready, j + 1)
                        pe.wait_ge(xT_free, j + 1)
                        for q in range(QT):
                            nc.tensor.transpose(xT_ps[:, k, q * P:q * P + P], xn[:, k, q], t.ident[:])\
                                .then_inc(xT_done, 1)
                        pe.wait_ge(xT_done, j * QT + QT)
                        pe.sem_inc(xn_free, 1)
                        pe.wait_ge(wq_scaled, j + 1)
                        pe.wait_ge(wT_free, j + 1)
                        for i in range(4):
                            nc.tensor.transpose(wT_ps[:, k, i], w_in[:, k, i], t.ident[:]).then_inc(wT_done, 1)
                        pe.wait_ge(wT_done, j * 4 + 4)
                        pe.sem_inc(w_free, 1)

            @block.scalar
            def _(act):
                act.sem_inc(xT_free, 2)
                act.sem_inc(wT_free, 2)
                with act.Fori(0, steps // 2) as it:
                    for k in range(2):
                        j = it * 2 + k
                        act.wait_ge(var_ready, j + 1)
                        nc.scalar.activation(rstd[:, k], mv[:, k, :, 1], ACT.Sqrt, bias=out_bias[:, 3:4]).then_inc(std_ready, 1)
                        act.wait_ge(xT_done, j * QT + QT)
                        nc.scalar.activation(t.xs[:, bass.ds(j * 2 * N, N)], xT_ps[:, k], ACT.Copy).then_inc(x_high, 1)
                        act.wait_ge(wT_done, j * 4 + 4)
                        w0 = j * WCOLS
                        nc.scalar.activation(t.wall[:, bass.ds(w0 + QH, P)], wT_ps[:, k, 0], ACT.Copy)
                        for head in range(2):
                            src = wT_ps[:, k, 1, head * HD:head * HD + HD].unsqueeze(1).broadcast_to([P, 2, HD])
                            nc.scalar.activation(t.wall[:, bass.ds(w0 + KH + head * P, P)].rearrange("p (c n) -> p c n", c=2),
                                                 src, ACT.Copy)
                        nc.scalar.activation(t.wall[:, bass.ds(w0 + VH, P)], wT_ps[:, k, 2], ACT.Copy)
                        for head in range(2):
                            for half in range(2):
                                last = nc.scalar.activation(
                                    t.wo_all[half * HD:half * HD + HD, bass.ds(j * 2 * P + head * P, P)],
                                    wT_ps[head * HD:head * HD + HD, k, 3], ACT.Copy)
                        last.then_inc(w_high, 1)


def attention(nc, t):
    with ExitStack() as ctx:
        def sb(name, shape, dt=F32):
            return ctx.enter_context(nc.sbuf_tensor(name, shape, dt))

        def psum(name, shape):
            return ctx.enter_context(nc.psum_tensor(name, shape, F32))

        def sem(name):
            return ctx.enter_context(nc.semaphore(name))

        x_st = sb("x_st", [P, 2, 2 * N], F32R)
        w_st = sb("w_st", [P, 2, WCOLS], F32R)
        b_st = sb("b_st", [P, 2, 3])
        wo_st = sb("wo_st", [P, 2, 2 * P])
        row_st = sb("row_st", [P, 2, 1], I32)
        picked = sb("picked_sb", [P, 2, D])
        k_full = sb("k_full", [P, N])
        q_sb = sb("q_sb", [P, 4, N], F32R)
        kh_sb = sb("kh_sb", [P, 4, N], F32R)
        kl_sb = sb("kl_sb", [P, 4, N], F32R)
        v_sb = sb("v_sb", [P, 2, 2, QT, P], F32R)
        probs = sb("probs", [P, 4, N])
        pth = sb("pth", [P, 2, QT, N], F32R)
        ptl = sb("ptl", [P, 2, QT, N], F32R)
        o_sb = sb("o_sb", [P, 2, N])
        nmax = sb("nmax", [P, 8])
        rsum = sb("rsum", [P, 8])
        rinv = sb("rinv", [P, 8])
        s_ps = psum("s_ps", [P, 2, N])
        t_ps = psum("t_ps", [P, 2, N])
        o_ps = psum("o_ps", [P, 2, N])
        qo_ps = psum("qo_ps", [P, N])
        kv_ps = psum("kv_ps", [P, N])

        st_loaded = [sem("st_loaded0"), sem("st_loaded1")]
        wo_loaded = [sem("wo_loaded0"), sem("wo_loaded1")]
        rows_loaded, picked_up, picked_stored = ([sem(f"{n}{i}") for i in range(2)]
                                                 for n in ("rows_loaded", "picked_up", "picked_stored"))
        s_done, t_done, pv_done = sem("s_done"), sem("t_done"), sem("pv_done")
        q_mm, k_mm, v_mm, wo_mm = sem("q_mm"), sem("k_mm"), sem("v_mm"), sem("wo_mm")
        k_copied, q_high, k_high, v_high = sem("k_copied"), sem("q_high"), sem("k_high"), sem("v_high")
        q_low, k_low, v_low, y_added = sem("q_low"), sem("k_low"), sem("v_low"), sem("y_added")
        max_done, exp_done, inv_done, norm_done = sem("max_done"), sem("exp_done"), sem("inv_done"), sem("norm_done")
        ph_done, pl_done, o_done = sem("ph_done"), sem("pl_done"), sem("o_done")

        def valid(it, unit, low=0, high=UNITS):
            return not isinstance(it, int) or low <= 16 * it + unit < high

        def pair_ok(it, pair):
            return not isinstance(it, int) or 0 <= 2 * it + pair < PAIRS

        PE_TASKS = {0: ("q", 0, 1), 1: ("k", 0, 1), 3: ("k", 1, 1), 4: ("wo", 0, -1), 5: ("wo", 1, -1), 6: ("v", 0, 1)}
        ACT_TASKS = {1: ("q", 0, 1), 2: ("k", 0, 1), 3: ("q", 1, 1), 5: ("k", 1, 1), 7: ("v", 0, 1)}
        DVE_TASKS = {0: ("v", 0, 0), 2: ("q", 0, 1), 3: ("k", 0, 1), 4: ("q", 1, 1), 6: ("k", 1, 1), 7: ("wo", 0, -1)}
        POOL_TASKS = {3: ("k", 0, 1), 6: ("k", 1, 1)}

        def task(it, l, tasks):
            found = tasks.get(l % 8)
            if not found or not pair_ok(it, l // 8 + found[2]):
                return None
            return found[0], found[1], l // 8 + found[2], it * 2 + l // 8 + found[2]

        def pe_slot(pe, it, l):
            u = it * 16 + l
            if valid(it, l + 3):
                g, qt, bank = (l + 3) // 4, (l + 3) % 4, (l + 3) % 2
                if qt == 0:
                    pe.wait_ge(q_low, it * 4 + g + 1)
                    pe.wait_ge(k_low, it * 4 + g + 1)
                below(pe, exp_done, u + 2)
                lhs = q_sb[:, g % 4, qt * P:qt * P + P]
                nc.tensor.matmul(s_ps[:, bank], lhs, kh_sb[:, g % 4], start=True, stop=False)
                nc.tensor.matmul(s_ps[:, bank], lhs, kl_sb[:, g % 4], start=False, stop=True).then_inc(s_done, 1)
            if valid(it, l):
                below(pe, norm_done, u + 1)
                below(pe, pl_done, u - 1)
                for kc in range(QT):
                    last = nc.tensor.transpose(t_ps[:, l % 2, kc * P:kc * P + P], probs[:, l % 4, kc * P:kc * P + P],
                                               t.ident[:])
                last.then_inc(t_done, 1)
            if valid(it, l - 4):
                g, kc = l // 4 - 1, l % 4
                if kc == 0:
                    pe.wait_ge(pl_done, it * 16 + 4 * g + 4)
                    below(pe, o_done, it * 4 + g - 1)
                    if g % 2 == 0:
                        pe.wait_ge(v_low, it * 2 + g // 2 + 1)
                for part, pt in enumerate((pth, ptl)):
                    last = nc.tensor.matmul(o_ps[:, g % 2], v_sb[:, (g // 2) % 2, g % 2, kc], pt[:, g % 2, kc],
                                            start=kc + part == 0, stop=kc + part == QT)
                if kc == 3:
                    last.then_inc(pv_done, 1)
            found = task(it, l, PE_TASKS)
            if found:
                kind, head, pr, pi = found
                st = pr % 2
                xh, xl = x_st[:, st, 0:N], x_st[:, st, N:2 * N]
                w = w_st[:, st]
                if kind == "q":
                    pe.wait_ge(st_loaded[st], (it + pr // 2 + 1) * 48)
                    below(pe, y_added, pi - 2)
                    nc.tensor.matmul(qo_ps[:], w[:, QH:QH + P], xh, start=True, stop=False)
                    nc.tensor.matmul(qo_ps[:], w[:, QH:QH + P], xl, start=False, stop=False)
                    nc.tensor.matmul(qo_ps[:], w[:, QL:QL + P], xh, start=False, stop=True).then_inc(q_mm, 1)
                elif kind == "k":
                    if head == 0:
                        below(pe, v_low, pi)
                    else:
                        pe.wait_ge(k_copied, pi * 2 + 1)
                    hi = w[:, KH + head * P:KH + head * P + P]
                    nc.tensor.matmul(kv_ps[:], hi, xh, start=True, stop=False)
                    nc.tensor.matmul(kv_ps[:], hi, xl, start=False, stop=False)
                    nc.tensor.matmul(kv_ps[:], w[:, KL + head * P:KL + head * P + P], xh, start=False, stop=True)\
                        .then_inc(k_mm, 1)
                elif kind == "v":
                    pe.wait_ge(k_copied, pi * 2 + 2)
                    for kc in range(QT):
                        out = kv_ps[:, kc * P:kc * P + P]
                        xhk, xlk = xh[:, kc * P:kc * P + P], xl[:, kc * P:kc * P + P]
                        nc.tensor.matmul(out, xhk, w[:, VH:VH + P], start=True, stop=False)
                        nc.tensor.matmul(out, xhk, w[:, VL:VL + P], start=False, stop=False)
                        last = nc.tensor.matmul(out, xlk, w[:, VH:VH + P], start=False, stop=True)
                    last.then_inc(v_mm, 1)
                else:
                    pe.wait_ge(o_done, pi * 2 + head + 1)
                    if head == 0:
                        pe.wait_ge(wo_loaded[st], (it + pr // 2 + 1) * 16)
                        if pair_ok(it, pr + 2):
                            pe.wait_ge(q_low, pi * 2 + 6)
                        else:
                            pe.wait_ge(y_added, pi)
                    nc.tensor.matmul(qo_ps[:], wo_st[:, st, head * P:head * P + P], o_sb[:, head],
                                     start=head == 0, stop=head == 1).then_inc(wo_mm, 1)

        def act_slot(act, it, l):
            u = it * 16 + l
            if l % 4 == 0 and valid(it, l - 8):
                g = l // 4 - 2
                gi = it * 4 + g
                act.wait_ge(pv_done, gi + 1)
                below(act, wo_mm, gi - 1)
                nc.scalar.activation(o_sb[:, g % 2], o_ps[:, g % 2], ACT.Copy).then_inc(o_done, 1)
            if valid(it, l + 2):
                act.wait_ge(max_done, u + 3)
                below(act, t_done, u - 1)
                m = (l + 2) % 8
                nc.scalar.activation(probs[:, (l + 2) % 4], s_ps[:, l % 2], ACT.Exp, bias=nmax[:, m:m + 1],
                                     accum_out=rsum[:, m:m + 1]).then_inc(exp_done, 1)
            if valid(it, l):
                g, qt = l // 4, l % 4
                act.wait_ge(t_done, u + 1)
                if qt == 0:
                    below(act, pv_done, it * 4 + g - 1)
                nc.scalar.activation(pth[:, g % 2, :, qt * P:qt * P + P],
                                     t_ps[:, l % 2].rearrange("p (c q) -> p c q", c=QT), ACT.Copy).then_inc(ph_done, 1)
            found = task(it, l, ACT_TASKS)
            if found:
                kind, head, pr, pi = found
                st = pr % 2
                if kind == "q":
                    rows = slice(head * HD, head * HD + HD)
                    act.wait_ge(q_mm, pi + 1)
                    below(act, s_done, pi * 8 - 8)
                    nc.scalar.activation(q_sb[rows, st * 2 + head], qo_ps[rows], ACT.Identity, bias=b_st[rows, st, 0:1])\
                        .then_inc(q_high, 1)
                elif kind == "k":
                    act.wait_ge(k_mm, pi * 2 + head + 1)
                    below(act, k_low, pi * 2 + head)
                    nc.scalar.activation(k_full[:], kv_ps[:], ACT.Identity, bias=b_st[:, st, 1 + head:2 + head])\
                        .then_inc(k_copied, 1)
                else:
                    act.wait_ge(v_mm, pi + 1)
                    below(act, pv_done, pi * 2 - 2)
                    nc.scalar.activation(v_sb[:, st, :, :, 0:HD].rearrange("p h c n -> p c h n"),
                                         kv_ps[:].rearrange("p (c h n) -> p c h n", c=QT, h=2), ACT.Copy).then_inc(v_high, 1)

        def dve_slot(dve, it, l):
            u = it * 16 + l
            if valid(it, l + 1):
                dve.wait_ge(exp_done, u + 2)
                m = (l + 1) % 8
                nc.vector.reciprocal(rinv[:, m:m + 1], rsum[:, m:m + 1]).then_inc(inv_done, 1)
            found = task(it, l, DVE_TASKS)
            if found:
                kind, head, pr, pi = found
                st = pr % 2
                if kind == "q":
                    rows, other = slice(head * HD, head * HD + HD), slice(HD - head * HD, P - head * HD)
                    dve.wait_ge(q_high, pi * 2 + head + 1)
                    nc.vector.scalar_tensor_tensor(q_sb[other, st * 2 + head], qo_ps[rows], b_st[rows, st, 0:1],
                                                   q_sb[rows, st * 2 + head], ALU.add, ALU.subtract).then_inc(q_low, 1)
                elif kind == "k":
                    dve.wait_ge(k_copied, pi * 2 + head + 1)
                    below(dve, s_done, pi * 8 - 8)
                    nc.vector.tensor_copy(kh_sb[:, st * 2 + head], k_full[:]).then_inc(k_high, 1)
                elif kind == "v":
                    dve.wait_ge(v_high, pi + 1)
                    nc.vector.tensor_tensor(v_sb[:, st, :, :, HD:P].rearrange("p h c n -> p c h n"),
                                            kv_ps[:].rearrange("p (c h n) -> p c h n", c=QT, h=2),
                                            v_sb[:, st, :, :, 0:HD].rearrange("p h c n -> p c h n"), ALU.subtract)\
                        .then_inc(v_low, 1)
                else:
                    dve.wait_ge(wo_mm, pi * 2 + 2)
                    below(dve, y_added, pi)
                    acc = t.yacc[:, bass.ds(pi // NPAIR * N, N)]
                    nc.vector.tensor_tensor(acc, qo_ps[:], acc, ALU.add).then_inc(y_added, 1)
            if valid(it, l + 3):
                dve.wait_ge(s_done, u + 4)
                m = (l + 3) % 8
                nc.vector.tensor_reduce(nmax[:, m:m + 1], s_ps[:, (l + 3) % 2], axis=AX.X, op=ALU.max, negate=True)\
                    .then_inc(max_done, 1)
            if valid(it, l):
                g, qt = l // 4, l % 4
                dve.wait_ge(ph_done, u + 1)
                sl = slice(qt * P, qt * P + P)
                nc.vector.tensor_tensor(ptl[:, g % 2, :, sl], t_ps[:, l % 2].rearrange("p (c q) -> p c q", c=QT),
                                        pth[:, g % 2, :, sl], ALU.subtract).then_inc(pl_done, 1)

        def pool_slot(pool, it, l):
            u = it * 16 + l
            fetch = l % 8 == 4 and pair_ok(it, l // 8)
            if fetch:
                st, i = l // 8 % 2, it + l // 8 // 2
                pool.wait_ge(rows_loaded[st], i * 16 + 16)
                below(pool, picked_stored[st], i * 16)
            if valid(it, l + 1):
                pool.wait_ge(inv_done, u + 2)
                m, pb = (l + 1) % 8, probs[:, (l + 1) % 4]
                nc.gpsimd.tensor_tensor(pb, pb, rinv[:, m:m + 1].broadcast_to([P, N]), ALU.mult).then_inc(norm_done, 1)
            if fetch:
                pool.indirect_dma_start(picked[:, st], None, t.y_rows, bass.IndirectOffsetOnAxis(ap=row_st[:, st], axis=0))\
                    .then_inc(picked_up[st], 16)
            found = task(it, l, POOL_TASKS)
            if found:
                kind, head, pr, pi = found
                pool.wait_ge(k_high, pi * 2 + head + 1)
                nc.gpsimd.tensor_tensor(kl_sb[:, pr % 2 * 2 + head], k_full[:], kh_sb[:, pr % 2 * 2 + head], ALU.subtract)\
                    .then_inc(k_low, 1)

        def engine_program(eng, slot):
            for l in range(-8, 16):
                slot(eng, 0, l)
            with eng.Fori(1, PAIRS // 2 - 1) as it:
                for l in range(16):
                    slot(eng, it, l)
            for l in range(16, 16 + 16 + 12):
                slot(eng, PAIRS // 2 - 2, l)

        with nc.Block() as block:
            @block.sync
            def _(sp):
                def stage(it, pr):
                    st, pi = pr % 2, it * 2 + pr
                    below(sp, v_mm, pi - 1)
                    below(sp, k_copied, pi * 2 - 2)
                    below(sp, q_low, pi * 2 - 2)
                    sp.dma_start(x_st[:, st].bitcast(F32), t.xs[:, bass.ds(pi // NPAIR * (2 * N), 2 * N)].bitcast(F32)).then_inc(st_loaded[st], 16)
                    sp.dma_start(w_st[:, st].bitcast(F32), t.wall[:, bass.ds(pi % NPAIR * WCOLS, WCOLS)].bitcast(F32)).then_inc(st_loaded[st], 16)
                    sp.dma_start(b_st[:, st], t.bias_all[:, bass.ds(pi % NPAIR, 1), :].rearrange("p o c -> p (o c)"))\
                        .then_inc(st_loaded[st], 16)

                def stage_wo(it, pr):
                    st, pi = pr % 2, it * 2 + pr
                    below(sp, wo_mm, pi * 2 - 2)
                    sp.dma_start(wo_st[:, st], t.wo_all[:, bass.ds(pi % NPAIR * (2 * P), 2 * P)]).then_inc(wo_loaded[st], 16)

                def fetch_rows(it, pr):
                    i = it + pr // 2
                    below(sp, picked_up[pr % 2], i * 16)
                    sp.dma_start(row_st[:, pr % 2], t.token_rows[:, pr % 2, bass.ds(i, 1)]).then_inc(rows_loaded[pr % 2], 16)

                def store_rows(it, pr):
                    i = it + pr // 2
                    sp.wait_ge(picked_up[pr % 2], i * 16 + 16)
                    sp.dma_start(t.picked[pr % 2, bass.ds(i * P, P), :], picked[:, pr % 2]).then_inc(picked_stored[pr % 2], 16)

                stage(0, 0)
                stage(0, 1)
                fetch_rows(0, 0)
                fetch_rows(0, 1)
                for pr in range(2):
                    stage_wo(0, pr)
                    stage(0, pr + 2)
                    store_rows(0, pr)
                    fetch_rows(0, pr + 2)
                with sp.Fori(1, PAIRS // 2 - 1) as it:
                    for pr in range(2):
                        stage_wo(it, pr)
                        stage(it, pr + 2)
                        store_rows(it, pr)
                        fetch_rows(it, pr + 2)
                for pr in range(2):
                    stage_wo(PAIRS // 2 - 1, pr)
                    store_rows(PAIRS // 2 - 1, pr)
                for s in picked_stored:
                    sp.wait_ge(s, PAIRS // 2 * 16)

            @block.tensor
            def _(pe):
                engine_program(pe, pe_slot)

            @block.scalar
            def _(act):
                engine_program(act, act_slot)

            @block.vector
            def _(dve):
                engine_program(dve, dve_slot)

            @block.gpsimd
            def _(pool):
                engine_program(pool, pool_slot)


def finish(nc, a, t, out):
    with ExitStack() as ctx:
        def sb(name, shape, dt=F32):
            return ctx.enter_context(nc.sbuf_tensor("fin_" + name, shape, dt))

        def sem(name):
            return ctx.enter_context(nc.semaphore("fin_" + name))

        x_in = sb("x_in", [P, 2, QT, P])
        yb = sb("yb", [P, 2, N])
        stats = sb("stats", [P, 2, QT, 6])
        mv = sb("mv", [P, 2, QT, 2])
        rstd = sb("rstd", [P, 2, QT])
        stored = [sem("stored0"), sem("stored1")]
        yn = sb("yn", [P, 2, QT, P])
        picked = sb("picked", [P, 2, 2, N])
        out_sb = sb("out_sb", [P, 2, QT, P])
        gamma, beta, eps = sb("gamma", [P, P]), sb("beta", [P, P]), sb("eps", [P, 1])
        yT_ps = ctx.enter_context(nc.psum_tensor("fin_yT_ps", [P, 2, QT, P], F32))
        once, eps_set, experts_added = sem("once"), sem("eps_set"), sem("experts_added")
        x_loaded = [sem("x_loaded0"), sem("x_loaded1")]
        y_copied, yT_done = sem("y_copied"), sem("yT_done")
        chain, var_ready, std_ready, block_done = sem("chain"), sem("var_ready"), sem("std_ready"), sem("block_done")
        x_v = a["x"].rearrange("b (t p) d -> b p t d", p=P)
        out_v = out.rearrange("b (t p) d -> b p t d", p=P)

        with nc.Block() as block:
            @block.sync
            def _(sp):
                for dst, src in ((gamma, "gamma"), (beta, "beta")):
                    sp.dma_start(dst[:], a[src].rearrange("(o n) -> o n", o=1).broadcast_to([P, P])).then_inc(once, 16)
                with sp.Fori(0, B // 2) as it:
                    for k in range(2):
                        sp.wait_ge(block_done, it * 2 + k + 1)
                        sp.dma_start(x_in[:, k], x_v[bass.ds(it * 2 + k, 1)].rearrange("o p t d -> p (o t) d"))\
                            .then_inc(x_loaded[k], 16)
                        for which in range(2):
                            sp.dma_start(picked[:, k, which].rearrange("p (t d) -> p t d", d=P),
                                         t.picked[which].rearrange("(b t p) d -> b p t d", p=P, t=QT)[bass.ds(it * 2 + k, 1)]
                                         .rearrange("o p t d -> p (o t) d")).then_inc(x_loaded[k], 16)

                for s in stored:
                    sp.wait_ge(s, 16 + B // 2 * 16)

            @block.scalar
            def _(act):
                act.wait_ge(eps_set, 1)
                with act.Fori(0, B // 2) as it:
                    for k in range(2):
                        j = it * 2 + k
                        act.wait_ge(block_done, j + 1)
                        nc.scalar.activation(yb[:, k], t.yacc[:, bass.ds(j * N, N)], ACT.Copy).then_inc(y_copied, 1)
                        act.wait_ge(var_ready, j + 1)
                        nc.scalar.activation(rstd[:, k], mv[:, k, :, 1], ACT.Sqrt, bias=eps[:]).then_inc(std_ready, 1)
                        act.wait_ge(block_done, j + 3)
                        act.dma_start(out_v[bass.ds(j, 1)].rearrange("o p t d -> p (o t) d"), out_sb[:, k])\
                            .then_inc(stored[k], 16)

            @block.tensor
            def _(pe):
                with pe.Fori(0, B // 2) as it:
                    for k in range(2):
                        pe.wait_ge(y_copied, it * 2 + k + 1)
                        for q in range(QT):
                            last = nc.tensor.transpose(yT_ps[:, k, q], yb[:, k, q * P:q * P + P], t.ident[:])
                        last.then_inc(yT_done, 1)

            @block.vector
            def _(dve):
                dve.sem_inc(block_done, 2)
                for s in stored:
                    dve.sem_inc(s, 16)
                nc.vector.memset(eps[:], LN_EPS).then_inc(eps_set, 1)
                dve.wait_ge(once, 32)
                with dve.Fori(0, B // 2) as it:
                    for k in range(2):
                        j = it * 2 + k
                        c0 = j * (2 * QT + 5)
                        dve.wait_ge(yT_done, j + 1)
                        for q in range(QT):
                            nc.vector.bn_stats(stats[:, k, q], yT_ps[:, k, q]).then_inc(chain, 1)
                        dve.wait_ge(chain, c0 + QT)
                        dve.wait_ge(x_loaded[k], it * 48 + 48)
                        nc.vector.tensor_tensor(x_in[:, k], x_in[:, k], beta[:].unsqueeze(1).broadcast_to([P, QT, P]), ALU.add)\
                            .then_inc(chain, 1)
                        for q in range(QT):
                            last = nc.vector.bn_aggr(mv[:, k, q], stats[:, k, q]).then_inc(chain, 1)
                        dve.wait_ge(chain, c0 + 2 * QT + 1)
                        dve.sem_inc(var_ready, 1)
                        dve.wait_ge(std_ready, j + 1)
                        nc.vector.reciprocal(rstd[:, k], rstd[:, k]).then_inc(chain, 1)
                        dve.wait_ge(chain, c0 + 2 * QT + 2)
                        for q in range(QT):
                            last = nc.vector.tensor_scalar(yn[:, k, q], yT_ps[:, k, q], mv[:, k, q, 0:1], rstd[:, k, q:q + 1],
                                                           ALU.subtract, ALU.mult)
                        last.then_inc(chain, 1)
                        dve.wait_ge(chain, c0 + 2 * QT + 3)
                        nc.vector.tensor_tensor(yn[:, k], yn[:, k], gamma[:].unsqueeze(1).broadcast_to([P, QT, P]), ALU.mult)\
                            .then_inc(chain, 1)
                        dve.wait_ge(chain, c0 + 2 * QT + 4)
                        nc.vector.tensor_tensor(yn[:, k], yn[:, k], x_in[:, k], ALU.add).then_inc(chain, 1)
                        dve.wait_ge(chain, c0 + 2 * QT + 5)
                        dve.wait_ge(experts_added, j + 1)
                        dve.wait_ge(stored[k], it * 16 + 16)
                        nc.vector.tensor_tensor(out_sb[:, k].rearrange("p t d -> p (t d)"), picked[:, k, 0],
                                                yn[:, k].rearrange("p t d -> p (t d)"), ALU.add).then_inc(block_done, 1)

            @block.gpsimd
            def _(pool):
                with pool.Fori(0, B // 2) as it:
                    for k in range(2):
                        pool.wait_ge(x_loaded[k], it * 48 + 48)
                        nc.gpsimd.tensor_tensor(picked[:, k, 0], picked[:, k, 0], picked[:, k, 1], ALU.add)\
                            .then_inc(experts_added, 1)



def route(nc, a, t):
    with ExitStack() as ctx:
        def sb(name, shape, dt=F32):
            return ctx.enter_context(nc.sbuf_tensor("rt_" + name, shape, dt))

        def sem(name):
            return ctx.enter_context(nc.semaphore("rt_" + name))

        gate_in, gate_sq = sb("gate_in", [P, P]), sb("gate_sq", [E, P])
        gate_s = sb("gate_s", [E, 4])
        gateT_h, gateT_l = sb("gateT_h", [P, P], F32R), sb("gateT_l", [P, P], F32R)
        lgT = sb("lgT", [E, B, N])
        lg = sb("lg", [P, TILES, E])
        lmax = sb("lmax", [P, TILES])
        cmp_a, cmp_b = sb("cmp_a", [P, TILES, E, E]), sb("cmp_b", [P, TILES, E, E])
        before = sb("before", [P, E, E])
        earlier = sb("earlier", [P, P], BF16)
        ones = sb("ones", [P, P], BF16)
        chosen = sb("chosen", [P, TILES, E])
        chosen_b = sb("chosen_b", [P, TILES, E], BF16)
        count = sb("count", [P, 2, E, TILES])
        steps128 = sb("steps128", [P, BLOCKS])
        steps_i = sb("steps_i", [P, BLOCKS], I32)
        over = sb("over", [P, BLOCKS, E])
        blocks = sb("blocks", [P, 3, E])
        row = sb("row", [P, TILES, E])
        pick = sb("pick", [P, TILES, E])
        sel = sb("sel", [P, 2, TILES])
        ids = sb("ids", [P, BLOCKS])
        g_ps = ctx.enter_context(nc.psum_tensor("rt_g_ps", [P, 2, 512], F32))
        c_ps = ctx.enter_context(nc.psum_tensor("rt_c_ps", [P, 2, 512], F32))
        r_ps = ctx.enter_context(nc.psum_tensor("rt_r_ps", [P, P], F32))
        cleared, once, made = sem("cleared"), sem("once"), sem("made")
        chain, sq_ready, std_ready, gate_ready = sem("chain"), sem("sq_ready"), sem("std_ready"), sem("gate_ready")
        gateT_done, lgT_done, lgT_ready, lg_done = sem("gateT_done"), sem("lgT_done"), sem("lgT_ready"), sem("lg_done")
        chosen_ready, counted = sem("chosen_ready"), sem("counted")

        with nc.Block() as block:
            @block.sync
            def _(sp):
                sp.wait_ge(cleared, 1)
                sp.dma_start(gate_in[0:E, :], a["gate_v"]).then_inc(once, 16)
                sp.dma_start(gate_s[:, 1:2], a["gate_g"].rearrange("(p o) -> p o", o=1)).then_inc(once, 16)
                sp.dma_start(gate_s[:, 2:3], a["gate_b"].rearrange("(p o) -> p o", o=1)).then_inc(once, 16)

            @block.gpsimd
            def _(pool):
                pool.memset(gate_in[:], 0.0).then_inc(cleared, 1)
                pool.memset(before[:], 1.0).then_inc(made, 1)
                pool.memset(earlier[:], 1.0).then_inc(made, 1)
                pool.memset(ones[:], 1.0).then_inc(made, 1)
                pool.wait_ge(made, 3)
                pool.affine_select(out=before[:], in_=before[:], compare_op=ALU.is_gt, fill=0.0, base=0,
                                   pattern=[[1, E], [-1, E]], channel_multiplier=0).then_inc(made, 1)
                pool.affine_select(out=earlier[:], in_=earlier[:], compare_op=ALU.is_gt, fill=0.0, base=0,
                                   pattern=[[1, P]], channel_multiplier=-1).then_inc(made, 1)
                pool.iota(steps_i[:], pattern=[[P, BLOCKS]], base=0, channel_multiplier=0).then_inc(made, 1)

            @block.scalar
            def _(act):
                act.wait_ge(sq_ready, 1)
                nc.scalar.activation(gate_s[:, 0:1], gate_s[:, 3:4], ACT.Sqrt).then_inc(std_ready, 1)
                for j in range(B):
                    act.wait_ge(lgT_done, j + 1)
                    nc.scalar.activation(lgT[:, j], g_ps[0:E, j % 2], ACT.Identity, bias=gate_s[:, 2:3]).then_inc(lgT_ready, 1)

            @block.tensor
            def _(pe):
                pe.wait_ge(gate_ready, 1)
                nc.tensor.transpose(r_ps[:], gate_in[:], t.ident[:]).then_inc(gateT_done, 1)
                pe.wait_ge(gate_ready, 2)
                for j in range(B):
                    xh, xl = (t.xs[:, (2 * j + i) * N:(2 * j + i + 1) * N] for i in range(2))
                    below(pe, lgT_ready, j - 1)
                    nc.tensor.matmul(g_ps[:, j % 2], gateT_h[:], xh, start=True, stop=False)
                    nc.tensor.matmul(g_ps[:, j % 2], gateT_h[:], xl, start=False, stop=False)
                    nc.tensor.matmul(g_ps[:, j % 2], gateT_l[:], xh, start=False, stop=True).then_inc(lgT_done, 1)
                pe.wait_ge(lgT_ready, B)
                for j in range(TILES):
                    last = nc.tensor.transpose(g_ps[:, 0, j * E:j * E + E], lgT[:, j // QT, j % QT * P:j % QT * P + P],
                                               t.ident[0:E, 0:E])
                last.then_inc(lg_done, 1)
                pe.wait_ge(chosen_ready, 1)
                flat = chosen_b[:].rearrange("p t e -> p (t e)")
                nc.tensor.matmul(c_ps[:, 0, 0:TILES * E], earlier[:], flat, start=True, stop=True)
                nc.tensor.matmul(c_ps[:, 1, 0:TILES * E], ones[:], flat, start=True, stop=True).then_inc(counted, 1)

            @block.vector
            def _(dve):
                n = [0]

                def link(ins):
                    n[0] += 1
                    ins.then_inc(chain, 1)
                    dve.wait_ge(chain, n[0])

                def tt(out, x, y, op):
                    link(nc.vector.tensor_tensor(out, x, y, op))

                dve.wait_ge(once, 16 * 3)
                tt(gate_sq[:], gate_in[0:E, :], gate_in[0:E, :], ALU.mult)
                nc.vector.reduce_sum(gate_s[:, 3:4], gate_sq[:], axis=AX.X).then_inc(sq_ready, 1)
                dve.wait_ge(std_ready, 1)
                link(nc.vector.tensor_scalar(gate_s[:, 0:1], gate_s[:, 0:1], WN_EPS, None, ALU.max))
                link(nc.vector.reciprocal(gate_s[:, 0:1], gate_s[:, 0:1]))
                nc.vector.tensor_scalar(gate_in[0:E, :], gate_in[0:E, :], gate_s[:, 0:1], gate_s[:, 1:2], ALU.mult, ALU.mult)\
                    .then_inc(gate_ready, 1)
                dve.wait_ge(gateT_done, 1)
                link(nc.vector.tensor_copy(gateT_h[:], r_ps[:]))
                nc.vector.tensor_tensor(gateT_l[:], r_ps[:], gateT_h[:], ALU.subtract).then_inc(gate_ready, 1)
                dve.wait_ge(made, 6)
                link(nc.vector.tensor_copy(steps128[:], steps_i[:]))
                dve.wait_ge(lg_done, 1)
                link(nc.vector.tensor_copy(lg[:], g_ps[:, 0, 0:TILES * E].rearrange("p (t e) -> p t e", e=E)))
                link(nc.vector.reduce_max(lmax[:], lg[:], axis=AX.X))
                by_expert = [P, TILES, E]
                tt(lg[:], lg[:], lmax[:].unsqueeze(2).broadcast_to(by_expert), ALU.subtract)
                link(nc.vector.tensor_scalar(lg[:], lg[:], -104.0, None, ALU.max))
                shape = [P, TILES, E, E]
                li, lj = lg[:].unsqueeze(3).broadcast_to(shape), lg[:].unsqueeze(2).broadcast_to(shape)
                tt(cmp_a[:], lj, li, ALU.is_equal)
                tt(cmp_a[:], cmp_a[:], before[:].unsqueeze(1).broadcast_to(shape), ALU.mult)
                tt(cmp_b[:], lj, li, ALU.is_gt)
                tt(cmp_a[:], cmp_a[:], cmp_b[:], ALU.add)
                link(nc.vector.reduce_sum(chosen[:], cmp_a[:], axis=AX.X))
                link(nc.vector.tensor_scalar(chosen[:], chosen[:], 2.0, None, ALU.is_lt))
                nc.vector.tensor_copy(chosen_b[:], chosen[:]).then_inc(chosen_ready, 1)
                dve.wait_ge(counted, 1)
                link(nc.vector.tensor_copy(count[:, 0], c_ps[:, 1, 0:TILES * E].rearrange("p (t e) -> p e t", e=E)))
                src, step = 0, 1
                while step < TILES:
                    dst = 1 - src
                    nc.vector.tensor_copy(count[:, dst, :, 0:step], count[:, src, :, 0:step])
                    tt(count[:, dst, :, step:TILES], count[:, src, :, step:TILES], count[:, src, :, 0:TILES - step], ALU.add)
                    src, step = dst, 2 * step
                taken = over[:].rearrange("p b e -> p (b e)")[:, 0:E * TILES].rearrange("p (e s) -> p e s", s=TILES)
                tt(taken, count[:, src, :, TILES - 1:TILES].broadcast_to([P, E, TILES]),
                   steps128[:, 0:TILES].unsqueeze(1).broadcast_to([P, E, TILES]), ALU.is_gt)
                link(nc.vector.reduce_sum(blocks[:, 0], taken, axis=AX.X))
                bsrc, step = 0, 1
                while step < E:
                    bdst = 1 if bsrc != 1 else 2
                    nc.vector.tensor_copy(blocks[:, bdst, 0:step], blocks[:, bsrc, 0:step])
                    tt(blocks[:, bdst, step:E], blocks[:, bsrc, step:E], blocks[:, bsrc, 0:E - step], ALU.add)
                    bsrc, step = bdst, 2 * step
                link(nc.vector.tensor_scalar(blocks[:, bsrc], blocks[:, bsrc], float(P), None, ALU.mult))
                tt(over[:], steps128[:].unsqueeze(2).broadcast_to([P, BLOCKS, E]),
                   blocks[:, bsrc].unsqueeze(1).broadcast_to([P, BLOCKS, E]), ALU.is_ge)
                link(nc.vector.reduce_sum(ids[:], over[:], axis=AX.X))
                link(nc.vector.tensor_scalar(ids[:], ids[:], float(E - 1), None, ALU.min))
                link(nc.vector.tensor_copy(t.block_expert[:], ids[:]))
                link(nc.vector.tensor_scalar(blocks[:, 0], blocks[:, 0], float(P), None, ALU.mult))
                tt(blocks[:, bsrc], blocks[:, bsrc], blocks[:, 0], ALU.subtract)
                tt(row[:], c_ps[:, 0, 0:TILES * E].rearrange("p (t e) -> p t e", e=E),
                   count[:, src].rearrange("p e t -> p t e"), ALU.add)
                tt(row[:], c_ps[:, 1, 0:TILES * E].rearrange("p (t e) -> p t e", e=E), row[:], ALU.subtract)
                tt(row[:], blocks[:, bsrc].unsqueeze(1).broadcast_to(by_expert), row[:], ALU.subtract)
                far = float(4 * BLOCKS * P)
                link(nc.vector.tensor_scalar(pick[:], chosen[:], -far, far, ALU.mult, ALU.add))
                tt(pick[:], row[:], pick[:], ALU.add)
                link(nc.vector.tensor_reduce(sel[:, 0], pick[:], axis=AX.X, op=ALU.min))
                tt(pick[:], row[:], chosen[:], ALU.mult)
                link(nc.vector.reduce_max(sel[:, 1], pick[:], axis=AX.X))
                link(nc.vector.tensor_copy(t.token_rows[:], sel[:]))


def prepare_experts(nc, a, t):
    R_G1, R_G2, ROWS = 0, E * HC, E * HC + E
    with ExitStack() as ctx:
        def sb(name, shape, dt=F32):
            return ctx.enter_context(nc.sbuf_tensor("wex_" + name, shape, dt))

        def sem(name):
            return ctx.enter_context(nc.semaphore("wex_" + name))

        rows = sb("rows", [P, P])
        cols = sb("cols", [P, ROWS])
        w_in = sb("w_in", [P, 2, 2 * HC, P])
        w_sq = sb("w_sq", [P, 2 * HC, P])
        ss = sb("ss", [P, HC + 1])
        nrm = sb("nrm", [P, HC + 1])
        wscale = sb("wscale", [P, HC + 1])
        wT_ps = ctx.enter_context(nc.psum_tensor("wex_wT_ps", [P, 2, 2, FH], F32))
        r_ps = ctx.enter_context(nc.psum_tensor("wex_r_ps", [P, P], F32))
        rows_zero, once, rowsT, sent = sem("rows_zero"), sem("once"), sem("rowsT"), sem("sent")
        w_loaded = [sem("w_loaded0"), sem("w_loaded1")]
        chain, sq_ready, std_ready, wn_ready = sem("chain"), sem("sq_ready"), sem("std_ready"), sem("wn_ready")
        wT_done, high, w_free = sem("wT_done"), sem("high"), sem("w_free")

        with nc.Block() as block:
            @block.sync
            def _(sp):
                sp.wait_ge(rows_zero, 1)
                sp.dma_start(rows[R_G1:R_G2, :], a["w1_g"].rearrange("e (c p) -> (e c) p", p=P)).then_inc(once, 16)
                sp.dma_start(rows[R_G2:ROWS, :], a["w2_g"]).then_inc(once, 16)
                sp.dma_start(t.b1[:], a["b1"].rearrange("(o e) n -> o (e n)", o=1).broadcast_to([P, E * FH])).then_inc(once, 16)
                sp.dma_start(t.b2[:], a["b2"].rearrange("(o e) n -> o (e n)", o=1).broadcast_to([P, E * D])).then_inc(once, 16)
                with sp.Fori(0, E // 2) as it:
                    for k in range(2):
                        e = it * 2 + k
                        sp.wait_ge(wT_done, e * 2 + 2)
                        sp.dma_start(w_in[:, k, 0:HC], a["w1_v"].rearrange("e (c p) d -> e p c d", p=P)[bass.ds(e, 1)]
                                     .rearrange("o p c d -> p (o c) d")).then_inc(w_loaded[k], 16)
                        sp.dma_start(w_in[:, k, HC:2 * HC], a["w2_v"].rearrange("e p (c n) -> e p c n", n=P)[bass.ds(e, 1)]
                                     .rearrange("o p c n -> p (o c) n")).then_inc(w_loaded[k], 16)

            @block.gpsimd
            def _(pool):
                pool.memset(rows[:], 0.0).then_inc(rows_zero, 1)
                for i in range(TILES):
                    for which in range(2):
                        pool.indirect_dma_start(
                            t.x_rows, bass.IndirectOffsetOnAxis(ap=t.token_rows[:, which, i:i + 1], axis=0),
                            t.xn_rows[:, i * P:i * P + P], None).then_inc(sent, 16)
                pool.wait_ge(sent, 2 * TILES * 16)

            @block.vector
            def _(dve):
                dve.wait_ge(rowsT, 1)
                nc.vector.tensor_copy(cols[:], r_ps[:, 0:ROWS]).then_inc(chain, 1)
                dve.wait_ge(chain, 1)
                steps = 5
                with dve.Fori(0, E // 2) as it:
                    for k in range(2):
                        e = it * 2 + k
                        c0 = e * steps + 1
                        dve.wait_ge(w_loaded[k], it * 32 + 32)
                        nc.vector.tensor_tensor(w_sq[:], w_in[:, k], w_in[:, k], ALU.mult).then_inc(chain, 1)
                        dve.wait_ge(chain, c0 + 1)
                        nc.vector.reduce_sum(ss[:, 0:HC], w_sq[:, 0:HC], axis=AX.X)
                        nc.vector.reduce_sum(ss[:, HC:HC + 1], w_sq[:, HC:2 * HC], axis=AX.XY).then_inc(sq_ready, 1)
                        dve.wait_ge(std_ready, e + 1)
                        nc.vector.tensor_scalar(nrm[:], nrm[:], WN_EPS, None, ALU.max).then_inc(chain, 1)
                        dve.wait_ge(chain, c0 + 2)
                        nc.vector.reciprocal(nrm[:], nrm[:]).then_inc(chain, 1)
                        dve.wait_ge(chain, c0 + 3)
                        nc.vector.tensor_tensor(wscale[:, 0:HC], cols[:, bass.ds(e * HC + R_G1, HC)], nrm[:, 0:HC], ALU.mult)\
                            .then_inc(chain, 1)
                        nc.vector.tensor_tensor(wscale[:, HC:HC + 1], cols[:, bass.ds(e + R_G2, 1)], nrm[:, HC:HC + 1],
                                                ALU.mult).then_inc(chain, 1)
                        dve.wait_ge(chain, c0 + 5)
                        nc.vector.tensor_tensor(w_in[:, k, 0:HC], w_in[:, k, 0:HC],
                                                wscale[:, 0:HC].unsqueeze(2).broadcast_to([P, HC, P]), ALU.mult)
                        nc.vector.tensor_scalar(w_in[:, k, HC:2 * HC], w_in[:, k, HC:2 * HC], wscale[:, HC:HC + 1], None, ALU.mult)\
                            .then_inc(wn_ready, 1)
                        dve.wait_ge(high, e * 2 + 2)
                        w0 = e * 2 * FH
                        nc.vector.tensor_tensor(t.w1[:, bass.ds(w0 + FH, FH)], wT_ps[:, k, 0], t.w1[:, bass.ds(w0, FH)], ALU.subtract)
                        w2 = t.w2[:, bass.ds(w0, 2 * FH)].rearrange("p (c h d) -> p c h d", h=2, d=D)
                        nc.vector.tensor_tensor(w2[:, :, 1], wT_ps[:, k, 1].rearrange("p (c d) -> p c d", d=D), w2[:, :, 0],
                                                ALU.subtract).then_inc(w_free, 1)

            @block.tensor
            def _(pe):
                pe.wait_ge(once, 16 * 4)
                nc.tensor.transpose(r_ps[:], rows[:], t.ident[:]).then_inc(rowsT, 1)
                pe.sem_inc(wT_done, 2 * 2)
                with pe.Fori(0, E // 2) as it:
                    for k in range(2):
                        e = it * 2 + k
                        pe.wait_ge(wn_ready, e + 1)
                        pe.wait_ge(w_free, e + 1)
                        for half in range(2):
                            for c in range(HC):
                                last = nc.tensor.transpose(wT_ps[:, k, half, c * P:c * P + P], w_in[:, k, half * HC + c], t.ident[:])
                            last.then_inc(wT_done, 1)

            @block.scalar
            def _(act):
                act.sem_inc(w_free, 2)
                with act.Fori(0, E // 2) as it:
                    for k in range(2):
                        e = it * 2 + k
                        act.wait_ge(sq_ready, e + 1)
                        nc.scalar.activation(nrm[:], ss[:], ACT.Sqrt).then_inc(std_ready, 1)
                        act.wait_ge(wT_done, e * 2 + 6)
                        w0 = e * 2 * FH
                        nc.scalar.activation(t.w1[:, bass.ds(w0, FH)], wT_ps[:, k, 0], ACT.Copy).then_inc(high, 1)
                        w2 = t.w2[:, bass.ds(w0, 2 * FH)].rearrange("p (c h d) -> p c h d", h=2, d=D)
                        nc.scalar.activation(w2[:, :, 0], wT_ps[:, k, 1].rearrange("p (c d) -> p c d", d=D), ACT.Copy)\
                            .then_inc(high, 1)


def experts(nc, t):
    with ExitStack() as ctx:
        def sb(name, shape, dt=F32):
            return ctx.enter_context(nc.sbuf_tensor("exp_" + name, shape, dt))

        def psum(name, shape):
            return ctx.enter_context(nc.psum_tensor("exp_" + name, shape, F32))

        def sem(name):
            return ctx.enter_context(nc.semaphore("exp_" + name))

        x_blk = sb("x_blk", [P, 4, D])
        xT_h, xT_l = sb("xT_h", [P, 2, P], F32R), sb("xT_l", [P, 2, P], F32R)
        hid = sb("hid", [P, 2, FH])
        hT_h, hT_l = sb("hT_h", [P, 2, HC, P], F32R), sb("hT_l", [P, 2, HC, P], F32R)
        part, y_blk = sb("part", [P, D]), sb("y_blk", [P, 4, D])
        x_ps, h_ps, t_ps, y_ps = psum("x_ps", [P, 2, 512]), psum("h_ps", [P, 2, FH]), psum("t_ps", [P, 2, FH]), psum("y_ps", [P, 2, 512])
        loaded, stored = [sem("loaded0"), sem("loaded1")], [sem("stored0"), sem("stored1")]
        xT_done, x_high, x_low = sem("xT_done"), sem("x_high"), sem("x_low")
        h_done, biased, silu_done = sem("h_done"), sem("biased"), sem("silu_done")
        hT_done, h_high, h_low = sem("hT_done"), sem("h_high"), sem("h_low")
        y_done, half_done, y_ready = sem("y_done"), sem("half_done"), sem("y_ready")

        def ok(it, k):
            return not isinstance(it, int) or 0 <= 4 * it + k < BLOCKS

        def expert_of(eng, it, k):
            b = it * 4 + k
            at = t.block_expert[0:1, b:b + 1] if isinstance(b, int) else t.block_expert[0:1, bass.ds(b, 1)]
            return eng.value_load(at, min_val=0, max_val=E - 1)

        def pe_step(pe, it, k):
            b = it * 4 + k
            if ok(it, k + 2):
                s = k % 2
                if k % 2 == 0:
                    pair = (k + 2) // 2
                    pe.wait_ge(loaded[pair % 2], (it + pair // 2) * 16 + 16)
                below(pe, x_low, b + 1)
                nc.tensor.transpose(x_ps[:, s, 0:P], x_blk[:, (k + 2) % 4], t.ident[:]).then_inc(xT_done, 1)
            if ok(it, k + 1):
                s = (k + 1) % 2
                w0 = expert_of(pe, it, k + 1) * (2 * FH)
                wh, wl = t.w1[:, bass.ds(w0, FH)], t.w1[:, bass.ds(w0 + FH, FH)]
                pe.wait_ge(x_low, b + 2)
                below(pe, biased, b)
                nc.tensor.matmul(h_ps[:, s], xT_h[:, s], wh, start=True, stop=False)
                nc.tensor.matmul(h_ps[:, s], xT_h[:, s], wl, start=False, stop=False)
                nc.tensor.matmul(h_ps[:, s], xT_l[:, s], wh, start=False, stop=True).then_inc(h_done, 1)
            if ok(it, k):
                s = k % 2
                pe.wait_ge(silu_done, b + 1)
                below(pe, h_low, b - 1)
                for c in range(HC):
                    last = nc.tensor.transpose(t_ps[:, s, c * P:c * P + P], hid[:, s, c * P:c * P + P], t.ident[:])
                last.then_inc(hT_done, 1)
            if ok(it, k - 1):
                s = (k - 1) % 2
                w0 = expert_of(pe, it, k - 1) * (2 * FH)
                pe.wait_ge(h_low, b)
                below(pe, y_ready, b - 2)
                for p_, hT in enumerate((hT_h, hT_l)):
                    for c in range(HC):
                        last = nc.tensor.matmul(y_ps[:, s, 0:2 * D], hT[:, s, c], t.w2[:, bass.ds(w0 + c * 2 * D, 2 * D)],
                                                start=p_ + c == 0, stop=p_ + c == HC)
                last.then_inc(y_done, 1)

        def act_step(act, it, k):
            b = it * 4 + k
            if ok(it, k + 2):
                s = k % 2
                act.wait_ge(xT_done, b + 3)
                below(act, h_done, b + 1)
                nc.scalar.activation(xT_h[:, s], x_ps[:, s, 0:P], ACT.Copy).then_inc(x_high, 1)
            if ok(it, k + 1):
                s = (k + 1) % 2
                act.wait_ge(biased, b + 2)
                nc.scalar.activation(hid[:, s], hid[:, s], ACT.Silu).then_inc(silu_done, 1)
            if ok(it, k):
                s = k % 2
                act.wait_ge(hT_done, b + 1)
                below(act, y_done, b - 1)
                nc.scalar.activation(hT_h[:, s], t_ps[:, s].rearrange("p (c n) -> p c n", c=HC), ACT.Copy).then_inc(h_high, 1)
            if k % 2 == 1 and ok(it, k - 2):
                pair = (k - 3) // 2
                act.wait_ge(y_ready, b - 1)
                act.dma_start(rows_of(t.y_rows, it * 2 + pair), y_blk[:, pair % 2 * 2:pair % 2 * 2 + 2])\
                    .then_inc(stored[pair % 2], 16)

        def dve_step(dve, it, k):
            b = it * 4 + k
            if ok(it, k + 2):
                s = k % 2
                dve.wait_ge(x_high, b + 3)
                nc.vector.tensor_tensor(xT_l[:, s], x_ps[:, s, 0:P], xT_h[:, s], ALU.subtract).then_inc(x_low, 1)
            if ok(it, k + 1):
                s = (k + 1) % 2
                e = expert_of(dve, it, k + 1)
                dve.wait_ge(h_done, b + 2)
                below(dve, hT_done, b)
                nc.vector.tensor_tensor(hid[:, s], h_ps[:, s], t.b1[:, bass.ds(e * FH, FH)], ALU.add).then_inc(biased, 1)
            if ok(it, k - 1):
                s = (k - 1) % 2
                e = expert_of(dve, it, k - 1)
                dve.wait_ge(y_done, b)
                below(dve, y_ready, b - 1)
                nc.vector.tensor_tensor(part[:], y_ps[:, s, D:2 * D], t.b2[:, bass.ds(e * D, D)], ALU.add).then_inc(half_done, 1)
            if ok(it, k):
                s = k % 2
                dve.wait_ge(h_high, b + 1)
                nc.vector.tensor_tensor(hT_l[:, s], t_ps[:, s].rearrange("p (c n) -> p c n", c=HC), hT_h[:, s], ALU.subtract)\
                    .then_inc(h_low, 1)
            if ok(it, k - 1):
                s = (k - 1) % 2
                dve.wait_ge(half_done, b)
                if k % 2 == 1:
                    pair = (k - 1) // 2
                    below(dve, stored[pair % 2], (it + pair // 2) * 16)
                nc.vector.tensor_tensor(y_blk[:, (k - 1) % 4], y_ps[:, s, 0:D], part[:], ALU.add).then_inc(y_ready, 1)

        def rows_of(rows, pair):
            r0 = pair * 2 * P
            part = rows[r0:r0 + 2 * P, :] if isinstance(r0, int) else rows[bass.ds(r0, 2 * P), :]
            return part.rearrange("(c p) d -> p c d", p=P)

        def load(sp, it, k):
            pair = it * 2 + k
            below(sp, xT_done, pair * 2 - 2)
            sp.dma_start(x_blk[:, k % 2 * 2:k % 2 * 2 + 2], rows_of(t.x_rows, pair)).then_inc(loaded[k % 2], 16)

        def program(eng, step):
            for k in range(-2, 4):
                step(eng, 0, k)
            with eng.Fori(1, BLOCKS // 4 - 1) as it:
                for k in range(4):
                    step(eng, it, k)
            for k in range(4 + 2):
                step(eng, BLOCKS // 4 - 1, k)

        with nc.Block() as block:
            @block.sync
            def _(sp):
                for k in range(2):
                    load(sp, 0, k)
                with sp.Fori(1, BLOCKS // 4) as it:
                    for k in range(2):
                        load(sp, it, k)
                for s in stored:
                    sp.wait_ge(s, BLOCKS // 4 * 16)

            @block.tensor
            def _(pe):
                program(pe, pe_step)

            @block.scalar
            def _(act):
                program(act, act_step)

            @block.vector
            def _(dve):
                program(dve, dve_step)


def build(nc, a, out):
    class Shared:
        pass

    t = Shared()
    t.x_rows = nc.dram_tensor("x_rows", [BLOCKS * P, D], F32).ap()
    t.y_rows = nc.dram_tensor("y_rows", [BLOCKS * P, D], F32).ap()
    t.picked = nc.dram_tensor("picked", [2, B * N, D], F32).ap()
    with ExitStack() as ctx:
        def sb(name, shape, dt=F32):
            return ctx.enter_context(nc.sbuf_tensor(name, shape, dt))

        t.xs = sb("xs", [P, B * 2 * N], F32R)
        t.yacc = sb("yacc", [P, B * N])
        t.token_rows = sb("token_rows", [P, 2, TILES], I32)
        t.ident = make_identity(nc, ctx, "ident")
        with ExitStack() as inner:
            def sbi(name, shape, dt=F32):
                return inner.enter_context(nc.sbuf_tensor(name, shape, dt))

            t.wall = sbi("wall", [P, NPAIR * WCOLS], F32R)
            t.wo_all = sbi("wo_all", [P, NPAIR * 2 * P])
            t.bias_all = sbi("bias_all", [P, NPAIR, 3])
            with ExitStack() as deeper:
                def sbd(name, shape, dt=F32):
                    return deeper.enter_context(nc.sbuf_tensor(name, shape, dt))

                t.block_expert = sbd("block_expert", [P, BLOCKS], I32)
                t.xn_rows = sbd("xn_rows", [P, TILES * D])
                prepare_attention(nc, a, t)
                route(nc, a, t)
                t.w1 = sbd("w1", [P, E * 2 * FH], F32R)
                t.w2 = sbd("w2", [P, E * 2 * FH], F32R)
                t.b1, t.b2 = sbd("b1_all", [P, E * FH]), sbd("b2_all", [P, E * D])
                prepare_experts(nc, a, t)
                experts(nc, t)
            attention(nc, t)
        finish(nc, a, t, out)


_ATTN = ["x", "adaptive_scale", "Wq", "bq", "Wk", "bk", "Wv", "bv", "Wo", "bo", "gamma", "beta"]
_FFN = ["gate_v", "gate_g", "gate_b", "w1_v", "w1_g", "b1", "w2_v", "w2_g", "b2"]


def kernel(**inputs):
    import numpy as _np
    import concourse.bacc as _bacc
    from concourse import mybir as _mybir
    from concourse.bass_utils import run_bass_kernel_spmd as _run

    nc = _bacc.Bacc("TRN2", target_bir_lowering=False, num_devices=1)
    arrays, args = {}, {}
    for prefix, names in (("L0_attn_", _ATTN), ("L0_ffn_", _FFN)):
        for name in names:
            v = _np.ascontiguousarray(inputs[prefix + name])
            arrays[f"in_{name}"] = v
            args[name] = nc.dram_tensor(f"in_{name}", v.shape, _mybir.dt.from_np(v.dtype), kind="ExternalInput").ap()
    out = nc.dram_tensor("out_0", (B, N, D), F32, kind="ExternalOutput").ap()
    build(nc, args, out)
    r = _run(nc, [arrays], core_ids=[0])
    return r.results[0]["out_0"]
```

```python
from contextlib import ExitStack

import concourse.bass as bass
from concourse import mybir

F32 = mybir.dt.float32
F32R = mybir.dt.float32r
BF16 = mybir.dt.bfloat16
I32 = mybir.dt.int32
ALU = mybir.AluOpType
ACT = mybir.ActivationFunctionType
AX = mybir.AxisListType

P = 128
B, N, D = 8, 512, 128
H, HD = 16, 64
E, FH = 8, 512
QT = N // P
NPAIR = H // 2
PAIRS = B * NPAIR
UNITS = PAIRS * 2 * QT
HC = FH // P
SCALE = float(HD) ** -0.5
TILES = B * QT
BLOCKS = (2 * B * N + E * (P - 1)) // P
BLOCKS += -BLOCKS % 4
LOW_ROW = 32
LN_EPS = 1e-5
WN_EPS = 1e-12
QH, QL, KH, KL, QK_COLS = 0, P, 2 * P, 3 * P, 4 * P
VH, VL, TWO_COLS = 2 * QK_COLS, 2 * QK_COLS + 2 * P, 2 * QK_COLS + 4 * P


def below(eng, sem, value):
    if not isinstance(value, int) or value > 0:
        eng.wait_ge(sem, value)


def make_identity(nc, ctx, name):
    ident = ctx.enter_context(nc.sbuf_tensor(name, [P, P], F32))
    cleared = ctx.enter_context(nc.semaphore(name + "_cleared"))
    with nc.Block() as block:
        @block.gpsimd
        def _(pool):
            pool.memset(ident[:], 0.0).then_inc(cleared, 1)
            pool.wait_ge(cleared, 1)
            pool.affine_select(out=ident[:], in_=ident[:], compare_op=ALU.not_equal, fill=1.0,
                               base=0, pattern=[[-1, P]], channel_multiplier=1)
    return ident


def normalise(nc, a, t):
    with ExitStack() as ctx:
        def sb(name, shape, dt=F32):
            return ctx.enter_context(nc.sbuf_tensor("nrm_" + name, shape, dt))

        def sem(name):
            return ctx.enter_context(nc.semaphore("nrm_" + name))

        CHUNKS = B // 2
        CT = TILES // CHUNKS
        zeros = sb("zeros", [P, BLOCKS // 8 * P])
        stats, mv, rstd = sb("stats", [P, TILES, 6]), sb("mv", [P, TILES, 2]), sb("rstd", [P, TILES])
        eps = sb("eps", [P, 1])
        gate_in, gate_sq = sb("gate_in", [P, P]), sb("gate_sq", [E, P])
        gate_s = sb("gate_s", [E, 4])
        gateT_h, gateT_l = sb("gateT_h", [P, P], F32R), sb("gateT_l", [P, P], F32R)
        lgT = sb("lgT", [E, B, N])
        xT_ps = ctx.enter_context(nc.psum_tensor("nrm_xT_ps", [P, 4, N], F32))
        g_ps = ctx.enter_context(nc.psum_tensor("nrm_g_ps", [P, 2, N], F32))
        l_ps = ctx.enter_context(nc.psum_tensor("nrm_l_ps", [P, TILES, E], F32))
        r_ps = ctx.enter_context(nc.psum_tensor("nrm_r_ps", [P, P], F32))
        x_loaded = [sem(f"x_loaded{c}") for c in range(CHUNKS)]
        cleared, gate_loaded, zeroed, eps_set = sem("cleared"), sem("gate_loaded"), sem("zeroed"), sem("eps_set")
        chain, gate_squared, gate_norm, gate_ready, gateT_done = (
            sem(n) for n in ("chain", "gate_squared", "gate_norm", "gate_ready", "gateT_done"))
        var_ready, std_ready, xn_ready, xT_done = sem("var_ready"), sem("std_ready"), sem("xn_ready"), sem("xT_done")
        x_high, x_low = sem("x_high"), sem("x_low")
        lgT_done, lgT_ready, lg_done = sem("lgT_done"), sem("lgT_ready"), sem("lg_done")

        def tile(i):
            return t.xn_rows[:, i * D:i * D + D]

        with nc.Block() as block:
            @block.sync
            def _(sp):
                x_v = a["x"].rearrange("b n d -> (b n) d").rearrange("(c i p) d -> c p i d", p=P, i=CT)
                for c in range(CHUNKS):
                    sp.dma_start(t.xn_rows[:, c * CT * D:(c + 1) * CT * D].rearrange("p (i d) -> p i d", d=D), x_v[c])\
                        .then_inc(x_loaded[c], 16)
                    if c == 0:
                        sp.wait_ge(cleared, 1)
                        sp.dma_start(gate_in[0:E, :], a["gate_v"]).then_inc(gate_loaded, 16)
                        sp.dma_start(gate_s[:, 1:2], a["gate_g"].rearrange("(p o) -> p o", o=1)).then_inc(gate_loaded, 16)
                        sp.dma_start(gate_s[:, 2:3], a["gate_b"].rearrange("(p o) -> p o", o=1)).then_inc(gate_loaded, 16)
                sp.wait_ge(cleared, 2)
                for part in range(8):
                    sp.dma_start(t.x_rows.rearrange("(g p r) d -> g p (r d)", g=8, p=P)[part], zeros[:]).then_inc(zeroed, 16)
                sp.wait_ge(zeroed, 8 * 16)

            @block.gpsimd
            def _(pool):
                pool.memset(gate_in[:], 0.0).then_inc(cleared, 1)
                pool.memset(zeros[:], 0.0).then_inc(cleared, 1)
                with pool.Fori(0, B) as j:
                    pool.wait_ge(x_low, j + 1)
                    high, low = (t.xs[:, bass.ds(j * (2 * N) + i * N, N)] for i in range(2))
                    nc.gpsimd.tensor_tensor(t.yacc[:, bass.ds(j * N, N)], high, low, ALU.add)

            @block.tensor
            def _(pe):
                def transposes(c):
                    pe.wait_ge(xn_ready, c + 1)
                    for j in (2 * c, 2 * c + 1):
                        below(pe, x_low, j - 3)
                        for q in range(QT):
                            last = nc.tensor.transpose(xT_ps[:, j % 4, q * P:q * P + P], tile(j * QT + q), t.ident[:])
                        last.then_inc(xT_done, 1)

                def logits(c):
                    for j in (2 * c, 2 * c + 1):
                        xh, xl = (t.xs[:, (2 * j + i) * N:(2 * j + i + 1) * N] for i in range(2))
                        pe.wait_ge(x_low, j + 1)
                        below(pe, lgT_ready, j - 1)
                        nc.tensor.matmul(g_ps[:, j % 2], gateT_h[:], xh, start=True, stop=False)
                        nc.tensor.matmul(g_ps[:, j % 2], gateT_h[:], xl, start=False, stop=False)
                        nc.tensor.matmul(g_ps[:, j % 2], gateT_l[:], xh, start=False, stop=True).then_inc(lgT_done, 1)
                    for j in (2 * c, 2 * c + 1):
                        pe.wait_ge(lgT_ready, j + 1)
                        for q in range(QT):
                            last = nc.tensor.transpose(l_ps[:, j * QT + q, :], lgT[:, j, q * P:q * P + P], t.ident[0:E, 0:E])
                        last.then_inc(lg_done, 1)

                pe.wait_ge(gate_ready, 1)
                nc.tensor.transpose(r_ps[:], gate_in[:], t.ident[:]).then_inc(gateT_done, 1)
                transposes(0)
                pe.wait_ge(gate_ready, 2)
                for c in range(1, CHUNKS):
                    transposes(c)
                    logits(c - 1)
                logits(CHUNKS - 1)

            @block.scalar
            def _(act):
                def root(c):
                    act.wait_ge(var_ready, c + 1)
                    nc.scalar.activation(rstd[:, c * CT:(c + 1) * CT], mv[:, c * CT:(c + 1) * CT, 1], ACT.Sqrt, bias=eps[:])\
                        .then_inc(std_ready, 1)

                def high_parts(c):
                    for j in (2 * c, 2 * c + 1):
                        act.wait_ge(xT_done, j + 1)
                        nc.scalar.activation(t.xs[:, 2 * j * N:(2 * j + 1) * N], xT_ps[:, j % 4], ACT.Copy).then_inc(x_high, 1)

                def add_gate_bias(c):
                    for j in (2 * c, 2 * c + 1):
                        act.wait_ge(lgT_done, j + 1)
                        nc.scalar.activation(lgT[:, j], g_ps[0:E, j % 2], ACT.Identity, bias=gate_s[:, 2:3]).then_inc(lgT_ready, 1)

                act.wait_ge(gate_squared, 1)
                nc.scalar.activation(gate_s[:, 0:1], gate_s[:, 3:4], ACT.Sqrt).then_inc(gate_norm, 1)
                act.wait_ge(eps_set, 1)
                root(0)
                root(1)
                for c in range(CHUNKS):
                    high_parts(c)
                    if c + 2 < CHUNKS:
                        root(c + 2)
                    if c > 0:
                        add_gate_bias(c - 1)
                add_gate_bias(CHUNKS - 1)

            @block.vector
            def _(dve):
                n = [0]

                def link(ins):
                    n[0] += 1
                    ins.then_inc(chain, 1)

                def linked():
                    dve.wait_ge(chain, n[0])

                def statistics(c):
                    dve.wait_ge(x_loaded[c], 16)
                    for i in range(c * CT, (c + 1) * CT):
                        link(nc.vector.bn_stats(stats[:, i], tile(i)))
                    linked()
                    for i in range(c * CT, (c + 1) * CT):
                        last = nc.vector.bn_aggr(mv[:, i], stats[:, i])
                    last.then_inc(var_ready, 1)

                def norm(c):
                    dve.wait_ge(std_ready, c + 1)
                    dve.wait_ge(var_ready, c + 1)
                    link(nc.vector.reciprocal(rstd[:, c * CT:(c + 1) * CT], rstd[:, c * CT:(c + 1) * CT]))
                    linked()
                    for i in range(c * CT, (c + 1) * CT):
                        last = nc.vector.tensor_scalar(tile(i), tile(i), mv[:, i, 0:1], rstd[:, i:i + 1], ALU.subtract, ALU.mult)
                    last.then_inc(xn_ready, 1)

                def low_parts(c):
                    for j in (2 * c, 2 * c + 1):
                        dve.wait_ge(x_high, j + 1)
                        nc.vector.tensor_tensor(t.xs[:, (2 * j + 1) * N:(2 * j + 2) * N], xT_ps[:, j % 4],
                                                t.xs[:, 2 * j * N:(2 * j + 1) * N], ALU.subtract).then_inc(x_low, 1)

                nc.vector.memset(eps[:], LN_EPS).then_inc(eps_set, 1)
                dve.wait_ge(gate_loaded, 16 * 3)
                link(nc.vector.tensor_tensor(gate_sq[:], gate_in[0:E, :], gate_in[0:E, :], ALU.mult))
                linked()
                nc.vector.reduce_sum(gate_s[:, 3:4], gate_sq[:], axis=AX.X).then_inc(gate_squared, 1)
                statistics(0)
                dve.wait_ge(gate_norm, 1)
                link(nc.vector.tensor_scalar(gate_s[:, 0:1], gate_s[:, 0:1], WN_EPS, None, ALU.max))
                linked()
                link(nc.vector.reciprocal(gate_s[:, 0:1], gate_s[:, 0:1]))
                linked()
                nc.vector.tensor_scalar(gate_in[0:E, :], gate_in[0:E, :], gate_s[:, 0:1], gate_s[:, 1:2], ALU.mult, ALU.mult)\
                    .then_inc(gate_ready, 1)
                statistics(1)
                dve.wait_ge(gateT_done, 1)
                link(nc.vector.tensor_copy(gateT_h[:], r_ps[:]))
                linked()
                nc.vector.tensor_tensor(gateT_l[:], r_ps[:], gateT_h[:], ALU.subtract).then_inc(gate_ready, 1)
                norm(0)
                statistics(2)
                norm(1)
                low_parts(0)
                statistics(3)
                for c in range(2, CHUNKS):
                    norm(c)
                    low_parts(c - 1)
                low_parts(CHUNKS - 1)
                dve.wait_ge(lg_done, B)
                nc.vector.tensor_copy(t.logits[:], l_ps[:])


def attention(nc, t):
    with ExitStack() as ctx:
        def sb(name, shape, dt=F32):
            return ctx.enter_context(nc.sbuf_tensor(name, shape, dt))

        def psum(name, shape):
            return ctx.enter_context(nc.psum_tensor(name, shape, F32))

        def sem(name):
            return ctx.enter_context(nc.semaphore(name))

        w_st = sb("w_st", [P, 2, QK_COLS], F32R)
        wo_st = sb("wo_st", [P, 2, 2 * P])
        row_st = sb("row_st", [P, 2, 1], I32)
        picked = sb("picked_sb", [P, 2, D])
        xv_st = sb("xv_st", [P, 2 * N], F32R)
        wv_st = sb("wv_st", [P, 4 * P], F32R)
        q_pair = sb("q_pair", [P, 2, N], F32R)
        k_pair = sb("k_pair", [P, 2, N], F32R)
        q_sb = sb("q_sb", [P, 4, N], F32R)
        k_sb = sb("k_sb", [P, 4, 2, N], F32R)
        v_sb = sb("v_sb", [P, 8, QT, P], F32R)
        probs = sb("probs", [P, 4, N])
        pth = sb("pth", [P, 2, QT, N], F32R)
        ptl = sb("ptl", [P, 2, QT, N], F32R)
        o_sb = sb("o_sb", [P, 2, N])
        nmax = sb("nmax", [P, 8])
        rsum = sb("rsum", [P, 8])
        rinv = sb("rinv", [P, 8])
        s_ps = psum("s_ps", [P, 2, N])
        t_ps = psum("t_ps", [P, 2, N])
        o_ps = psum("o_ps", [P, 2, N])
        qo_ps = psum("qo_ps", [P, N])
        kv_ps = psum("kv_ps", [P, N])

        st_loaded = [sem("st_loaded0"), sem("st_loaded1")]
        v_loaded = sem("v_loaded")
        wo_loaded = [sem("wo_loaded0"), sem("wo_loaded1")]
        rows_loaded, picked_up = ([sem(f"{n}{i}") for i in range(2)] for n in ("rows_loaded", "picked_up"))
        rows_added = sem("rows_added")
        s_done, t_done, pv_done = sem("s_done"), sem("t_done"), sem("pv_done")
        q_mm, k_mm, v_mm, wo_mm = sem("q_mm"), sem("k_mm"), sem("v_mm"), sem("wo_mm")
        q_high, k_high, v_high = sem("q_high"), sem("k_high"), sem("v_high")
        moved = [sem("moved0"), sem("moved1")]
        q_low, k_low, v_low, y_added = sem("q_low"), sem("k_low"), sem("v_low"), sem("y_added")
        max_done, exp_done, inv_done, norm_done = sem("max_done"), sem("exp_done"), sem("inv_done"), sem("norm_done")
        ph_done, pl_done, o_done = sem("ph_done"), sem("pl_done"), sem("o_done")

        def valid(it, unit):
            return not isinstance(it, int) or 0 <= 32 * it + unit < UNITS

        def pair_ok(it, pair):
            return not isinstance(it, int) or 0 <= 4 * it + pair < PAIRS

        PE_TASKS = {1: ("wo", 0, -1), 3: ("v", 0, 1), 4: ("wo", 1, -1), 6: ("q", 0, 2), 7: ("k", 0, 2)}
        ACT_TASKS = {0: ("k", 0, 1), 5: ("v", 0, 1), 7: ("q", 0, 2)}
        DVE_TASKS = {0: ("q", 0, 1), 1: ("k", 0, 1), 5: ("wo", 0, -1), 6: ("v", 0, 1)}

        def task(it, l, tasks):
            found = tasks.get(l % 8)
            if not found:
                return None
            kind, head, ahead = found
            pair = l // 8 + ahead
            if not pair_ok(it, pair + 1 if kind == "v" else pair):
                return None
            return kind, head, pair, it * 4 + pair

        def wait_moved(eng, it, pr):
            if pair_ok(it, pr):
                eng.wait_ge(moved[pr % 2], (it * 2 + pr // 2 + 1) * (8 * 16))

        def bias(pi, which):
            return t.bias_all[:, bass.ds(pi % NPAIR * 2 + which, 1)]

        def value_half(pr):
            half, first = (pr + 1) % 2, (pr + 1) // 2 % 2 * 4
            dst = v_sb[:, first:first + 4, half * 2:half * 2 + 2].rearrange("p g c n -> p c g n")
            return dst[:, :, :, 0:HD], dst[:, :, :, HD:P], kv_ps[:].rearrange("p (c g n) -> p c g n", c=2, g=4)

        def pe_slot(pe, it, l):
            u = it * 32 + l
            if valid(it, l + 3):
                g, qt, bank = (l + 3) // 4, (l + 3) % 4, (l + 3) % 2
                if qt == 0 and g % 2 == 0:
                    wait_moved(pe, it, g // 2)
                below(pe, exp_done, u + 2)
                lhs = q_sb[:, g % 4, qt * P:qt * P + P]
                nc.tensor.matmul(s_ps[:, bank], lhs, k_sb[:, g % 4, 0], start=True, stop=False)
                nc.tensor.matmul(s_ps[:, bank], lhs, k_sb[:, g % 4, 1], start=False, stop=True).then_inc(s_done, 1)
            if valid(it, l):
                below(pe, norm_done, u + 1)
                below(pe, pl_done, u - 1)
                for kc in range(QT):
                    last = nc.tensor.transpose(t_ps[:, l % 2, kc * P:kc * P + P], probs[:, l % 4, kc * P:kc * P + P],
                                               t.ident[:])
                last.then_inc(t_done, 1)
            if valid(it, l - 4):
                g, kc = l // 4 - 1, l % 4
                if kc == 0:
                    pe.wait_ge(pl_done, it * 32 + 4 * g + 4)
                    below(pe, o_done, it * 8 + g - 1)
                    if g % 4 == 0:
                        pe.wait_ge(v_low, it * 4 + g // 2 + 2)
                for part, pt in enumerate((pth, ptl)):
                    last = nc.tensor.matmul(o_ps[:, g % 2], v_sb[:, g % 8, kc], pt[:, g % 2, kc],
                                            start=kc + part == 0, stop=kc + part == QT)
                if kc == 3:
                    last.then_inc(pv_done, 1)
            found = task(it, l, PE_TASKS)
            if found:
                kind, head, pr, pi = found
                st = pr % 2
                w = w_st[:, st]
                if kind in "qk":
                    x0 = pi // NPAIR * (2 * N)
                    xh, xl = t.xs[:, bass.ds(x0, N)], t.xs[:, bass.ds(x0 + N, N)]
                if kind == "q":
                    pe.wait_ge(st_loaded[st], (it * 2 + pr // 2 + 1) * 16)
                    below(pe, y_added, pi - 2)
                    nc.tensor.matmul(qo_ps[:], w[:, QH:QH + P], xh, start=True, stop=False)
                    nc.tensor.matmul(qo_ps[:], w[:, QH:QH + P], xl, start=False, stop=False)
                    nc.tensor.matmul(qo_ps[:], w[:, QL:QL + P], xh, start=False, stop=True).then_inc(q_mm, 1)
                elif kind == "k":
                    below(pe, v_low, pi + 1)
                    nc.tensor.matmul(kv_ps[:], w[:, KH:KH + P], xh, start=True, stop=False)
                    nc.tensor.matmul(kv_ps[:], w[:, KH:KH + P], xl, start=False, stop=False)
                    nc.tensor.matmul(kv_ps[:], w[:, KL:KL + P], xh, start=False, stop=True).then_inc(k_mm, 1)
                elif kind == "v":
                    half, pairs = (pr + 1) % 2, (pr + 1) // 2
                    below(pe, k_low, pi + 1)
                    if half == 0:
                        pe.wait_ge(v_loaded, (it * 2 + pairs + 1) * 32)
                    for c in range(2):
                        out = kv_ps[:, c * 2 * P:(c + 1) * 2 * P]
                        k0 = (half * 2 + c) * P
                        xhk, xlk = xv_st[:, k0:k0 + P], xv_st[:, N + k0:N + k0 + P]
                        nc.tensor.matmul(out, xhk, wv_st[:, 0:2 * P], start=True, stop=False)
                        nc.tensor.matmul(out, xhk, wv_st[:, 2 * P:4 * P], start=False, stop=False)
                        last = nc.tensor.matmul(out, xlk, wv_st[:, 0:2 * P], start=False, stop=True)
                    last.then_inc(v_mm, 1)
                else:
                    pe.wait_ge(o_done, pi * 2 + head + 1)
                    if head == 0:
                        pe.wait_ge(wo_loaded[st], (it * 2 + pr // 2 + 1) * 16)
                        if pair_ok(it, pr + 2):
                            pe.wait_ge(q_low, pi + 3)
                        else:
                            pe.wait_ge(y_added, pi)
                    nc.tensor.matmul(qo_ps[:], wo_st[:, st, head * P:head * P + P], o_sb[:, head],
                                     start=head == 0, stop=head == 1).then_inc(wo_mm, 1)

        def act_slot(act, it, l):
            u = it * 32 + l
            if l % 4 == 0 and valid(it, l - 8):
                g = l // 4 - 2
                gi = it * 8 + g
                act.wait_ge(pv_done, gi + 1)
                below(act, wo_mm, gi - 1)
                nc.scalar.activation(o_sb[:, g % 2], o_ps[:, g % 2], ACT.Copy).then_inc(o_done, 1)
            if valid(it, l + 2):
                act.wait_ge(max_done, u + 3)
                below(act, t_done, u - 1)
                m = (l + 2) % 8
                nc.scalar.activation(probs[:, (l + 2) % 4], s_ps[:, l % 2], ACT.Exp, bias=nmax[:, m:m + 1],
                                     accum_out=rsum[:, m:m + 1]).then_inc(exp_done, 1)
            if valid(it, l):
                g, qt = l // 4, l % 4
                act.wait_ge(t_done, u + 1)
                if qt == 0:
                    below(act, pv_done, it * 8 + g - 1)
                nc.scalar.activation(pth[:, g % 2, :, qt * P:qt * P + P],
                                     t_ps[:, l % 2].rearrange("p (c q) -> p c q", c=QT), ACT.Copy).then_inc(ph_done, 1)
            found = task(it, l, ACT_TASKS)
            if found:
                kind, head, pr, pi = found
                if kind == "q":
                    act.wait_ge(q_mm, pi + 1)
                    wait_moved(act, it, pr - 1)
                    nc.scalar.activation(q_pair[:, 0], qo_ps[:], ACT.Identity, bias=bias(pi, 0)).then_inc(q_high, 1)
                elif kind == "k":
                    act.wait_ge(k_mm, pi + 1)
                    wait_moved(act, it, pr - 1)
                    nc.scalar.activation(k_pair[:, 0], kv_ps[:], ACT.Identity, bias=bias(pi, 1)).then_inc(k_high, 1)
                else:
                    high, _, values = value_half(pr)
                    act.wait_ge(v_mm, pi + 2)
                    if pr % 2 == 1:
                        below(act, pv_done, pi * 2 - 2)
                    nc.scalar.activation(high, values, ACT.Copy).then_inc(v_high, 1)

        def dve_slot(dve, it, l):
            u = it * 32 + l
            if valid(it, l + 1):
                dve.wait_ge(exp_done, u + 2)
                m = (l + 1) % 8
                nc.vector.reciprocal(rinv[:, m:m + 1], rsum[:, m:m + 1]).then_inc(inv_done, 1)
            found = task(it, l, DVE_TASKS)
            if found:
                kind, head, pr, pi = found
                if kind == "q":
                    dve.wait_ge(q_high, pi + 1)
                    nc.vector.scalar_tensor_tensor(q_pair[:, 1], qo_ps[:], bias(pi, 0), q_pair[:, 0], ALU.add, ALU.subtract)\
                        .then_inc(q_low, 1)
                elif kind == "k":
                    dve.wait_ge(k_high, pi + 1)
                    nc.vector.scalar_tensor_tensor(k_pair[:, 1], kv_ps[:], bias(pi, 1), k_pair[:, 0], ALU.add, ALU.subtract)\
                        .then_inc(k_low, 1)
                elif kind == "v":
                    high, low, values = value_half(pr)
                    dve.wait_ge(v_high, pi + 2)
                    nc.vector.tensor_tensor(low, values, high, ALU.subtract).then_inc(v_low, 1)
                else:
                    dve.wait_ge(wo_mm, pi * 2 + 2)
                    below(dve, y_added, pi)
                    acc = t.yacc[:, bass.ds(pi // NPAIR * N, N)]
                    nc.vector.tensor_tensor(acc, qo_ps[:], acc, ALU.add).then_inc(y_added, 1)
            if valid(it, l + 3):
                dve.wait_ge(s_done, u + 4)
                m = (l + 3) % 8
                nc.vector.tensor_reduce(nmax[:, m:m + 1], s_ps[:, (l + 3) % 2], axis=AX.X, op=ALU.max, negate=True)\
                    .then_inc(max_done, 1)
            if valid(it, l):
                g, qt = l // 4, l % 4
                dve.wait_ge(ph_done, u + 1)
                sl = slice(qt * P, qt * P + P)
                nc.vector.tensor_tensor(ptl[:, g % 2, :, sl], t_ps[:, l % 2].rearrange("p (c q) -> p c q", c=QT),
                                        pth[:, g % 2, :, sl], ALU.subtract).then_inc(pl_done, 1)

        def pool_slot(pool, it, l):
            u = it * 32 + l
            pr = l // 8
            fetch = l % 8 == 4 and pair_ok(it, pr)
            add = l % 16 == 3 and pair_ok(it, pr - 2)
            if fetch:
                pool.wait_ge(rows_loaded[pr % 2], (it * 2 + pr // 2) * 16 + 16)
                below(pool, rows_added, it * 2 + pr // 2)
            if add:
                for got in picked_up:
                    pool.wait_ge(got, (it * 2 + pr // 2) * 16)
            if valid(it, l + 1):
                pool.wait_ge(inv_done, u + 2)
                m, pb = (l + 1) % 8, probs[:, (l + 1) % 4]
                nc.gpsimd.tensor_tensor(pb, pb, rinv[:, m:m + 1].broadcast_to([P, N]), ALU.mult).then_inc(norm_done, 1)
            if fetch:
                pool.indirect_dma_start(picked[:, pr % 2], None, t.y_rows,
                                        bass.IndirectOffsetOnAxis(ap=row_st[:, pr % 2], axis=0)).then_inc(picked_up[pr % 2], 16)
            if add:
                both = t.expert_sum[:, bass.ds((it * 2 + pr // 2 - 1) * D, D)]
                nc.gpsimd.tensor_tensor(both, picked[:, 0], picked[:, 1], ALU.add).then_inc(rows_added, 1)

        def engine_program(eng, slot):
            for l in range(-16, 32):
                slot(eng, 0, l)
            with eng.Fori(1, PAIRS // 4 - 1) as it:
                for l in range(32):
                    slot(eng, it, l)
            for l in range(32, 32 + 32 + 12):
                slot(eng, PAIRS // 4 - 2, l)

        with nc.Block() as block:
            @block.sync
            def _(sp):
                def stage(it, pr):
                    st, pi = pr % 2, it * 4 + pr
                    w0 = pi % NPAIR // 2 * TWO_COLS + pr % 2 * QK_COLS
                    below(sp, k_low, pi - 1)
                    below(sp, q_low, pi - 1)
                    sp.dma_start(w_st[:, st].bitcast(F32), t.wall[:, bass.ds(w0, QK_COLS)].bitcast(F32))\
                        .then_inc(st_loaded[st], 16)

                def stage_values(it, m):
                    pairs = it * 2 + m
                    x0, v0 = pairs // (NPAIR // 2) * (2 * N), pairs % (NPAIR // 2) * TWO_COLS + VH
                    below(sp, v_mm, pairs * 2)
                    sp.dma_start(xv_st[:].bitcast(F32), t.xs[:, bass.ds(x0, 2 * N)].bitcast(F32)).then_inc(v_loaded, 16)
                    sp.dma_start(wv_st[:].bitcast(F32), t.wall[:, bass.ds(v0, 4 * P)].bitcast(F32)).then_inc(v_loaded, 16)

                def move(it, pr):
                    st, pi = pr % 2, it * 4 + pr
                    sp.wait_ge(q_low, pi + 1)
                    below(sp, s_done, pi * 8 - 8)
                    for head in range(2):
                        for part in range(2):
                            sp.dma_start(q_sb[part * HD:part * HD + HD, st * 2 + head].bitcast(F32),
                                         q_pair[head * HD:head * HD + HD, part].bitcast(F32)).then_inc(moved[st], 16)
                    sp.wait_ge(k_low, pi + 1)
                    for head in range(2):
                        for half in range(2):
                            sp.dma_start(k_sb[half * HD:half * HD + HD, st * 2 + head].bitcast(F32),
                                         k_pair[head * HD:head * HD + HD].bitcast(F32)).then_inc(moved[st], 16)

                def stage_wo(it, pr):
                    st, pi = pr % 2, it * 4 + pr
                    below(sp, wo_mm, pi * 2 - 2)
                    sp.dma_start(wo_st[:, st], t.wo_all[:, bass.ds(pi % NPAIR * (2 * P), 2 * P)]).then_inc(wo_loaded[st], 16)

                def fetch_rows(it, pr):
                    i = it * 2 + pr // 2
                    below(sp, picked_up[pr % 2], i * 16)
                    sp.dma_start(row_st[:, pr % 2], t.token_rows[:, pr % 2, bass.ds(i, 1)]).then_inc(rows_loaded[pr % 2], 16)

                def pair_ahead(it, pr):
                    if pair_ok(it, pr + 1):
                        move(it, pr + 1)
                    stage_wo(it, pr)
                    if pair_ok(it, pr + 2):
                        stage(it, pr + 2)
                    if pr % 2 == 1 and pair_ok(it, pr + 3):
                        stage_values(it, pr // 2 + 2)
                    if pair_ok(it, pr + 2):
                        fetch_rows(it, pr + 2)

                stage_values(0, 0)
                for pr in range(2):
                    stage(0, pr)
                    fetch_rows(0, pr)
                move(0, 0)
                stage_values(0, 1)
                for pr in range(4):
                    pair_ahead(0, pr)
                with sp.Fori(1, PAIRS // 4 - 1) as it:
                    for pr in range(4):
                        pair_ahead(it, pr)
                for pr in range(4):
                    pair_ahead(PAIRS // 4 - 1, pr)

            @block.tensor
            def _(pe):
                engine_program(pe, pe_slot)

            @block.scalar
            def _(act):
                engine_program(act, act_slot)

            @block.vector
            def _(dve):
                engine_program(dve, dve_slot)

            @block.gpsimd
            def _(pool):
                engine_program(pool, pool_slot)


def finish(nc, a, t, out):
    with ExitStack() as ctx:
        def sb(name, shape, dt=F32):
            return ctx.enter_context(nc.sbuf_tensor("fin_" + name, shape, dt))

        def sem(name):
            return ctx.enter_context(nc.semaphore("fin_" + name))

        CHUNKS = B // 2
        CT = TILES // CHUNKS
        CN = 2 * N
        x_in = sb("x_in", [P, TILES, D])
        yb = sb("yb", [P, B * N])
        stats, mv = sb("stats", [P, TILES, 6]), sb("mv", [P, TILES, 2])
        less_mean, rstd = sb("less_mean", [P, TILES]), sb("rstd", [P, TILES])
        centred, out_sb = sb("centred", [P, TILES, D]), sb("out_sb", [P, TILES, D])
        gamma, beta, eps = sb("gamma", [P, P]), sb("beta", [P, P]), sb("eps", [P, 1])
        yT_ps = ctx.enter_context(nc.psum_tensor("fin_yT_ps", [P, TILES, D], F32))
        once, eps_set, beta_added, rest_ready = sem("once"), sem("eps_set"), sem("beta_added"), sem("rest_ready")
        x_loaded = [sem(f"x_loaded{c}") for c in range(CHUNKS)]
        y_copied, yT_done = sem("y_copied"), sem("yT_done")
        chain, var_ready, std_ready, centred_ready = sem("chain"), sem("var_ready"), sem("std_ready"), sem("centred_ready")
        ready, stored = sem("ready"), sem("stored")

        def by_chunk(dram):
            return dram.rearrange("b n d -> (b n) d").rearrange("(c i p) d -> c p i d", p=P, i=CT)

        def tiles(c):
            return slice(c * CT, (c + 1) * CT)

        with nc.Block() as block:
            @block.sync
            def _(sp):
                for dst, src in ((gamma, "gamma"), (beta, "beta")):
                    sp.dma_start(dst[:], a[src].rearrange("(o n) -> o n", o=1).broadcast_to([P, P])).then_inc(once, 16)
                for c in range(CHUNKS):
                    sp.dma_start(x_in[:, tiles(c)], by_chunk(a["x"])[c]).then_inc(x_loaded[c], 16)
                for c in range(CHUNKS):
                    sp.wait_ge(ready, c + 1)
                    sp.dma_start(by_chunk(out)[c], out_sb[:, tiles(c)]).then_inc(stored, 16)
                sp.wait_ge(stored, CHUNKS * 16)

            @block.gpsimd
            def _(pool):
                pool.wait_ge(once, 32)
                for c in range(CHUNKS):
                    rest = t.expert_sum[:, c * CN:(c + 1) * CN].rearrange("p (i d) -> p i d", d=D)
                    nc.gpsimd.tensor_tensor(rest, rest, beta[:].unsqueeze(1).broadcast_to([P, CT, D]), ALU.add).then_inc(beta_added, 1)
                    pool.wait_ge(x_loaded[c], 16)
                    pool.wait_ge(beta_added, c + 1)
                    nc.gpsimd.tensor_tensor(rest, rest, x_in[:, tiles(c)], ALU.add).then_inc(rest_ready, 1)

            @block.scalar
            def _(act):
                for c in range(CHUNKS):
                    nc.scalar.activation(yb[:, c * CN:(c + 1) * CN], t.yacc[:, c * CN:(c + 1) * CN], ACT.Identity,
                                         bias=t.out_bias[:, 2:3]).then_inc(y_copied, 1)
                act.wait_ge(eps_set, 1)
                for c in range(CHUNKS):
                    act.wait_ge(var_ready, c + 1)
                    nc.scalar.activation(rstd[:, tiles(c)], mv[:, tiles(c), 1], ACT.Sqrt, bias=eps[:]).then_inc(std_ready, 1)
                    for i in range(c * CT, (c + 1) * CT):
                        last = nc.scalar.activation(centred[:, i], yT_ps[:, i], ACT.Identity, bias=less_mean[:, i:i + 1])
                    last.then_inc(centred_ready, 1)

            @block.tensor
            def _(pe):
                for c in range(CHUNKS):
                    pe.wait_ge(y_copied, c + 1)
                    for i in range(c * CT, (c + 1) * CT):
                        last = nc.tensor.transpose(yT_ps[:, i], yb[:, i * P:i * P + P], t.ident[:])
                    last.then_inc(yT_done, 1)

            @block.vector
            def _(dve):
                n = [0]

                def link(ins):
                    n[0] += 1
                    ins.then_inc(chain, 1)

                def linked():
                    dve.wait_ge(chain, n[0])

                def statistics(c):
                    dve.wait_ge(yT_done, c + 1)
                    for i in range(c * CT, (c + 1) * CT):
                        link(nc.vector.bn_stats(stats[:, i], yT_ps[:, i]))
                    linked()
                    for i in range(c * CT, (c + 1) * CT):
                        link(nc.vector.bn_aggr(mv[:, i], stats[:, i]))
                    linked()
                    nc.vector.tensor_scalar(less_mean[:, tiles(c)], mv[:, tiles(c), 0], -1.0, None, ALU.mult).then_inc(var_ready, 1)

                def norm(c):
                    dve.wait_ge(std_ready, c + 1)
                    link(nc.vector.reciprocal(rstd[:, tiles(c)], rstd[:, tiles(c)]))
                    linked()
                    dve.wait_ge(centred_ready, c + 1)
                    for i in range(c * CT, (c + 1) * CT):
                        link(nc.vector.scalar_tensor_tensor(centred[:, i], centred[:, i], rstd[:, i:i + 1], gamma[:],
                                                            ALU.mult, ALU.mult))
                    linked()
                    dve.wait_ge(rest_ready, c + 1)
                    rest = t.expert_sum[:, c * CN:(c + 1) * CN].rearrange("p (i d) -> p i d", d=D)
                    nc.vector.tensor_tensor(out_sb[:, tiles(c)], centred[:, tiles(c)], rest, ALU.add).then_inc(ready, 1)

                nc.vector.memset(eps[:], LN_EPS).then_inc(eps_set, 1)
                dve.wait_ge(once, 32)
                statistics(0)
                for c in range(1, CHUNKS):
                    statistics(c)
                    norm(c - 1)
                norm(CHUNKS - 1)


def route(nc, a, t):
    with ExitStack() as ctx:
        def sb(name, shape, dt=F32):
            return ctx.enter_context(nc.sbuf_tensor("rt_" + name, shape, dt))

        def sem(name):
            return ctx.enter_context(nc.semaphore("rt_" + name))

        lg = t.logits
        lmax = sb("lmax", [P, TILES])
        second = sb("second", [P, TILES, E])
        countdown, countdown_i = sb("countdown", [P, E]), sb("countdown_i", [P, E], I32)
        earlier = sb("earlier", [P, P], BF16)
        ones = sb("ones", [P, P], BF16)
        chosen = sb("chosen", [P, TILES, E])
        chosen_b = sb("chosen_b", [P, TILES, E], BF16)
        count = sb("count", [P, 2, E, TILES])
        steps128 = sb("steps128", [P, BLOCKS])
        steps_i = sb("steps_i", [P, BLOCKS], I32)
        over = sb("over", [P, BLOCKS, E])
        blocks = sb("blocks", [P, 3, E])
        row = sb("row", [P, TILES, E])
        pick = sb("pick", [P, TILES, E])
        sel = sb("sel", [P, 2, TILES])
        ids = sb("ids", [P, BLOCKS])
        same = sb("same", [P, BLOCKS])
        row_no = sb("row_no", [P, 2])
        row_no_i = sb("row_no_i", [P, 2], I32)
        c_ps = ctx.enter_context(nc.psum_tensor("rt_c_ps", [P, 2, 512], F32))
        made, chain = sem("made"), sem("chain")
        chosen_ready, counted = sem("chosen_ready"), sem("counted")

        with nc.Block() as block:
            @block.gpsimd
            def _(pool):
                pool.memset(earlier[:], 1.0).then_inc(made, 1)
                pool.memset(ones[:], 1.0).then_inc(made, 1)
                pool.wait_ge(made, 2)
                pool.affine_select(out=earlier[:], in_=earlier[:], compare_op=ALU.is_gt, fill=0.0, base=0,
                                   pattern=[[1, P]], channel_multiplier=-1).then_inc(made, 1)
                pool.iota(countdown_i[:], pattern=[[-1, E]], base=E, channel_multiplier=0).then_inc(made, 1)
                pool.iota(steps_i[:], pattern=[[P, BLOCKS]], base=0, channel_multiplier=0).then_inc(made, 1)
                pool.iota(row_no_i[:], pattern=[[-LOW_ROW, 2]], base=0, channel_multiplier=1).then_inc(made, 1)

            @block.tensor
            def _(pe):
                pe.wait_ge(chosen_ready, 1)
                flat = chosen_b[:].rearrange("p t e -> p (t e)")
                nc.tensor.matmul(c_ps[:, 0, 0:TILES * E], earlier[:], flat, start=True, stop=True)
                nc.tensor.matmul(c_ps[:, 1, 0:TILES * E], ones[:], flat, start=True, stop=True).then_inc(counted, 1)

            @block.vector
            def _(dve):
                n = [0]

                def link(ins):
                    n[0] += 1
                    ins.then_inc(chain, 1)
                    dve.wait_ge(chain, n[0])

                def tt(out, x, y, op):
                    link(nc.vector.tensor_tensor(out, x, y, op))

                link(nc.vector.reduce_max(lmax[:], lg[:], axis=AX.X))
                by_expert = [P, TILES, E]
                tt(lg[:], lg[:], lmax[:].unsqueeze(2).broadcast_to(by_expert), ALU.subtract)
                link(nc.vector.tensor_scalar(lg[:], lg[:], -104.0, None, ALU.max))
                dve.wait_ge(made, 6)
                link(nc.vector.tensor_copy(countdown[:], countdown_i[:]))
                link(nc.vector.tensor_copy(row_no[:], row_no_i[:]))
                link(nc.vector.tensor_copy(steps128[:], steps_i[:]))
                most = lmax[:].unsqueeze(2).broadcast_to(by_expert)
                for turn in range(2):
                    got = chosen if turn == 0 else second
                    link(nc.vector.reduce_max(lmax[:], lg[:], axis=AX.X))
                    tt(got[:], lg[:], most, ALU.is_equal)
                    tt(got[:], got[:], countdown[:].unsqueeze(1).broadcast_to(by_expert), ALU.mult)
                    link(nc.vector.reduce_max(lmax[:], got[:], axis=AX.X))
                    tt(got[:], got[:], most, ALU.is_equal)
                    if turn == 0:
                        link(nc.vector.scalar_tensor_tensor(lg[:], chosen[:], -1e4, lg[:], ALU.mult, ALU.add))
                tt(chosen[:], chosen[:], second[:], ALU.add)
                nc.vector.tensor_copy(chosen_b[:], chosen[:]).then_inc(chosen_ready, 1)
                dve.wait_ge(counted, 1)
                link(nc.vector.tensor_copy(count[:, 0], c_ps[:, 1, 0:TILES * E].rearrange("p (t e) -> p e t", e=E)))
                src, step = 0, 1
                while step < TILES:
                    dst = 1 - src
                    nc.vector.tensor_copy(count[:, dst, :, 0:step], count[:, src, :, 0:step])
                    tt(count[:, dst, :, step:TILES], count[:, src, :, step:TILES], count[:, src, :, 0:TILES - step], ALU.add)
                    src, step = dst, 2 * step
                taken = over[:].rearrange("p b e -> p (b e)")[:, 0:E * TILES].rearrange("p (e s) -> p e s", s=TILES)
                tt(taken, count[:, src, :, TILES - 1:TILES].broadcast_to([P, E, TILES]),
                   steps128[:, 0:TILES].unsqueeze(1).broadcast_to([P, E, TILES]), ALU.is_gt)
                link(nc.vector.reduce_sum(blocks[:, 0], taken, axis=AX.X))
                bsrc, step = 0, 1
                while step < E:
                    bdst = 1 if bsrc != 1 else 2
                    nc.vector.tensor_copy(blocks[:, bdst, 0:step], blocks[:, bsrc, 0:step])
                    tt(blocks[:, bdst, step:E], blocks[:, bsrc, step:E], blocks[:, bsrc, 0:E - step], ALU.add)
                    bsrc, step = bdst, 2 * step
                link(nc.vector.tensor_scalar(blocks[:, bsrc], blocks[:, bsrc], float(P), None, ALU.mult))
                tt(over[:], steps128[:].unsqueeze(2).broadcast_to([P, BLOCKS, E]),
                   blocks[:, bsrc].unsqueeze(1).broadcast_to([P, BLOCKS, E]), ALU.is_ge)
                link(nc.vector.reduce_sum(ids[:], over[:], axis=AX.X))
                link(nc.vector.tensor_scalar(ids[:], ids[:], float(E - 1), None, ALU.min))
                link(nc.vector.tensor_copy(t.block_expert[:], ids[:]))
                link(nc.vector.tensor_scalar(same[:], ids[:], row_no[:, 0:1], None, ALU.is_equal))
                link(nc.vector.tensor_scalar(ids[:], ids[:], row_no[:, 1:2], None, ALU.is_equal))
                tt(t.block_rows[:], ids[:], same[:], ALU.add)
                link(nc.vector.tensor_scalar(blocks[:, 0], blocks[:, 0], float(P), None, ALU.mult))
                tt(blocks[:, bsrc], blocks[:, bsrc], blocks[:, 0], ALU.subtract)
                tt(row[:], c_ps[:, 0, 0:TILES * E].rearrange("p (t e) -> p t e", e=E),
                   count[:, src].rearrange("p e t -> p t e"), ALU.add)
                tt(row[:], c_ps[:, 1, 0:TILES * E].rearrange("p (t e) -> p t e", e=E), row[:], ALU.subtract)
                tt(row[:], blocks[:, bsrc].unsqueeze(1).broadcast_to(by_expert), row[:], ALU.subtract)
                far = float(4 * BLOCKS * P)
                link(nc.vector.tensor_scalar(pick[:], chosen[:], -far, far, ALU.mult, ALU.add))
                tt(pick[:], row[:], pick[:], ALU.add)
                link(nc.vector.tensor_reduce(sel[:, 0], pick[:], axis=AX.X, op=ALU.min))
                tt(pick[:], row[:], chosen[:], ALU.mult)
                link(nc.vector.reduce_max(sel[:, 1], pick[:], axis=AX.X))
                link(nc.vector.tensor_copy(t.token_rows[:], sel[:]))


def prepare_weights(nc, a, t):
    R_G1, R_G2, ROWS = 0, E * HC, E * HC + E
    with ExitStack() as ctx:
        def sb(name, shape, dt=F32):
            return ctx.enter_context(nc.sbuf_tensor("wex_" + name, shape, dt))

        def sem(name):
            return ctx.enter_context(nc.semaphore("wex_" + name))

        rows = sb("rows", [P, P])
        cols = sb("cols", [P, ROWS])
        w_in = sb("w_in", [P, 2, 2 * HC, P])
        wn = sb("wn", [P, 2, 2 * HC, P])
        w_sq = sb("w_sq", [P, 2 * HC, P])
        ss = sb("ss", [P, 2, HC + 1])
        nrm = sb("nrm", [P, 2, HC + 1])
        wscale = sb("wscale", [P, 2, HC + 1])
        wT_ps = ctx.enter_context(nc.psum_tensor("wex_wT_ps", [P, 2, 2, FH], F32))
        r_ps = ctx.enter_context(nc.psum_tensor("wex_r_ps", [P, P], F32))
        b_in = sb("b_in", [P, FH + 2 * D])
        aw_in = sb("aw_in", [P, 4, NPAIR, P])
        bv_row = w_sq[:].rearrange("p c n -> p (c n)")
        q_scale = sb("q_scale", [P, NPAIR])
        ab_in = sb("ab_in", [P, 2, NPAIR])
        aT_ps = ctx.enter_context(nc.psum_tensor("wex_aT_ps", [P, 2, 4, P], F32))
        bv_loaded = sem("bv_loaded")
        a_loaded, a_chain, wq_scaled, aT_done, a_high, a_free = (
            sem(n) for n in ("a_loaded", "a_chain", "wq_scaled", "aT_done", "a_high", "a_free"))
        rows_zero, once, rowsT, sent = sem("rows_zero"), sem("once"), sem("rowsT"), sem("sent")
        w_loaded = [sem("w_loaded0"), sem("w_loaded1")]
        chain, sq_ready, std_ready, wn_ready = sem("chain"), sem("sq_ready"), sem("std_ready"), sem("wn_ready")
        wT_done, high, w_free, summed = sem("wT_done"), sem("high"), sem("w_free"), sem("summed")

        with nc.Block() as block:
            @block.sync
            def _(sp):
                sp.wait_ge(rows_zero, 2)
                sp.dma_start(rows[R_G1:R_G2, :], a["w1_g"].rearrange("e (c p) -> (e c) p", p=P)).then_inc(once, 16)
                sp.dma_start(rows[R_G2:ROWS, :], a["w2_g"]).then_inc(once, 16)
                for r0 in (0, LOW_ROW):
                    sp.dma_start(b_in[r0:r0 + E, 0:FH], a["b1"]).then_inc(once, 16)
                    sp.dma_start(b_in[r0:r0 + E, FH:FH + D], a["b2"]).then_inc(once, 16)
                with sp.Fori(0, E // 2) as it:
                    for k in range(2):
                        e = it * 2 + k
                        sp.wait_ge(wn_ready, e + 1)
                        sp.dma_start(w_in[:, k, 0:HC], a["w1_v"].rearrange("e (c p) d -> e p c d", p=P)[bass.ds(e, 1)]
                                     .rearrange("o p c d -> p (o c) d")).then_inc(w_loaded[k], 16)
                        sp.dma_start(w_in[:, k, HC:2 * HC], a["w2_v"].rearrange("e p (c n) -> e p c n", n=P)[bass.ds(e, 1)]
                                     .rearrange("o p c n -> p (o c) n")).then_inc(w_loaded[k], 16)
                for i, name in enumerate(("Wq", "Wk", "Wv")):
                    sp.dma_start(aw_in[:, i], a[name].rearrange("(j p) d -> p j d", p=P)).then_inc(a_loaded, 16)
                sp.dma_start(aw_in[:, 3].rearrange("p j d -> p (j d)"), a["Wo"]).then_inc(a_loaded, 16)
                sp.dma_start(t.out_bias[:, 0:1], a["bo"].rearrange("(p o) -> p o", o=1)).then_inc(a_loaded, 16)
                for half in range(2):
                    sp.dma_start(q_scale[half * HD:half * HD + HD, :], a["adaptive_scale"]
                                 .rearrange("(o r h) -> h o r", h=2, o=1)[half].broadcast_to([HD, NPAIR]),
                                 allow_slow_non_contiguous=True).then_inc(a_loaded, 16)
                for i, name in enumerate(("bq", "bk")):
                    sp.dma_start(ab_in[:, i, :], a[name].rearrange("(r p) -> p r", p=P), allow_slow_non_contiguous=True)\
                        .then_inc(a_loaded, 16)
                sp.wait_ge(std_ready, E)
                sp.dma_start(bv_row, a["bv"].rearrange("(o n) -> o n", o=1).broadcast_to([P, H * HD])).then_inc(bv_loaded, 16)

            @block.gpsimd
            def _(pool):
                pool.memset(rows[:], 0.0).then_inc(rows_zero, 1)
                pool.memset(b_in[:], 0.0).then_inc(rows_zero, 1)
                for i in range(TILES):
                    for which in range(2):
                        pool.indirect_dma_start(
                            t.x_rows, bass.IndirectOffsetOnAxis(ap=t.token_rows[:, which, i:i + 1], axis=0),
                            t.xn_rows[:, i * P:i * P + P], None).then_inc(sent, 16)
                pool.wait_ge(sent, 2 * TILES * 16)

            @block.vector
            def _(dve):
                dve.wait_ge(rowsT, 1)
                nc.vector.tensor_copy(cols[:], r_ps[:, 0:ROWS]).then_inc(chain, 1)
                nc.vector.tensor_copy(t.biases[:], b_in[:]).then_inc(chain, 1)
                dve.wait_ge(chain, 2)
                low = slice(LOW_ROW, 2 * LOW_ROW)
                nc.vector.tensor_tensor(t.biases[low], b_in[low], t.biases[low], ALU.subtract).then_inc(chain, 1)
                dve.sem_inc(wn_ready, 2)
                c1, steps = 3, 4

                def scale(e, k, used):
                    c0 = e * steps + c1
                    dve.wait_ge(std_ready, e + 1)
                    nc.vector.tensor_scalar(nrm[:, k], nrm[:, k], WN_EPS, None, ALU.max).then_inc(chain, 1)
                    dve.wait_ge(chain, c0 + 1)
                    nc.vector.reciprocal(nrm[:, k], nrm[:, k]).then_inc(chain, 1)
                    dve.wait_ge(chain, c0 + 2)
                    nc.vector.tensor_tensor(wscale[:, k, 0:HC], cols[:, bass.ds(e * HC + R_G1, HC)], nrm[:, k, 0:HC], ALU.mult)\
                        .then_inc(chain, 1)
                    nc.vector.tensor_tensor(wscale[:, k, HC:HC + 1], cols[:, bass.ds(e + R_G2, 1)], nrm[:, k, HC:HC + 1],
                                            ALU.mult).then_inc(chain, 1)
                    dve.wait_ge(chain, c0 + 4)
                    if used:
                        dve.wait_ge(wT_done, e * 2 - 2)
                    nc.vector.tensor_tensor(wn[:, k, 0:HC], w_in[:, k, 0:HC],
                                            wscale[:, k, 0:HC].unsqueeze(2).broadcast_to([P, HC, P]), ALU.mult)
                    nc.vector.tensor_scalar(wn[:, k, HC:2 * HC], w_in[:, k, HC:2 * HC], wscale[:, k, HC:HC + 1], None, ALU.mult)\
                        .then_inc(wn_ready, 1)

                def low_parts(e, k):
                    dve.wait_ge(high, e * 2 + 2)
                    w0 = e * 2 * FH
                    nc.vector.tensor_tensor(t.w1[:, bass.ds(w0 + FH, FH)], wT_ps[:, k, 0], t.w1[:, bass.ds(w0, FH)], ALU.subtract)
                    w2 = t.w2[:, bass.ds(w0, 2 * FH)].rearrange("p (c h d) -> p c h d", h=2, d=D)
                    nc.vector.tensor_tensor(w2[:, :, 1], wT_ps[:, k, 1].rearrange("p (c d) -> p c d", d=D), w2[:, :, 0],
                                            ALU.subtract).then_inc(w_free, 1)

                scale(0, 0, used=False)
                scale(1, 1, used=False)
                with dve.Fori(1, E // 2) as it:
                    for k in range(2):
                        low_parts(it * 2 + k - 2, k)
                        scale(it * 2 + k, k, used=True)
                low_parts(E - 2, 0)
                low_parts(E - 1, 1)

                dve.wait_ge(a_loaded, 9 * 16)
                nc.vector.tensor_scalar(q_scale[:], q_scale[:], SCALE, None, ALU.mult).then_inc(a_chain, 1)
                dve.wait_ge(bv_loaded, 16)
                nc.vector.tensor_tensor(bv_row, aw_in[:, 3].rearrange("p j d -> p (j d)"), bv_row, ALU.mult).then_inc(a_chain, 1)
                dve.wait_ge(a_chain, 2)
                nc.vector.tensor_tensor(aw_in[:, 0], aw_in[:, 0], q_scale[:].unsqueeze(2).broadcast_to([P, NPAIR, P]), ALU.mult)\
                    .then_inc(wq_scaled, 1)
                biases = t.bias_all[:].rearrange("p (r c) -> p r c", c=2)
                nc.vector.tensor_tensor(biases[:, :, 0], ab_in[:, 0, :], q_scale[:], ALU.mult)
                nc.vector.tensor_copy(biases[:, :, 1], ab_in[:, 1, :])
                nc.vector.reduce_sum(t.out_bias[:, 1:2], bv_row, axis=AX.X).then_inc(a_chain, 1)
                dve.wait_ge(a_chain, 3)
                nc.vector.tensor_tensor(t.out_bias[:, 2:3], t.out_bias[:, 0:1], t.out_bias[:, 1:2], ALU.add)
                with dve.Fori(0, NPAIR // 2) as it:
                    for k in range(2):
                        w0, v0 = it * TWO_COLS + k * QK_COLS, it * TWO_COLS + k * P
                        dve.wait_ge(a_high, it * 2 + k + 1)
                        qk = t.wall[:, bass.ds(w0, QK_COLS)].rearrange("p (i h n) -> p i h n", i=2, h=2)
                        nc.vector.tensor_tensor(qk[:, :, 1], aT_ps[:, k, 0:2], qk[:, :, 0], ALU.subtract)
                        nc.vector.tensor_tensor(t.wall[:, bass.ds(v0 + VL, P)], aT_ps[:, k, 2],
                                                t.wall[:, bass.ds(v0 + VH, P)], ALU.subtract).then_inc(a_free, 1)

            @block.tensor
            def _(pe):
                pe.wait_ge(once, 16 * 6)
                nc.tensor.transpose(r_ps[:], rows[:], t.ident[:]).then_inc(rowsT, 1)
                with pe.Fori(0, E // 2) as it:
                    for k in range(2):
                        e = it * 2 + k
                        pe.wait_ge(wn_ready, e + 3)
                        pe.wait_ge(w_free, e + 1)
                        for half in range(2):
                            for c in range(HC):
                                last = nc.tensor.transpose(wT_ps[:, k, half, c * P:c * P + P], wn[:, k, half * HC + c], t.ident[:])
                            last.then_inc(wT_done, 1)
                pe.wait_ge(a_loaded, 9 * 16)
                pe.wait_ge(wq_scaled, 1)
                for j in range(NPAIR):
                    pe.wait_ge(a_free, j + 1)
                    for i in range(4):
                        last = nc.tensor.transpose(aT_ps[:, j % 2, i], aw_in[:, i, j], t.ident[:])
                    last.then_inc(aT_done, 1)

            @block.scalar
            def _(act):
                act.sem_inc(w_free, 2)

                def norms(e, k, count):
                    act.wait_ge(w_loaded[k], count)
                    act.wait_ge(wn_ready, e + 1)
                    for c in range(HC):
                        nc.scalar.activation(w_sq[:, c], w_in[:, k, c], ACT.Square, accum_out=ss[:, k, c:c + 1]).then_inc(summed, 1)
                    nc.scalar.activation(w_sq[:, HC:2 * HC], w_in[:, k, HC:2 * HC], ACT.Square,
                                         accum_out=ss[:, k, HC:HC + 1]).then_inc(summed, 1)
                    act.wait_ge(summed, e * (HC + 1) + HC + 1)
                    nc.scalar.activation(nrm[:, k], ss[:, k], ACT.Sqrt).then_inc(std_ready, 1)

                def high_parts(e, k):
                    act.wait_ge(wT_done, e * 2 + 2)
                    w0 = e * 2 * FH
                    nc.scalar.activation(t.w1[:, bass.ds(w0, FH)], wT_ps[:, k, 0], ACT.Copy).then_inc(high, 1)
                    w2 = t.w2[:, bass.ds(w0, 2 * FH)].rearrange("p (c h d) -> p c h d", h=2, d=D)
                    nc.scalar.activation(w2[:, :, 0], wT_ps[:, k, 1].rearrange("p (c d) -> p c d", d=D), ACT.Copy)\
                        .then_inc(high, 1)

                norms(0, 0, 32)
                norms(1, 1, 32)
                with act.Fori(1, E // 2) as it:
                    for k in range(2):
                        high_parts(it * 2 + k - 2, k)
                        norms(it * 2 + k, k, it * 32 + 32)
                high_parts(E - 2, 0)
                high_parts(E - 1, 1)
                act.sem_inc(a_free, 2)
                with act.Fori(0, NPAIR // 2) as it:
                    for k in range(2):
                        j = it * 2 + k
                        w0, v0 = it * TWO_COLS + k * QK_COLS, it * TWO_COLS + k * P
                        act.wait_ge(aT_done, j + 1)
                        qk = t.wall[:, bass.ds(w0, QK_COLS)].rearrange("p (i h n) -> p i h n", i=2, h=2)
                        nc.scalar.activation(qk[:, :, 0], aT_ps[:, k, 0:2], ACT.Copy)
                        nc.scalar.activation(t.wall[:, bass.ds(v0 + VH, P)], aT_ps[:, k, 2], ACT.Copy)
                        for head in range(2):
                            for half in range(2):
                                last = nc.scalar.activation(
                                    t.wo_all[half * HD:half * HD + HD, bass.ds(j * 2 * P + head * P, P)],
                                    aT_ps[head * HD:head * HD + HD, k, 3], ACT.Copy)
                        last.then_inc(a_high, 1)


def experts(nc, t):
    with ExitStack() as ctx:
        def sb(name, shape, dt=F32):
            return ctx.enter_context(nc.sbuf_tensor("exp_" + name, shape, dt))

        def psum(name, shape):
            return ctx.enter_context(nc.psum_tensor("exp_" + name, shape, F32))

        def sem(name):
            return ctx.enter_context(nc.semaphore("exp_" + name))

        x_blk = sb("x_blk", [P, 4, D])
        xT_h, xT_l = sb("xT_h", [P, 2, P], F32R), sb("xT_l", [P, 2, P], F32R)
        hid = sb("hid", [P, 2, FH])
        pick = sb("pick", [P, 4, P], F32R)
        hT_h, hT_l = sb("hT_h", [P, 2, HC, P], F32R), sb("hT_l", [P, 2, HC, P], F32R)
        part, y_blk = sb("part", [P, D]), sb("y_blk", [P, 4, D])
        x_ps, h_ps, t_ps, y_ps = psum("x_ps", [P, 2, 512]), psum("h_ps", [P, 2, FH]), psum("t_ps", [P, 2, FH]), psum("y_ps", [P, 2, 512])
        loaded, stored = [sem("loaded0"), sem("loaded1")], [sem("stored0"), sem("stored1")]
        xT_done, x_high, x_low = sem("xT_done"), sem("x_high"), sem("x_low")
        h_done, picked, silu_done = sem("h_done"), sem("picked"), sem("silu_done")
        hT_done, h_high, h_low = sem("hT_done"), sem("h_high"), sem("h_low")
        y_done, half_done, y_ready = sem("y_done"), sem("half_done"), sem("y_ready")

        def ok(it, k):
            return not isinstance(it, int) or 0 <= 4 * it + k < BLOCKS

        def expert_of(eng, it, k):
            b = it * 4 + k
            at = t.block_expert[0:1, b:b + 1] if isinstance(b, int) else t.block_expert[0:1, bass.ds(b, 1)]
            return eng.value_load(at, min_val=0, max_val=E - 1)

        first_cols = {}

        def find_weights(pe, it, k):
            if ok(it, k):
                first_cols[k] = expert_of(pe, it, k) * (2 * FH)

        def pe_step(pe, it, k):
            b = it * 4 + k
            if ok(it, k + 2):
                s = k % 2
                if k % 2 == 0:
                    pair = (k + 2) // 2
                    pe.wait_ge(loaded[pair % 2], (it + pair // 2) * 16 + 16)
                below(pe, x_low, b + 1)
                nc.tensor.transpose(x_ps[:, s, 0:P], x_blk[:, (k + 2) % 4], t.ident[:]).then_inc(xT_done, 1)
            if ok(it, k + 1):
                s = (k + 1) % 2
                if k in (-1, 0):
                    find_weights(pe, it, k + 1)
                w0 = first_cols[k + 1]
                wh, wl = t.w1[:, bass.ds(w0, FH)], t.w1[:, bass.ds(w0 + FH, FH)]
                pe.wait_ge(x_low, b + 2)
                below(pe, silu_done, b)
                pe.wait_ge(picked, b + 2)
                nc.tensor.matmul(h_ps[:, s], xT_h[:, s], wh, start=True, stop=False)
                nc.tensor.matmul(h_ps[:, s], xT_h[:, s], wl, start=False, stop=False)
                nc.tensor.matmul(h_ps[:, s], xT_l[:, s], wh, start=False, stop=False)
                nc.tensor.matmul(h_ps[:, s], pick[:, (k + 1) % 4], t.biases[:, 0:FH], start=False, stop=True).then_inc(h_done, 1)
            if k <= 1:
                find_weights(pe, it, k - 1)
            if ok(it, k):
                s = k % 2
                pe.wait_ge(silu_done, b + 1)
                below(pe, h_low, b - 1)
                for c in range(HC):
                    last = nc.tensor.transpose(t_ps[:, s, c * P:c * P + P], hid[:, s, c * P:c * P + P], t.ident[:])
                last.then_inc(hT_done, 1)
            if ok(it, k - 1):
                s = (k - 1) % 2
                w0 = first_cols[k - 1]
                pe.wait_ge(h_low, b)
                below(pe, y_ready, b - 2)
                for hT in (hT_h, hT_l):
                    for c in range(HC):
                        nc.tensor.matmul(y_ps[:, s, 0:2 * D], hT[:, s, c], t.w2[:, bass.ds(w0 + c * 2 * D, 2 * D)],
                                         start=hT is hT_h and c == 0, stop=False)
                nc.tensor.matmul(y_ps[:, s, 0:2 * D], pick[:, (k - 1) % 4], t.biases[:, FH:FH + 2 * D], start=False, stop=True)\
                    .then_inc(y_done, 1)
            if 0 <= k < 3:
                find_weights(pe, it, k + 2)

        def act_step(act, it, k):
            b = it * 4 + k
            if ok(it, k + 2):
                s = k % 2
                act.wait_ge(xT_done, b + 3)
                below(act, h_done, b + 1)
                nc.scalar.activation(xT_h[:, s], x_ps[:, s, 0:P], ACT.Copy).then_inc(x_high, 1)
            if ok(it, k + 1):
                s = (k + 1) % 2
                act.wait_ge(h_done, b + 2)
                below(act, hT_done, b)
                nc.scalar.activation(hid[:, s], h_ps[:, s], ACT.Silu).then_inc(silu_done, 1)
            if ok(it, k):
                s = k % 2
                act.wait_ge(hT_done, b + 1)
                below(act, y_done, b - 1)
                nc.scalar.activation(hT_h[:, s], t_ps[:, s].rearrange("p (c n) -> p c n", c=HC), ACT.Copy).then_inc(h_high, 1)
            if ok(it, k - 1):
                act.wait_ge(y_done, b)
                below(act, y_ready, b - 1)
                nc.scalar.activation(part[:], y_ps[:, (k - 1) % 2, D:2 * D], ACT.Copy).then_inc(half_done, 1)
            if k % 2 == 1 and ok(it, k - 2):
                pair = (k - 3) // 2
                act.wait_ge(y_ready, b - 1)
                act.dma_start(rows_of(t.y_rows, it * 2 + pair), y_blk[:, pair % 2 * 2:pair % 2 * 2 + 2])\
                    .then_inc(stored[pair % 2], 16)

        def dve_step(dve, it, k):
            b = it * 4 + k
            if ok(it, k + 2):
                s = k % 2
                dve.wait_ge(x_high, b + 3)
                nc.vector.tensor_tensor(xT_l[:, s], x_ps[:, s, 0:P], xT_h[:, s], ALU.subtract).then_inc(x_low, 1)
            if ok(it, k):
                s = k % 2
                dve.wait_ge(h_high, b + 1)
                nc.vector.tensor_tensor(hT_l[:, s], t_ps[:, s].rearrange("p (c n) -> p c n", c=HC), hT_h[:, s], ALU.subtract)\
                    .then_inc(h_low, 1)
            if ok(it, k - 1):
                s = (k - 1) % 2
                dve.wait_ge(half_done, b)
                if k % 2 == 1:
                    pair = (k - 1) // 2
                    below(dve, stored[pair % 2], (it + pair // 2) * 16)
                nc.vector.tensor_tensor(y_blk[:, (k - 1) % 4], y_ps[:, s, 0:D], part[:], ALU.add).then_inc(y_ready, 1)

        def pool_step(pool, it, k):
            b = it * 4 + k
            if ok(it, k + 2):
                below(pool, y_done, b - 1)
                at = t.block_rows[:, b + 2:b + 3] if isinstance(b, int) else t.block_rows[:, bass.ds(b + 2, 1)]
                nc.gpsimd.tensor_copy(pick[:, (k + 2) % 4], at.broadcast_to([P, P])).then_inc(picked, 1)

        def rows_of(rows, pair):
            r0 = pair * 2 * P
            part = rows[r0:r0 + 2 * P, :] if isinstance(r0, int) else rows[bass.ds(r0, 2 * P), :]
            return part.rearrange("(c p) d -> p c d", p=P)

        def load(sp, it, k):
            pair = it * 2 + k
            below(sp, xT_done, pair * 2 - 2)
            sp.dma_start(x_blk[:, k % 2 * 2:k % 2 * 2 + 2], rows_of(t.x_rows, pair)).then_inc(loaded[k % 2], 16)

        def program(eng, step):
            for k in range(-2, 4):
                step(eng, 0, k)
            with eng.Fori(1, BLOCKS // 4 - 1) as it:
                for k in range(4):
                    step(eng, it, k)
            for k in range(4 + 2):
                step(eng, BLOCKS // 4 - 1, k)

        with nc.Block() as block:
            @block.sync
            def _(sp):
                for k in range(2):
                    load(sp, 0, k)
                with sp.Fori(1, BLOCKS // 4) as it:
                    for k in range(2):
                        load(sp, it, k)
                for s in stored:
                    sp.wait_ge(s, BLOCKS // 4 * 16)

            @block.tensor
            def _(pe):
                program(pe, pe_step)

            @block.scalar
            def _(act):
                program(act, act_step)

            @block.vector
            def _(dve):
                program(dve, dve_step)

            @block.gpsimd
            def _(pool):
                program(pool, pool_step)


def build(nc, a, out):
    class Shared:
        pass

    t = Shared()
    t.x_rows = nc.dram_tensor("x_rows", [BLOCKS * P, D], F32).ap()
    t.y_rows = nc.dram_tensor("y_rows", [BLOCKS * P, D], F32).ap()
    with ExitStack() as ctx:
        def sb(name, shape, dt=F32):
            return ctx.enter_context(nc.sbuf_tensor(name, shape, dt))

        t.xs = sb("xs", [P, B * 2 * N], F32R)
        t.yacc = sb("yacc", [P, B * N])
        t.out_bias = sb("out_bias", [P, 3])
        t.token_rows = sb("token_rows", [P, 2, TILES], I32)
        t.ident = make_identity(nc, ctx, "ident")
        with ExitStack() as inner:
            def sbi(name, shape, dt=F32):
                return inner.enter_context(nc.sbuf_tensor(name, shape, dt))

            t.wall = sbi("wall", [P, NPAIR // 2 * TWO_COLS], F32R)
            t.wo_all = sbi("wo_all", [P, NPAIR * 2 * P])
            t.bias_all = sbi("bias_all", [P, NPAIR * 2])
            with ExitStack() as deeper:
                def sbd(name, shape, dt=F32):
                    return deeper.enter_context(nc.sbuf_tensor(name, shape, dt))

                t.block_expert = sbd("block_expert", [P, BLOCKS], I32)
                t.block_rows = sbd("block_rows", [P, BLOCKS])
                t.xn_rows = sbd("xn_rows", [P, TILES * D])
                t.logits = sbd("logits", [P, TILES, E])
                normalise(nc, a, t)
                route(nc, a, t)
                t.w1 = sbd("w1", [P, E * 2 * FH], F32R)
                t.w2 = sbd("w2", [P, E * 2 * FH], F32R)
                t.biases = sbd("biases", [P, FH + 2 * D], F32R)
                prepare_weights(nc, a, t)
                experts(nc, t)
            t.expert_sum = sbi("expert_sum", [P, TILES * D])
            attention(nc, t)
            finish(nc, a, t, out)


_ATTN = ["x", "adaptive_scale", "Wq", "bq", "Wk", "bk", "Wv", "bv", "Wo", "bo", "gamma", "beta"]
_FFN = ["gate_v", "gate_g", "gate_b", "w1_v", "w1_g", "b1", "w2_v", "w2_g", "b2"]


def kernel(**inputs):
    import numpy as _np
    import concourse.bacc as _bacc
    from concourse import mybir as _mybir
    from concourse.bass_utils import run_bass_kernel_spmd as _run

    nc = _bacc.Bacc("TRN2", target_bir_lowering=False, num_devices=1)
    arrays, args = {}, {}
    for prefix, names in (("L0_attn_", _ATTN), ("L0_ffn_", _FFN)):
        for name in names:
            v = _np.ascontiguousarray(inputs[prefix + name])
            arrays[f"in_{name}"] = v
            args[name] = nc.dram_tensor(f"in_{name}", v.shape, _mybir.dt.from_np(v.dtype), kind="ExternalInput").ap()
    out = nc.dram_tensor("out_0", (B, N, D), F32, kind="ExternalOutput").ap()
    build(nc, args, out)
    r = _run(nc, [arrays], core_ids=[0])
    return r.results[0]["out_0"]
```
